# Optimizing a Trainium2 kernel written in Bass

```python
import numpy as np
import jax
import jax.numpy as jnp

def _softmax(x, axis=-1):
    return jax.nn.softmax(x, axis=axis)

def _gelu(x):
    return jax.nn.gelu(x, approximate=True)

def _silu(x):
    return jax.nn.silu(x)

def _sigmoid(x):
    return jax.nn.sigmoid(x)

def _layernorm(x, axis=-1, eps=1e-05):
    m = jnp.mean(x, axis=axis, keepdims=True)
    v = jnp.var(x, axis=axis, keepdims=True)
    return (x - m) / jnp.sqrt(v + eps)

def _scatter_add(tgt, idx, src, axis=0):
    return tgt.at[idx].add(src)

def _segment_sum(src, seg, n):
    return jax.ops.segment_sum(src, seg, n)
kernel_name = 'mk_vit_tower_d2_tok_img768_r4_787efd'

def setup_inputs(seed: int=0):
    np.random.seed(seed)
    _w = jnp.asarray

    def _rec_inputs():
        import jax
        import jax.numpy as jnp
        _rk = jax.random.key(seed)
        x = -0.00040386 + 0.999972 * jax.random.normal(jax.random.fold_in(_rk, 1), (64, 64, 64, 3), jnp.float32)
        return x
    x = _rec_inputs()

    def _L0_tok_setup():
        import jax, jax.numpy as jnp
        import numpy as np
        IMG = 64
        PATCH = 16
        C = 3
        D = 192
        NP_ = (IMG // PATCH) ** 2
        B = 64

        def _patchify(x):
            Bn, H, Wd, Cn = x.shape
            hp, wp = (H // PATCH, Wd // PATCH)
            x = x.reshape(Bn, hp, PATCH, wp, PATCH, Cn)
            x = x.transpose(0, 1, 3, 2, 4, 5)
            return x.reshape(Bn, hp * wp, PATCH * PATCH * Cn)
        key = jax.random.key(seed)
        k1, k2, k3 = jax.random.split(key, 3)
        x = jax.random.normal(k1, (B, IMG, IMG, C), dtype=jnp.float32)
        patch_dim = C * PATCH * PATCH
        W = jax.random.normal(k2, (patch_dim, D), dtype=jnp.float32) / np.sqrt(patch_dim)
        b = jnp.zeros((D,), dtype=jnp.float32)
        pos_emb = jax.random.normal(k3, (NP_, D), dtype=jnp.float32) * 0.02
        return {'x': x, 'W': W, 'b': b, 'pos_emb': pos_emb}
    _L0_tok_all = _L0_tok_setup()
    _L0_tok_in = {k: v for k, v in _L0_tok_all.items() if k in ('W', 'b', 'pos_emb')}
    del _L0_tok_all

    def _L0_attn_setup():
        import jax, jax.numpy as jnp
        import numpy as np
        NUM_HEADS = 12
        key = jax.random.key(seed)
        k1, k2 = jax.random.split(key)
        B, N, D = (8, 256, 192)
        x = jax.random.normal(k1, (B, N, D), dtype=jnp.float32)
        W_qkv = jax.random.normal(k2, (D, 3 * D), dtype=jnp.float32) * (1.0 / np.sqrt(D))
        b_qkv = jnp.zeros((3 * D,), dtype=jnp.float32)
        return {'x': x, 'W_qkv': W_qkv, 'b_qkv': b_qkv}
    _L0_attn_all = _L0_attn_setup()
    _L0_attn_in = {k: v for k, v in _L0_attn_all.items() if k in ('W_qkv', 'b_qkv')}
    del _L0_attn_all

    def _L0_ffn_setup():
        import jax, jax.numpy as jnp
        import numpy as np
        key = jax.random.key(seed)
        ks = jax.random.split(key, 6)
        B, N, D, E, S, H = (4, 1024, 192, 4, 256, 768)
        sc = lambda d: 1.0 / np.sqrt(d)
        return {'x': jax.random.normal(ks[0], (B, N, D), dtype=jnp.float32), 'phi': jax.random.normal(ks[1], (E, S, D), dtype=jnp.float32) * sc(D), 'w1': jax.random.normal(ks[2], (E, D, H), dtype=jnp.float32) * sc(D), 'b1': jnp.zeros((E, H), dtype=jnp.float32), 'w2': jax.random.normal(ks[3], (E, H, D), dtype=jnp.float32) * sc(H), 'b2': jnp.zeros((E, D), dtype=jnp.float32)}
    _L0_ffn_all = _L0_ffn_setup()
    _L0_ffn_in = {k: v for k, v in _L0_ffn_all.items() if k in ('phi', 'w1', 'b1', 'w2', 'b2')}
    del _L0_ffn_all

    def _L1_attn_setup():
        import jax, jax.numpy as jnp
        import numpy as np
        import math
        D_MODEL = 192
        N_HEADS = 6
        HD = D_MODEL // N_HEADS
        RANK = D_MODEL // 4
        B, T = (128, 64)

        def _rope_tables(T, dim):
            inv = 1.0 / 10000.0 ** (jnp.arange(0, dim, 2, dtype=jnp.float32) / dim)
            t = jnp.arange(T, dtype=jnp.float32)
            freqs = jnp.outer(t, inv)
            emb = jnp.concatenate([freqs, freqs], axis=-1)
            return (jnp.cos(emb), jnp.sin(emb))

        def _rot(x):
            h = x.shape[-1] // 2
            return jnp.concatenate([-x[..., h:], x[..., :h]], axis=-1)
        key = jax.random.key(seed)
        ks = jax.random.split(key, 8)
        s_in = 1.0 / math.sqrt(D_MODEL)
        s_r = 1.0 / math.sqrt(RANK)
        inp = {'x': jax.random.normal(ks[0], (B, T, D_MODEL), dtype=jnp.float32), 'qA': jax.random.normal(ks[1], (D_MODEL, RANK), dtype=jnp.float32) * s_in, 'qB': jax.random.normal(ks[2], (RANK, D_MODEL), dtype=jnp.float32) * s_r, 'kA': jax.random.normal(ks[3], (D_MODEL, RANK), dtype=jnp.float32) * s_in, 'kB': jax.random.normal(ks[4], (RANK, D_MODEL), dtype=jnp.float32) * s_r, 'vA': jax.random.normal(ks[5], (D_MODEL, RANK), dtype=jnp.float32) * s_in, 'vB': jax.random.normal(ks[6], (RANK, D_MODEL), dtype=jnp.float32) * s_r, 'o_w': jax.random.normal(ks[7], (D_MODEL, D_MODEL), dtype=jnp.float32) * s_in}
        return inp
    _L1_attn_all = _L1_attn_setup()
    _L1_attn_in = {k: v for k, v in _L1_attn_all.items() if k in ('qA', 'qB', 'kA', 'kB', 'vA', 'vB', 'o_w')}
    del _L1_attn_all

    def _L1_ffn_setup():
        import jax, jax.numpy as jnp
        import numpy as np
        G, E = (4, 8)
        KG, KE = (2, 2)
        D, M = (192, 768)
        SCALE = 0.02

        def _combine_weights(xf, Wg, bg, Wge, bge):
            N = xf.shape[0]
            glog = xf @ Wg + bg
            gtop, gidx = jax.lax.top_k(glog, KG)
            ggate = jax.nn.softmax(gtop, axis=-1)
            elog_all = jnp.einsum('nd,gde->nge', xf, Wge) + bge
            elog = jnp.take_along_axis(elog_all, gidx[:, :, None], axis=1)
            etop, eidx = jax.lax.top_k(elog, KE)
            egate = jax.nn.softmax(etop, axis=-1)
            w = ggate[:, :, None] * egate
            flat = gidx[:, :, None] * E + eidx
            comb = jnp.zeros((N, G * E), xf.dtype).at[jnp.arange(N)[:, None, None], flat].add(w)
            return comb
        key = jax.random.key(seed)
        ks = jax.random.split(key, 8)
        x = jax.random.normal(ks[0], (1, 128, D), jnp.float32)
        Wg = jax.random.normal(ks[1], (D, G), jnp.float32) * SCALE
        bg = jnp.zeros((G,), jnp.float32)
        Wge = jax.random.normal(ks[2], (G, D, E), jnp.float32) * SCALE
        bge = jnp.zeros((G, E), jnp.float32)
        W1 = jax.random.normal(ks[3], (G * E, D, M), jnp.float32) * SCALE
        b1 = jnp.zeros((G * E, M), jnp.float32)
        W2 = jax.random.normal(ks[4], (G * E, M, D), jnp.float32) * SCALE
        b2 = jnp.zeros((G * E, D), jnp.float32)
        return {'x': x, 'Wg': Wg, 'bg': bg, 'Wge': Wge, 'bge': bge, 'W1': W1, 'b1': b1, 'W2': W2, 'b2': b2}
    _L1_ffn_all = _L1_ffn_setup()
    _L1_ffn_in = {k: v for k, v in _L1_ffn_all.items() if k in ('Wg', 'bg', 'Wge', 'bge', 'W1', 'b1', 'W2', 'b2')}
    del _L1_ffn_all
    return {'x': x, 'L0_tok_W': _L0_tok_in['W'], 'L0_tok_b': _L0_tok_in['b'], 'L0_tok_pos_emb': _L0_tok_in['pos_emb'], 'L0_attn_W_qkv': _L0_attn_in['W_qkv'], 'L0_attn_b_qkv': _L0_attn_in['b_qkv'], 'L0_ffn_phi': _L0_ffn_in['phi'], 'L0_ffn_w1': _L0_ffn_in['w1'], 'L0_ffn_b1': _L0_ffn_in['b1'], 'L0_ffn_w2': _L0_ffn_in['w2'], 'L0_ffn_b2': _L0_ffn_in['b2'], 'L1_attn_qA': _L1_attn_in['qA'], 'L1_attn_qB': _L1_attn_in['qB'], 'L1_attn_kA': _L1_attn_in['kA'], 'L1_attn_kB': _L1_attn_in['kB'], 'L1_attn_vA': _L1_attn_in['vA'], 'L1_attn_vB': _L1_attn_in['vB'], 'L1_attn_o_w': _L1_attn_in['o_w'], 'L1_ffn_Wg': _L1_ffn_in['Wg'], 'L1_ffn_bg': _L1_ffn_in['bg'], 'L1_ffn_Wge': _L1_ffn_in['Wge'], 'L1_ffn_bge': _L1_ffn_in['bge'], 'L1_ffn_W1': _L1_ffn_in['W1'], 'L1_ffn_b1': _L1_ffn_in['b1'], 'L1_ffn_W2': _L1_ffn_in['W2'], 'L1_ffn_b2': _L1_ffn_in['b2']}

def reference(x, L0_tok_W, L0_tok_b, L0_tok_pos_emb, L0_attn_W_qkv, L0_attn_b_qkv, L0_ffn_phi, L0_ffn_w1, L0_ffn_b1, L0_ffn_w2, L0_ffn_b2, L1_attn_qA, L1_attn_qB, L1_attn_kA, L1_attn_kB, L1_attn_vA, L1_attn_vB, L1_attn_o_w, L1_ffn_Wg, L1_ffn_bg, L1_ffn_Wge, L1_ffn_bge, L1_ffn_W1, L1_ffn_b1, L1_ffn_W2, L1_ffn_b2):
    import jax
    import jax.numpy as jnp

    def _L0_tok_ref(x, W, b, pos_emb):
        import jax, jax.numpy as jnp
        import numpy as np
        IMG = 64
        PATCH = 16
        C = 3
        D = 192
        NP_ = (IMG // PATCH) ** 2
        B = 64

        def _patchify(x):
            Bn, H, Wd, Cn = x.shape
            hp, wp = (H // PATCH, Wd // PATCH)
            x = x.reshape(Bn, hp, PATCH, wp, PATCH, Cn)
            x = x.transpose(0, 1, 3, 2, 4, 5)
            return x.reshape(Bn, hp * wp, PATCH * PATCH * Cn)
        patches = _patchify(x)
        proj = jnp.einsum('bnd,de->bne', patches, W) + b
        return proj + pos_emb[None, :, :]

    def _L0_attn_ref(x, W_qkv, b_qkv):
        import jax, jax.numpy as jnp
        import numpy as np
        NUM_HEADS = 12
        B, N, D = x.shape
        H = NUM_HEADS
        Dh = D // H
        qkv = (x @ W_qkv + b_qkv).reshape(B, N, 3, H, Dh)
        q = jnp.transpose(qkv[:, :, 0], (0, 2, 1, 3))
        k = jnp.transpose(qkv[:, :, 1], (0, 2, 1, 3))
        v = jnp.transpose(qkv[:, :, 2], (0, 2, 1, 3))
        att = jnp.einsum('bhid,bhjd->bhij', q, k)
        att = jax.nn.softmax(att, axis=-1)
        out = jnp.einsum('bhij,bhjd->bhid', att, v)
        return out.transpose(0, 2, 1, 3).reshape(B, N, D)

    def _L0_ffn_ref(x, phi, w1, b1, w2, b2):
        import jax, jax.numpy as jnp
        import numpy as np
        logits = jnp.einsum('bnd,esd->bnes', x, phi)
        B, N, E, S = logits.shape
        dispatch = jax.nn.softmax(logits, axis=1)
        combine = jax.nn.softmax(logits.reshape(B, N, E * S), axis=-1).reshape(B, N, E, S)
        slots = jnp.einsum('bnd,bnes->besd', x, dispatch)
        h = jax.nn.gelu(jnp.einsum('besd,edh->besh', slots, w1) + b1[None, :, None, :])
        y = jnp.einsum('besh,ehd->besd', h, w2) + b2[None, :, None, :]
        out = jnp.einsum('besd,bnes->bnd', y, combine)
        return out

    def _L1_attn_ref(x, qA, qB, kA, kB, vA, vB, o_w):
        import jax, jax.numpy as jnp
        import numpy as np
        import math
        D_MODEL = 192
        N_HEADS = 6
        HD = D_MODEL // N_HEADS
        RANK = D_MODEL // 4
        B, T = (128, 64)

        def _rope_tables(T, dim):
            inv = 1.0 / 10000.0 ** (jnp.arange(0, dim, 2, dtype=jnp.float32) / dim)
            t = jnp.arange(T, dtype=jnp.float32)
            freqs = jnp.outer(t, inv)
            emb = jnp.concatenate([freqs, freqs], axis=-1)
            return (jnp.cos(emb), jnp.sin(emb))

        def _rot(x):
            h = x.shape[-1] // 2
            return jnp.concatenate([-x[..., h:], x[..., :h]], axis=-1)
        Bb, Tt, _ = x.shape

        def proj(A, W):
            h = x @ A @ W
            return h.reshape(Bb, Tt, N_HEADS, HD).transpose(0, 2, 1, 3)
        q = proj(qA, qB)
        k = proj(kA, kB)
        v = proj(vA, vB)
        cos, sin = _rope_tables(Tt, HD)
        q = q * cos + _rot(q) * sin
        k = k * cos + _rot(k) * sin
        att = jnp.einsum('bhqd,bhkd->bhqk', q, k) / math.sqrt(HD)
        causal = jnp.tril(jnp.ones((Tt, Tt), dtype=bool))
        att = jnp.where(causal, att, -jnp.inf)
        att = jax.nn.softmax(att, axis=-1)
        out = jnp.einsum('bhqk,bhkd->bhqd', att, v)
        out = out.transpose(0, 2, 1, 3).reshape(Bb, Tt, D_MODEL)
        return out @ o_w

    def _L1_ffn_ref(x, Wg, bg, Wge, bge, W1, b1, W2, b2):
        import jax, jax.numpy as jnp
        import numpy as np
        G, E = (4, 8)
        KG, KE = (2, 2)
        D, M = (192, 768)
        SCALE = 0.02

        def _combine_weights(xf, Wg, bg, Wge, bge):
            N = xf.shape[0]
            glog = xf @ Wg + bg
            gtop, gidx = jax.lax.top_k(glog, KG)
            ggate = jax.nn.softmax(gtop, axis=-1)
            elog_all = jnp.einsum('nd,gde->nge', xf, Wge) + bge
            elog = jnp.take_along_axis(elog_all, gidx[:, :, None], axis=1)
            etop, eidx = jax.lax.top_k(elog, KE)
            egate = jax.nn.softmax(etop, axis=-1)
            w = ggate[:, :, None] * egate
            flat = gidx[:, :, None] * E + eidx
            comb = jnp.zeros((N, G * E), xf.dtype).at[jnp.arange(N)[:, None, None], flat].add(w)
            return comb
        shp = x.shape
        xf = x.reshape(-1, D)
        comb = _combine_weights(xf, Wg, bg, Wge, bge)
        h = jax.nn.gelu(jnp.einsum('nd,edm->nem', xf, W1) + b1, approximate=False)
        y = jnp.einsum('nem,emd->ned', h, W2) + b2
        out = jnp.einsum('ne,ned->nd', comb, y)
        return out.reshape(shp)
    h = _L0_tok_ref(x, L0_tok_W, L0_tok_b, L0_tok_pos_emb)
    h = h + _L0_attn_ref(_layernorm(h, axis=-1), L0_attn_W_qkv, L0_attn_b_qkv)
    h = h + _L0_ffn_ref(_layernorm(h, axis=-1), L0_ffn_phi, L0_ffn_w1, L0_ffn_b1, L0_ffn_w2, L0_ffn_b2)
    h = h + _L1_attn_ref(_layernorm(h, axis=-1), L1_attn_qA, L1_attn_qB, L1_attn_kA, L1_attn_kB, L1_attn_vA, L1_attn_vB, L1_attn_o_w)
    h = h + _L1_ffn_ref(_layernorm(h, axis=-1), L1_ffn_Wg, L1_ffn_bg, L1_ffn_Wge, L1_ffn_bge, L1_ffn_W1, L1_ffn_b1, L1_ffn_W2, L1_ffn_b2)
    return h

_drawn_inputs = setup_inputs


def setup_inputs(seed=0):
    import zlib

    import numpy as np

    out = dict(_drawn_inputs(seed))
    spreads = {'L0_tok_b': (0.0, 0.1),
     'L0_attn_b_qkv': (0.0, 0.1),
     'L0_ffn_b1': (0.0, 0.31),
     'L0_ffn_b2': (0.0, 0.1),
     'L1_ffn_bg': (0.0, 0.363),
     'L1_ffn_bge': (0.0, 0.273),
     'L1_ffn_b1': (0.0, 0.718),
     'L1_ffn_b2': (0.0, 0.1)}
    factors = {'L0_ffn_phi': 4.353}
    for name, (base, spread) in spreads.items():
        noise = np.random.default_rng([zlib.crc32(name.encode()), seed]).standard_normal(out[name].shape)
        drawn = base * np.exp(spread * noise) if base else spread * noise
        out[name] = jnp.asarray(drawn.astype(out[name].dtype))
    for name, factor in factors.items():
        out[name] = (out[name] * factor).astype(out[name].dtype)
    return out
```

```python
import numpy as np

import concourse.bass as bass
from concourse import mybir
from contextlib import ExitStack

F32 = mybir.dt.float32
BF16 = mybir.dt.bfloat16
U32 = mybir.dt.uint32
I32 = mybir.dt.int32
ACT = mybir.ActivationFunctionType
ALU = mybir.AluOpType
AX = mybir.AxisListType

P = 128
IMAGES, PATCHES, D = 64, 16, 192
TOKENS = IMAGES * PATCHES
TILES = TOKENS // P
TILE_IMAGES = P // PATCHES
KD, NKD = 96, 2
PATCH_CHUNKS = 768 // P
EPS = 1e-5
BIG = float(2.0 ** 100)
SLOT_E, SLOTS, HID = 4, 256, 768
ALL_SLOTS = SLOT_E * SLOTS
SLOT_CHUNKS = ALL_SLOTS // P
HC = HID // P
HALF = HID // 2
PAIRS = ((0, 0), (0, 1), (0, 2), (1, 0), (1, 1), (2, 0))
PROWS = len(PAIRS) * PATCHES
BROWS = PROWS + 3
G1, E1 = 4, 8
EXPERTS = G1 * E1
TOPK = 4
MOE_TILES = (TOPK * TOKENS + EXPERTS * (P - 1)) // P
LANE_BITS = 7


class Chain:

    def __init__(self, eng, sem, base=0, turn=None):
        self.eng, self.sem, self.base, self.n, self.turn = eng, sem, base, 0, turn

    def after(self, ins):
        self.n += 1
        ins.then_inc(self.sem, 1)
        self.eng.wait_ge(self.sem, self.base + self.n)
        if self.turn is not None:
            self.eng.sem_inc(self.turn, 1)


class Scope(ExitStack):

    ended = []

    def __init__(self, nc, stage):
        super().__init__()
        self.nc, self.stage = nc, stage

    def sb(self, name, shape, dt=F32):
        return self.enter_context(self.nc.sbuf_tensor(f"{self.stage}_{name}", shape, dt))

    def ps(self, name, shape, dt=F32):
        return self.enter_context(self.nc.psum_tensor(f"{self.stage}_{name}", shape, dt))

    def sem(self, name):
        sem = self.nc.alloc_semaphore(f"{self.stage}_{name}")
        Scope.ended.append(sem)
        return sem

    @staticmethod
    def retire(nc):
        nc.clear_and_free_semaphores(Scope.ended)
        nc.all_engine_barrier()
        Scope.ended = []

    def block(self):
        return self.enter_context(self.nc.Block())


def embed(nc, g, xT, tokW, pos_rows, tok_b_rows):
    with Scope(nc, "emb") as s:
        x_sb = s.sb("x", [P, PATCH_CHUNKS, TOKENS])
        w_sb = s.sb("w", [P, PATCH_CHUNKS, D])
        pos = s.sb("pos", [P, D])
        tokb = s.sb("tokb", [P, D])
        acc = [s.ps(f"acc{i}", [P, 512]) for i in range(TILES)]
        w_in = [s.sem(f"w_in{j}") for j in range(PATCH_CHUNKS)]
        rows_in, bias_ready, acc_ready, h_done = (s.sem(n) for n in ("rows_in", "bias_ready", "acc_ready", "h_done"))
        block = s.block()

        @block.sync
        def _(sp):
            for j in range(PATCH_CHUNKS):
                sp.dma_start(w_sb[:, j, :], tokW[:, j, :]).then_inc(w_in[j], 16)
                sp.dma_start(x_sb[:, j, :], xT[:, j, :]).then_inc(w_in[j], 16)
            sp.dma_start(g.phi[:], g.d_phi).then_inc(g.phi_in, 16)
            sp.dma_start(g.w1[:], g.d_w1).then_inc(g.w1_in, 16)

        @block.scalar
        def _(act):
            act.dma_start(pos[:], pos_rows).then_inc(rows_in, 16)
            act.dma_start(tokb[:], tok_b_rows).then_inc(rows_in, 16)
            act.dma_start(g.ident[:], g.d_ident).then_inc(g.ident_in, 16)
            act.dma_start(g.w2[:], g.d_w2).then_inc(g.w2_in, 16)

        @block.tensor
        def _(pe):
            for j in range(PATCH_CHUNKS):
                pe.wait_ge(w_in[j], 32)
                for i in range(TILES):
                    mm = pe.matmul(acc[i][:, 0:D], x_sb[:, j, i * P:(i + 1) * P], w_sb[:, j, :],
                                   start=(j == 0), stop=(j == PATCH_CHUNKS - 1))
                    if j == PATCH_CHUNKS - 1:
                        mm.then_inc(acc_ready, 1)

        @block.vector
        def _(dve):
            dve.wait_ge(rows_in, 32)
            dve.tensor_tensor(pos[:], pos[:], tokb[:], ALU.add).then_inc(bias_ready, 1)
            dve.wait_ge(bias_ready, 1)
            for i in range(TILES):
                dve.wait_ge(acc_ready, i + 1)
                dve.tensor_tensor(g.h[:, i, :], acc[i][:, 0:D], pos[:], ALU.add).then_inc(h_done, 1)
            dve.wait_ge(h_done, TILES)


def layernorm(nc, g, stage):
    with Scope(nc, stage) as s:
        stats = s.sb("stats", [P, TILES, 6])
        mv = s.sb("mv", [P, TILES, 2])
        ve, sd, r, t, nmr = (s.sb(n, [P, TILES]) for n in ("ve", "sd", "r", "t", "nmr"))
        psT = [s.ps(f"psT{i}", [P, 512]) for i in range(TILES // 2)]
        step, var_ready, sd_ready, xn_ready, t_ready, xnT_done = (
            s.sem(n) for n in ("step", "var_ready", "sd_ready", "xn_ready", "t_ready", "xnT_done"))
        block = s.block()

        @block.vector
        def _(dve):
            c = Chain(dve, step)
            for i in range(TILES):
                c.after(dve.bn_stats(stats[:, i, :], g.h[:, i, :]))
            for i in range(TILES):
                c.after(dve.bn_aggr(mv[:, i, :], stats[:, i, :]))
            dve.tensor_scalar(ve[:], mv[:, :, 1], EPS, None, ALU.add).then_inc(var_ready, 1)
            dve.wait_ge(sd_ready, 1)
            c.after(dve.reciprocal(r[:], sd[:]))
            c.after(dve.tensor_tensor(t[:], r[:], r[:], ALU.mult))
            c.after(dve.tensor_tensor(t[:], t[:], ve[:], ALU.mult))
            c.after(dve.tensor_scalar(t[:], t[:], -0.5, 1.5, ALU.mult, ALU.add))
            c.after(dve.tensor_tensor(r[:], r[:], t[:], ALU.mult))
            c.after(dve.scalar_tensor_tensor(nmr[:], mv[:, :, 0], -1.0, r[:], ALU.mult, ALU.mult))
            for i in range(TILES):
                dve.tensor_scalar(g.xn[:, i, :], g.h[:, i, :], r[:, i:i + 1], nmr[:, i:i + 1],
                                  ALU.mult, ALU.add).then_inc(xn_ready, 1)

        @block.tensor
        def _(pe):
            pe.wait_ge(g.ident_in, 16)
            for i in range(TILES):
                pe.wait_ge(xn_ready, i + 1)
                for k in range(NKD):
                    at = (i % 2 * NKD + k) * P
                    tr = pe.transpose(psT[i // 2][0:KD, at:at + P], g.xn[:, i, k * KD:(k + 1) * KD], g.ident[:])
                tr.then_inc(t_ready, 1)

        @block.scalar
        def _(act):
            act.wait_ge(var_ready, 1)
            act.activation(sd[:], ve[:], ACT.Sqrt).then_inc(sd_ready, 1)
            for j in range(TILES // 2):
                act.wait_ge(t_ready, 2 * j + 2)
                for k in range(NKD):
                    src = psT[j][0:KD, :].rearrange("p (i k c) -> p i k c", i=2, k=NKD)[:, :, k, :]
                    dst = g.xnT[:, k, 2 * j * P:(2 * j + 2) * P].rearrange("p (i c) -> p i c", i=2)
                    act.activation(dst, src, ACT.Copy).then_inc(xnT_done, 1)


HEADS_U = 6


class Attend:

    def __init__(self, s, g, units, scale, rows, heads_per_group):
        self.s, self.g, self.units, self.scale = s, g, units, scale
        self.qT = s.sb("qT", [rows, 2, TOKENS])
        self.kT = s.sb("kT", [KD, 2, TOKENS])
        self.kTm = s.sb("kTm", [rows, 2, HEADS_U, P])
        self.hm = s.sb("hm", [KD, heads_per_group])
        self.v = s.sb("v", [P, TILES, D])
        self.nmax, self.rsum, self.rinv = (s.sb(n, [P, 2, HEADS_U]) for n in ("nmax", "rsum", "rinv"))
        self.prob = s.sb("prob", [P, 2, HEADS_U, P])
        self.probT = s.sb("probT", [P, 2, HEADS_U, P])
        self.sc = [s.ps(f"sc{i}", [P, 2, 512]) for i in range(2)]
        self.pt = [s.ps(f"pt{i}", [P, 512]) for i in range(2)]
        self.av = [s.ps(f"av{i}", [P, 512]) for i in range(2)]
        (self.km_ready, self.sc_ready, self.max_raw, self.max_ready, self.exp_done, self.rinv_ready, self.prob_ready,
         self.pt_ready, self.ptc_act, self.ptc_dve, self.av_ready, self.av_done) = (
            s.sem(n) for n in ("km_ready", "sc_ready", "max_raw", "max_ready", "exp_done", "rinv_ready", "prob_ready",
                               "pt_ready", "ptc_act", "ptc_dve", "av_ready", "av_done"))

    def scores(self, pe, u, operands):
        pe.wait_ge(self.km_ready, u + 1)
        if u >= 2:
            pe.wait_ge(self.exp_done, HEADS_U * (u - 1))
        for b in range(2):
            q, k = operands(u, b)
            mm = pe.matmul(self.sc[u % 2][:, b, 0:3 * P], q, k, start=True, stop=True)
        mm.then_inc(self.sc_ready, 1)

    def transposes(self, pe, u):
        pe.wait_ge(self.prob_ready, u + 1)
        if u >= 1:
            pe.wait_ge(self.ptc_act, u)
            pe.wait_ge(self.ptc_dve, u)
        for hd in range(HEADS_U):
            tr = pe.transpose(self.pt[hd // 4][:, (hd % 4) * P:(hd % 4 + 1) * P], self.prob[:, u % 2, hd, :], self.g.ident[:])
        tr.then_inc(self.pt_ready, 1)

    def wait_values(self, pe, u):
        pe.wait_ge(self.ptc_act, u + 1)
        pe.wait_ge(self.ptc_dve, u + 1)
        if u >= 2:
            pe.wait_ge(self.av_done, u - 1)

    def exps(self, act, u):
        act.wait_ge(self.max_ready, u + 1)
        if u >= 2:
            act.wait_ge(self.pt_ready, u - 1)
            act.wait_ge(self.rinv_ready, u - 1)
        for hd in range(HEADS_U):
            act.activation(self.prob[:, u % 2, hd, :], self.sc[u % 2][:, hd // 3, (hd % 3) * P:(hd % 3 + 1) * P], ACT.Exp,
                           bias=self.nmax[:, u % 2, hd:hd + 1], scale=self.scale,
                           accum_out=self.rsum[:, u % 2, hd:hd + 1]).then_inc(self.exp_done, 1)

    def leave_act(self, act, u):
        act.wait_ge(self.pt_ready, u + 1)
        if u >= 2:
            act.wait_ge(self.av_ready, u - 1)
        act.activation(self.probT[:, u % 2, 0:4, :], self.pt[0][:].rearrange("p (h c) -> p h c", h=4), ACT.Copy
                       ).then_inc(self.ptc_act, 1)

    def leave_dve(self, dve, u):
        dve.wait_ge(self.pt_ready, u + 1)
        if u >= 2:
            dve.wait_ge(self.av_ready, u - 1)
        dve.tensor_copy(self.probT[:, u % 2, 4:6, :], self.pt[1][:, 0:2 * P].rearrange("p (h c) -> p h c", h=2)
                        ).then_inc(self.ptc_dve, 1)

    def maximum(self, dve, u):
        dve.wait_ge(self.sc_ready, u + 1)
        if u >= 2:
            dve.wait_ge(self.exp_done, HEADS_U * (u - 1))
        b = u % 2
        dve.tensor_reduce(self.nmax[:, b, :].rearrange("p (a h) -> p a h", a=2),
                          self.sc[b][:, :, 0:3 * P].rearrange("p a (h c) -> p a h c", h=3), AX.X, ALU.max, negate=True
                          ).then_inc(self.max_raw, 1)
        dve.wait_ge(self.max_raw, u + 1)
        dve.tensor_scalar(self.nmax[:, b, :], self.nmax[:, b, :], self.scale, None, ALU.mult).then_inc(self.max_ready, 1)

    def inverse(self, dve, u):
        dve.wait_ge(self.exp_done, HEADS_U * (u + 1))
        dve.reciprocal(self.rinv[:, u % 2, :], self.rsum[:, u % 2, :]).then_inc(self.rinv_ready, 1)
        dve.wait_ge(self.rinv_ready, u + 1)


def attention0(nc, g, a):
    DH, GH = 16, 6
    KM = KD + TILE_IMAGES
    UNITS = 2 * TILES
    with Scope(nc, "at0") as s:
        w = s.sb("w", [KD, NKD, 3 * D])
        bias = s.sb("bias", [KD, 4])
        bv = s.sb("bv", [P, D])
        o = s.sb("o", [P, 2, D // 2])
        t = Attend(s, g, UNITS, 1.0, KM, GH)
        w_in, qk_ready, qk_done, v_ready, v_done, step = (
            s.sem(n) for n in ("w_in", "qk_ready", "qk_done", "v_ready", "v_done", "step"))
        banks = [t.sc[0][:, 0], t.sc[0][:, 1], t.sc[1][:, 0], t.sc[1][:, 1], t.pt[0][:], t.pt[1][:], t.av[0][:], t.av[1][:]]
        loads = [(w[:], a["wqkv"]), (bias[:], a["bqk"]), (bv[:], a["bv_rows"]), (t.hm[:], a["head_mask0"])]
        for b in range(2):
            loads.append((t.qT[KD:KM, b, :], a["mask_q"][0:TILE_IMAGES]))
            loads.append((t.kTm[KD:KM, b, :, :], a["mask_k"][0:TILE_IMAGES]))
        block = s.block()

        @block.sync
        def _(sp):
            for dst, src in loads:
                sp.dma_start(dst, src).then_inc(w_in, 16)

        @block.tensor
        def _(pe):
            pe.wait_ge(w_in, 16 * len(loads))
            for n in range(8):
                part, half = n // 2, n % 2
                for k in range(NKD):
                    mm = pe.matmul(banks[n][0:KD, :], w[:, k, part * KD:(part + 1) * KD],
                                   g.xnT[:, k, half * 512:(half + 1) * 512], start=(k == 0), stop=(k == NKD - 1))
                mm.then_inc(qk_ready, 1)
            for i in range(TILES):
                pe.wait_ge(qk_done, i + 1)
                for k in range(NKD):
                    mm = pe.matmul(banks[i][:, 0:D], g.xnT[:, k, i * P:(i + 1) * P], w[:, k, 2 * D:3 * D],
                                   start=(k == 0), stop=(k == NKD - 1))
                mm.then_inc(v_ready, 1)

            def operands(u, b):
                i, grp = u // 2, u % 2
                return t.qT[:, grp, i * P:(i + 1) * P], t.kTm[:, u % 2, 3 * b:3 * b + 3, :]

            def values(u):
                i, grp = u // 2, u % 2
                t.wait_values(pe, u)
                for hd in range(GH):
                    at = (grp * GH + hd) * DH
                    mm = pe.matmul(t.av[u % 2][:, hd * DH:(hd + 1) * DH], t.probT[:, u % 2, hd, :], t.v[:, i, at:at + DH],
                                   start=True, stop=True)
                mm.then_inc(t.av_ready, 1)

            pe.wait_ge(v_done, TILES)
            t.scores(pe, 0, operands)
            for u in range(UNITS):
                if u + 1 < UNITS:
                    t.scores(pe, u + 1, operands)
                t.transposes(pe, u)
                if u >= 1:
                    values(u - 1)
            values(UNITS - 1)

        @block.scalar
        def _(act):
            act.wait_ge(w_in, 16 * len(loads))
            for n in range(8):
                part, half = n // 2, n % 2
                act.wait_ge(qk_ready, n + 1)
                dst = (t.qT[0:KD] if part < 2 else t.kT[:])[:, part % 2, half * 512:(half + 1) * 512]
                act.activation(dst, banks[n][0:KD, :], ACT.Identity, bias=bias[:, part:part + 1]).then_inc(qk_done, 1)
            for u in range(UNITS):
                t.exps(act, u)
                t.leave_act(act, u)

        @block.vector
        def _(dve):
            c = Chain(dve, step)
            dve.wait_ge(w_in, 16 * len(loads))
            for i in range(TILES):
                dve.wait_ge(v_ready, i + 1)
                dve.tensor_tensor(t.v[:, i, :], banks[i][:, 0:D], bv[:], ALU.add).then_inc(v_done, 1)

            def keys(u):
                i, grp = u // 2, u % 2
                if u >= 2:
                    dve.wait_ge(t.sc_ready, u - 1)
                for hd in range(GH):
                    op = dve.tensor_scalar(t.kTm[0:KD, u % 2, hd, :], t.kT[:, grp, i * P:(i + 1) * P],
                                           t.hm[:, hd:hd + 1], None, ALU.mult)
                op.then_inc(t.km_ready, 1)

            def finish(u):
                i, grp = u // 2, u % 2
                hs = g.h[:, i, grp * 96:(grp + 1) * 96]
                dve.wait_ge(t.av_ready, u + 1)
                dve.tensor_tensor(o[:, u % 2, :].rearrange("p (h d) -> p h d", h=GH),
                                  t.av[u % 2][:, 0:GH * DH].rearrange("p (h d) -> p h d", h=GH),
                                  t.rinv[:, u % 2, :].unsqueeze(2).to_broadcast([P, GH, DH]), ALU.mult).then_inc(t.av_done, 1)
                dve.wait_ge(t.av_done, u + 1)
                c.after(dve.tensor_tensor(hs, hs, o[:, u % 2, :], ALU.add))

            dve.wait_ge(qk_done, 8)
            keys(0)
            keys(1)
            for u in range(UNITS):
                t.maximum(dve, u)
                if u + 2 < UNITS:
                    keys(u + 2)
                t.inverse(dve, u)
                dve.sem_inc(t.prob_ready, 1)
                t.leave_dve(dve, u)
                if u >= 1:
                    finish(u - 1)
            finish(UNITS - 1)


def attention1(nc, g, a):
    DH, GH, RANK = 32, 3, 48
    KM = KD + TILE_IMAGES + PATCHES
    UNITS = TILES
    with Scope(nc, "at1") as s:
        wa = s.sb("wa", [KD, NKD, 3, RANK])
        wb = s.sb("wb", [RANK, 3, D])
        wr = s.sb("wr", [RANK, 2, D])
        ow = s.sb("ow", [KD, NKD, D])
        low = s.sb("low", [RANK, 3, TOKENS])
        cosT, sinT = (s.sb(n, [KD, 512]) for n in ("cosT", "sinT"))
        rope = s.sb("rope", [KD, 2, 2, 512])
        oT = s.sb("oT", [KD, 2, 2, P])
        t = Attend(s, g, UNITS, 1.0 / float(np.sqrt(DH)), KM, GH)
        w_in, rot_ready, low_ready, low_done, qk_ready, cs_done, rope_done, v_ready, v_done, oT_ready, o_ready, o_done, step = (
            s.sem(n) for n in ("w_in", "rot_ready", "low_ready", "low_done", "qk_ready", "cs_done", "rope_done", "v_ready",
                               "v_done", "oT_ready", "o_ready", "o_done", "step"))
        banks = [t.sc[0][:, 0], t.sc[0][:, 1], t.sc[1][:, 0], t.sc[1][:, 1], t.pt[0][:], t.pt[1][:], t.av[0][:], t.av[1][:]]
        loads = [(ow[:], a["o_w"]), (t.hm[:], a["head_mask1"]), (cosT[:], a["cosT"]), (sinT[:], a["sinT"])]
        for n, x in enumerate("qkv"):
            loads += [(wa[:, :, n, :], a[x + "A"]), (wb[:, n, :], a[x + "B"])]
        for b in range(2):
            loads.append((t.qT[KD:KM, b, :], a["mask_q"]))
            loads.append((t.kTm[KD:KM, b, :, :], a["mask_k"]))
        block = s.block()

        @block.sync
        def _(sp):
            for dst, src in loads:
                sp.dma_start(dst, src).then_inc(w_in, 16)

        parts = [(x, grp, half) for x in range(2) for grp in range(2) for half in range(2)]

        @block.tensor
        def _(pe):
            pe.wait_ge(w_in, 16 * len(loads))
            for n in range(6):
                x, half = n // 2, n % 2
                for k in range(NKD):
                    mm = pe.matmul(banks[n][0:RANK, :], wa[:, k, x, :], g.xnT[:, k, half * 512:(half + 1) * 512],
                                   start=(k == 0), stop=(k == NKD - 1))
                mm.then_inc(low_ready, 1)
            pe.wait_ge(low_done, 6)
            pe.wait_ge(rot_ready, 4)
            for n, (x, grp, half) in enumerate(parts):
                if n >= 4:
                    pe.wait_ge(cs_done, 2 * (n - 3))
                for r, m in enumerate((wb, wr)):
                    mm = pe.matmul(banks[2 * (n % 4) + r][0:KD, :], m[:, x, grp * KD:(grp + 1) * KD],
                                   low[:, x, half * 512:(half + 1) * 512], start=True, stop=True)
                mm.then_inc(qk_ready, 1)
            for i in range(TILES):
                pe.wait_ge(cs_done, 2 * (5 + i // 2))
                pe.matmul(banks[i][:, 0:D], low[:, 2, i * P:(i + 1) * P], wb[:, 2, :], start=True, stop=True).then_inc(v_ready, 1)

            def operands(u, b):
                return t.qT[:, b, u * P:(u + 1) * P], t.kTm[:, u % 2, 3 * b:3 * b + 3, :]

            def values(u):
                t.wait_values(pe, u)
                for hd in range(HEADS_U):
                    grp, j = hd // GH, hd % GH
                    mm = pe.matmul(t.av[u % 2][j * DH:(j + 1) * DH, grp * P:(grp + 1) * P], t.v[:, u, hd * DH:(hd + 1) * DH],
                                   t.probT[:, u % 2, hd, :], start=True, stop=True)
                mm.then_inc(t.av_ready, 1)

            def project(u):
                pe.wait_ge(oT_ready, u + 1)
                for k in range(NKD):
                    mm = pe.matmul(t.av[u % 2][:, 256:256 + D], oT[:, u % 2, k, :], ow[:, k, :],
                                   start=(k == 0), stop=(k == NKD - 1))
                mm.then_inc(o_ready, 1)

            pe.wait_ge(v_done, TILES)
            t.scores(pe, 0, operands)
            for u in range(UNITS):
                if u + 1 < UNITS:
                    t.scores(pe, u + 1, operands)
                t.transposes(pe, u)
                if u >= 2:
                    project(u - 2)
                if u >= 1:
                    values(u - 1)
            project(UNITS - 2)
            values(UNITS - 1)
            project(UNITS - 1)

        @block.scalar
        def _(act):
            for n in range(6):
                x, half = n // 2, n % 2
                act.wait_ge(low_ready, n + 1)
                act.activation(low[:, x, half * 512:(half + 1) * 512], banks[n][0:RANK, :], ACT.Copy).then_inc(low_done, 1)

            def leave_values(u):
                act.wait_ge(t.av_ready, u + 1)
                if u >= 2:
                    act.wait_ge(o_ready, u - 1)
                act.activation(oT[:, u % 2, :, :], t.av[u % 2][0:KD, 0:2 * P].rearrange("p (g c) -> p g c", g=2), ACT.Copy
                               ).then_inc(oT_ready, 1)

            for u in range(UNITS):
                t.exps(act, u)
                if u >= 2:
                    leave_values(u - 2)
                t.leave_act(act, u)
            leave_values(UNITS - 2)
            leave_values(UNITS - 1)

        @block.vector
        def _(dve):
            c = Chain(dve, step)
            dve.wait_ge(w_in, 16 * len(loads))
            for x in range(2):
                src = wb[:, x, :].rearrange("p (h r d) -> p h r d", h=HEADS_U, r=2)
                dst = wr[:, x, :].rearrange("p (h r d) -> p h r d", h=HEADS_U, r=2)
                dve.tensor_scalar(dst[:, :, 0, :], src[:, :, 1, :], -1.0, None, ALU.mult).then_inc(rot_ready, 1)
                dve.tensor_copy(dst[:, :, 1, :], src[:, :, 0, :]).then_inc(rot_ready, 1)
            for n, (x, grp, half) in enumerate(parts):
                dst = (t.qT[0:KD] if x == 0 else t.kT[:])[:, grp, half * 512:(half + 1) * 512]
                dve.wait_ge(qk_ready, n + 1)
                if n >= 2:
                    dve.wait_ge(rope_done, n - 1)
                dve.tensor_tensor(rope[:, n % 2, 0, :], banks[2 * (n % 4)][0:KD, :], cosT[:], ALU.mult).then_inc(cs_done, 1)
                dve.tensor_tensor(rope[:, n % 2, 1, :], banks[2 * (n % 4) + 1][0:KD, :], sinT[:], ALU.mult).then_inc(cs_done, 1)
                dve.wait_ge(cs_done, 2 * n + 2)
                dve.tensor_tensor(dst, rope[:, n % 2, 0, :], rope[:, n % 2, 1, :], ALU.add).then_inc(rope_done, 1)
            for i in range(TILES):
                dve.wait_ge(v_ready, i + 1)
                dve.tensor_copy(t.v[:, i, :], banks[i][:, 0:D]).then_inc(v_done, 1)

            def keys(u):
                if u >= 2:
                    dve.wait_ge(t.sc_ready, u - 1)
                for j in range(GH):
                    op = dve.tensor_scalar(t.kTm[0:KD, u % 2, :, :].rearrange("p (g h) c -> p g h c", g=2)[:, :, j, :],
                                           t.kT[:, :, u * P:(u + 1) * P], t.hm[:, j:j + 1], None, ALU.mult)
                op.then_inc(t.km_ready, 1)

            def finish(u):
                dve.wait_ge(o_ready, u + 1)
                dve.tensor_tensor(g.h[:, u, :], g.h[:, u, :], t.av[u % 2][:, 256:256 + D], ALU.add).then_inc(t.av_done, 1)

            dve.wait_ge(rope_done, len(parts))
            keys(0)
            keys(1)
            for u in range(UNITS):
                t.maximum(dve, u)
                if u + 2 < UNITS:
                    keys(u + 2)
                t.inverse(dve, u)
                dve.tensor_tensor(t.prob[:, u % 2], t.prob[:, u % 2], t.rinv[:, u % 2, :].unsqueeze(2).to_broadcast([P, HEADS_U, P]),
                                  ALU.mult).then_inc(t.prob_ready, 1)
                t.leave_dve(dve, u)
                if u >= 2:
                    finish(u - 2)
            finish(UNITS - 2)
            finish(UNITS - 1)
            dve.wait_ge(t.av_done, UNITS)


def slot_weights(nc, g, CT, Dn, zn):
    with Scope(nc, "slw") as s:
        nmax, zsum, rz = (s.sb(n, [P, 2]) for n in ("nmax", "zsum", "rz"))
        ze = s.sb("ze", [P, 2, SLOT_E])
        ex = s.sb("ex", [P, 2, ALL_SLOTS])
        dmax, dsum = (s.sb(n, [P, 2, IMAGES]) for n in ("dmax", "dsum"))
        cl = s.ps("cl", [P, 2, 512])
        dl = s.ps("dl", [P, 2, 2, 512])
        tp = s.ps("tp", [P, 2, 512])
        step, cl_ready, cmax_ready, cexp_ready, cw_ready, tp_ready, ct_done, dl_ready, dsub_ready, dexp_ready = (
            s.sem(n) for n in ("step", "cl_ready", "cmax_ready", "cexp_ready", "cw_ready", "tp_ready", "ct_done",
                               "dl_ready", "dsub_ready", "dexp_ready"))
        block = s.block()

        @block.tensor
        def _(pe):
            pe.wait_ge(g.phi_in, 16)

            def combine_transposed(i):
                pe.wait_ge(cw_ready, i + 1)
                if i >= 1:
                    pe.wait_ge(ct_done, i)
                for c in range(SLOT_CHUNKS):
                    tr = pe.transpose(tp[:, c // 4, (c % 4) * P:(c % 4 + 1) * P], ex[:, i % 2, c * P:(c + 1) * P], g.ident[:])
                tr.then_inc(tp_ready, 1)

            for i in range(TILES):
                if i >= 1:
                    pe.wait_ge(cexp_ready, SLOT_E * i)
                for half in range(2):
                    for k in range(NKD):
                        mm = pe.matmul(cl[:, half, :], g.xnT[:, k, i * P:(i + 1) * P], g.phi[:, k, half * 512:(half + 1) * 512],
                                       start=(k == 0), stop=(k == NKD - 1))
                mm.then_inc(cl_ready, 1)
                if i >= 2:
                    pe.wait_ge(dsub_ready, i - 1)
                for half in range(2):
                    for k in range(NKD):
                        mm = pe.matmul(dl[:, i % 2, half, :], g.phi[:, k, i * P:(i + 1) * P], g.xnT[:, k, half * 512:(half + 1) * 512],
                                       start=(k == 0), stop=(k == NKD - 1))
                mm.then_inc(dl_ready, 1)
                if i >= 1:
                    combine_transposed(i - 1)
            combine_transposed(TILES - 1)

        @block.scalar
        def _(act):
            def leave(i):
                act.wait_ge(tp_ready, i + 1)
                act.activation(CT[:, :, i * P:(i + 1) * P], tp[:].rearrange("p a (c t) -> p (a c) t", c=4), ACT.Copy).then_inc(ct_done, 1)

            for i in range(TILES):
                act.wait_ge(cmax_ready, i + 1)
                if i >= 2:
                    act.wait_ge(tp_ready, i - 1)
                for e in range(SLOT_E):
                    act.activation(ex[:, i % 2, e * SLOTS:(e + 1) * SLOTS], cl[:, e // 2, (e % 2) * SLOTS:(e % 2 + 1) * SLOTS],
                                   ACT.Exp, bias=nmax[:, i % 2:i % 2 + 1], accum_out=ze[:, i % 2, e:e + 1]).then_inc(cexp_ready, 1)
                act.wait_ge(dsub_ready, i + 1)
                act.activation(Dn[:, i, :], Dn[:, i, :], ACT.Exp).then_inc(dexp_ready, 1)
                if i >= 1:
                    leave(i - 1)
            leave(TILES - 1)

        @block.vector
        def _(dve):
            c = Chain(dve, step)

            def by_image(x):
                return x.rearrange("p (b n) -> p b n", n=PATCHES)

            def spread(x):
                return x.unsqueeze(2).to_broadcast([P, IMAGES, PATCHES])

            def normalise(i):
                b = i % 2
                dve.wait_ge(dexp_ready, i + 1)
                c.after(dve.tensor_reduce(dsum[:, b, :], by_image(Dn[:, i, :]), AX.X, ALU.add))
                c.after(dve.reciprocal(dsum[:, b, :], dsum[:, b, :]))
                c.after(dve.tensor_tensor(by_image(Dn[:, i, :]), by_image(Dn[:, i, :]), spread(dsum[:, b, :]), ALU.mult))

            for i in range(TILES):
                b = i % 2
                dve.wait_ge(cl_ready, i + 1)
                dve.tensor_reduce(nmax[:, b:b + 1], cl[:], AX.XY, ALU.max, negate=True).then_inc(cmax_ready, 1)
                dve.wait_ge(dl_ready, i + 1)
                for half in range(2):
                    c.after(dve.tensor_reduce(dmax[:, b, 32 * half:32 * half + 32], by_image(dl[:, b, half, :]), AX.X, ALU.max))
                for half in range(2):
                    op = dve.tensor_tensor(by_image(Dn[:, i, half * 512:(half + 1) * 512]), by_image(dl[:, b, half, :]),
                                           dmax[:, b, 32 * half:32 * half + 32].unsqueeze(2).to_broadcast([P, 32, PATCHES]),
                                           ALU.subtract)
                op.then_inc(dsub_ready, 1)
                dve.wait_ge(cexp_ready, SLOT_E * (i + 1))
                c.after(dve.tensor_reduce(zsum[:, b:b + 1], ze[:, b, :], AX.X, ALU.add))
                c.after(dve.reciprocal(rz[:, b:b + 1], zsum[:, b:b + 1]))
                c.after(dve.tensor_scalar(zn[:, i, :], ze[:, b, :], rz[:, b:b + 1], None, ALU.mult))
                dve.tensor_scalar(ex[:, b, :], ex[:, b, :], rz[:, b:b + 1], None, ALU.mult).then_inc(cw_ready, 1)
                if i >= 1:
                    normalise(i - 1)
            normalise(TILES - 1)


def hidden_pieces(nc, g, b1, g_dram, b_dram):
    WIDE = SLOT_E * HID
    with Scope(nc, "hid") as s:
        gp = s.sb("gp", [P, 2, 3, WIDE], BF16)
        rest = s.sb("rest", [P, 2, HID])
        b1f = s.sb("b1f", [P, 2, WIDE // P])
        bp = s.sb("bp", [P, 3, WIDE // P], BF16)
        gps = [s.ps(f"gps{i}", [P, 2, 512]) for i in range(4)]
        b_in, step, g_ready, one, rest1, two, three, b_done, g_out = (
            s.sem(n) for n in ("b_in", "step", "g_ready", "one", "rest1", "two", "three", "b_done", "g_out"))
        out_done = [s.sem(f"out_done{i}") for i in range(2)]
        block = s.block()
        steps = [(i, e) for i in range(TILES) for e in range(SLOT_E)]

        @block.sync
        def _(sp):
            sp.dma_start(b1f[:, 0, :], b1).then_inc(b_in, 16)
            for i in range(TILES):
                sp.wait_ge(three, SLOT_E * (i + 1))
                for k in range(3):
                    sp.dma_start(g_dram[k, i * P:(i + 1) * P, :], gp[:, i % 2, k, :]).then_inc(out_done[i % 2], 16)
            sp.wait_ge(b_done, 1)
            sp.dma_start(b_dram.rearrange("k (p c) -> p k c", p=P), bp[:]).then_inc(g_out, 16)
            sp.wait_ge(g_out, 16)
            for k in range(2):
                sp.wait_ge(out_done[k], 48 * TILES // 2)

        @block.tensor
        def _(pe):
            pe.wait_ge(g.w1_in, 16)
            for n, (i, e) in enumerate(steps):
                if n >= 4:
                    pe.wait_ge(rest1, n - 3)
                for half in range(2):
                    for k in range(NKD):
                        at = e * HID + half * HALF
                        mm = pe.matmul(gps[n % 4][:, half, 0:HALF], g.xnT[:, k, i * P:(i + 1) * P],
                                       g.w1[:, k, at:at + HALF], start=(k == 0), stop=(k == NKD - 1))
                mm.then_inc(g_ready, 1)

        def piece(buf, k, e):
            return gp[:, buf, k, e * HID:(e + 1) * HID].rearrange("p (a c) -> p a c", a=2)

        def halves(x):
            return x.rearrange("p (a c) -> p a c", a=2)

        @block.scalar
        def _(act):
            def second(n):
                i, e = steps[n]
                act.wait_ge(rest1, n + 1)
                act.activation(piece(i % 2, 1, e), halves(rest[:, n % 2, :]), ACT.Copy).then_inc(two, 1)

            for n, (i, e) in enumerate(steps):
                act.wait_ge(g_ready, n + 1)
                if i >= 2:
                    act.wait_ge(out_done[i % 2], 48 * (i // 2))
                act.activation(piece(i % 2, 0, e), gps[n % 4][:, :, 0:HALF], ACT.Copy).then_inc(one, 1)
                if n >= 1:
                    second(n - 1)
            second(len(steps) - 1)

        @block.vector
        def _(dve):
            c = Chain(dve, step)
            dve.wait_ge(b_in, 16)
            c.after(dve.tensor_copy(bp[:, 0, :], b1f[:, 0, :]))
            c.after(dve.tensor_tensor(b1f[:, 1, :], b1f[:, 0, :], bp[:, 0, :], ALU.subtract))
            c.after(dve.tensor_copy(bp[:, 1, :], b1f[:, 1, :]))
            dve.tensor_tensor(bp[:, 2, :], b1f[:, 1, :], bp[:, 1, :], ALU.subtract).then_inc(b_done, 1)

            def third(n):
                i, e = steps[n]
                dve.wait_ge(two, n + 1)
                dve.tensor_tensor(piece(i % 2, 2, e), halves(rest[:, n % 2, :]), piece(i % 2, 1, e), ALU.subtract).then_inc(three, 1)

            for n, (i, e) in enumerate(steps):
                dve.wait_ge(one, n + 1)
                if n >= 2:
                    dve.wait_ge(three, n - 1)
                dve.tensor_tensor(halves(rest[:, n % 2, :]), gps[n % 4][:, :, 0:HALF], piece(i % 2, 0, e), ALU.subtract).then_inc(rest1, 1)
                if n >= 1:
                    third(n - 1)
            third(len(steps) - 1)


def slot_experts(nc, g, CT, Dn, zn, b2_rows, g_dram, b_dram):
    TP = TILE_IMAGES // 2
    with Scope(nc, "sle") as s:
        G = s.sb("G", [BROWS, 2, SLOT_E * HID], BF16)
        dp = s.sb("dp", [P, 2, SLOT_CHUNKS, BROWS], BF16)
        rest = s.sb("rest", [P, 2, SLOT_CHUNKS, PATCHES])
        dT = s.sb("dT", [BROWS, 2, ALL_SLOTS], BF16)
        cw = s.sb("cw", [P, 2, SLOT_CHUNKS, 32])
        H = s.sb("H", [P, 8, HID])
        U = s.sb("U", [P, HID])
        UT = s.sb("UT", [P, HC, SLOT_E, TILE_IMAGES, PATCHES])
        b2 = s.sb("b2", [P, SLOT_E, D])
        acc = s.sb("acc", [P, D])
        identb = s.sb("identb", [P, P], BF16)
        hp = [s.ps(f"hp{i}", [P, 2, 512]) for i in range(2)]
        up = s.ps("up", [P, 2, 512])
        dps = s.ps("dps", [P, 1024], BF16)
        tps = s.ps("tps", [P, 512])
        b_in, consts, identb_ready, turn, step, pstep, pieces_ready, cw_ready, dps_ready, dT_ready, hid_ready, gelu_done, mix_done, \
            u_ready, ut_ready, ut_done, y_ready, y_done = (s.sem(n) for n in (
                "b_in", "consts", "identb_ready", "turn", "step", "pstep", "pieces_ready", "cw_ready", "dps_ready", "dT_ready", "hid_ready",
                "gelu_done", "mix_done", "u_ready", "ut_ready", "ut_done", "y_ready", "y_done"))
        g_in = [s.sem(f"g_in{i}") for i in range(2)]
        block = s.block()
        ORDER = [0, 2, 4, 6, 1, 3, 5, 7]
        POOL_STEPS = 5

        def program(eng, pair):
            pair(0, None, True, 0)
            with eng.Fori(1, TP) as j:
                pair(j, None, False, j)
            with eng.Fori(1, TILES) as t:
                pair(TP * t, t - 1, False, 0)
                with eng.Fori(1, TP) as j:
                    pair(TP * t + j, None, False, j)

        @block.sync
        def _(sp):
            sp.dma_start(b2[:].rearrange("p e d -> p (e d)"), b2_rows).then_inc(b_in, 16)
            for p in range(2):
                sp.dma_start(G[PROWS:BROWS, p, :], b_dram).then_inc(b_in, 16)

            def pair(r, prev, first, j):
                for p in range(2):
                    n = 2 * r + p
                    if not first:
                        sp.wait_ge(hid_ready, 8 * n - 8)
                    row = 0
                    for k, copies in ((0, 3), (1, 2), (2, 1)):
                        src = g_dram[k, bass.ds(n * PATCHES, PATCHES), :]
                        for c in range(copies):
                            sp.dma_start(G[row:row + PATCHES, p, :], src).then_inc(g_in[p], 16)
                            row += PATCHES

            program(sp, pair)

        @block.gpsimd
        def _(pool):
            pool.memset(dp[:], 1.0).then_inc(consts, 1)
            pool.memset(cw[:], 0.0).then_inc(consts, 1)
            pool.wait_ge(consts, 2)

            def pieces(n, p, first, image):
                c = Chain(pool, pstep, base=POOL_STEPS * n, turn=turn)
                if not first:
                    pool.wait_ge(dps_ready, n - 1)
                    pool.sem_inc(turn, 1)
                q = PATCHES
                src = Dn[:, :, bass.ds(image * PATCHES, PATCHES)]
                d = dp[:, p]
                c.after(pool.tensor_copy(d[:, :, 0:q], src))
                c.after(pool.tensor_tensor(rest[:, p], src, d[:, :, 0:q], ALU.subtract))
                c.after(pool.tensor_copy(d[:, :, q:2 * q], rest[:, p]))
                c.after(pool.tensor_tensor(d[:, :, 2 * q:3 * q], rest[:, p], d[:, :, q:2 * q], ALU.subtract))
                c.after(pool.tensor_copy(d[:, :, 3 * q:5 * q], d[:, :, 0:2 * q]))
                pool.tensor_copy(d[:, :, 5 * q:6 * q], d[:, :, 0:q]).then_inc(pieces_ready, 1)

            def pair(r, prev, first, j):
                for p in range(2):
                    n = 2 * r + p
                    pieces(n, p, first, n)
                    if not first:
                        pool.wait_ge(mix_done, 4 * n - 4)
                        pool.sem_inc(turn, 1)
                    pool.tensor_copy(cw[:, p, :, 0:PATCHES], CT[:, :, bass.ds(n * PATCHES, PATCHES)]).then_inc(cw_ready, 1)

            program(pool, pair)
            pieces(IMAGES, 0, False, IMAGES - 1)

        @block.tensor
        def _(pe):
            pe.wait_ge(b_in, 48)
            pe.wait_ge(identb_ready, 1)
            pe.wait_ge(g.w2_in, 16)

            def transpose_pieces(n, p):
                pe.wait_ge(pieces_ready, n + 1)
                pe.wait_ge(dT_ready, n)
                for c in range(SLOT_CHUNKS):
                    tr = pe.transpose(dps[0:BROWS, c * P:(c + 1) * P], dp[:, p, c, :], identb[:])
                tr.then_inc(dps_ready, 1)

            def mix(n, p, grp, half):
                pe.wait_ge(gelu_done, 8 * n + 4 * grp + 4)
                if half == 0 and grp == 0:
                    pe.wait_ge(cw_ready, n + 1)
                    pe.wait_ge(u_ready, n)
                for e in range(SLOT_E):
                    mm = pe.matmul(up[32 * e:32 * e + 32, half, 0:HALF], cw[:, p, 2 * e + grp, :],
                                   H[:, 4 * grp + e, half * HALF:(half + 1) * HALF], start=(grp == 0), stop=(grp == 1))
                mm.then_inc(mix_done, 1)

            def transpose_u(n, part):
                pe.wait_ge(u_ready, n + 1)
                pe.wait_ge(ut_done, 2 * n + part)
                for c in range(3):
                    at = (3 * part + c) * P
                    tr = pe.transpose(tps[:, c * P:(c + 1) * P], U[:, at:at + P], g.ident[:])
                tr.then_inc(ut_ready, 1)

            def down(t):
                pe.wait_ge(ut_done, 2 * TILE_IMAGES * (t + 1))
                for e in range(SLOT_E):
                    for c in range(HC):
                        mm = pe.matmul(tps[:, 0:D], UT[:, c, e, :, :], g.w2[:, e * HC + c, :],
                                       start=(e == 0 and c == 0), stop=(e == SLOT_E - 1 and c == HC - 1))
                mm.then_inc(y_ready, 1)

            def pair(r, prev, first, j):
                for p in range(2):
                    n = 2 * r + p
                    start = first and p == 0
                    if start:
                        transpose_pieces(0, 0)
                    pe.wait_ge(dT_ready, n + 1)
                    pe.wait_ge(g_in[p], 96 * r + 96)
                    for st in range(4):
                        for x in range(2):
                            q = 2 * st + x
                            c = ORDER[q]
                            if not (start and q < 2):
                                pe.wait_ge(gelu_done, 8 * n + q - 1)
                            for half in range(2):
                                at = (c // 2) * HID + half * HALF
                                mm = pe.matmul(hp[x][:, half, 0:HALF], dT[:, p, c * P:(c + 1) * P],
                                               G[:, p, at:at + HALF], start=True, stop=True)
                            mm.then_inc(hid_ready, 1)
                        if st < 2:
                            if not start:
                                mix(n - 1, 1 - p, 1, st)
                        else:
                            mix(n, p, 0, st - 2)
                        if st == 0 and not first:
                            transpose_u(n - 2, 1)
                        if st == 1:
                            if prev is not None and p == 1:
                                down(prev)
                            transpose_pieces(n + 1, 1 - p)
                        if st == 3 and not start:
                            if prev is not None and p == 1:
                                pe.wait_ge(y_done, prev + 1)
                            transpose_u(n - 1, 0)

            program(pe, pair)
            n = IMAGES - 1
            for half in range(2):
                mix(n, 1, 1, half)
            transpose_u(n - 1, 1)
            transpose_u(n, 0)
            transpose_u(n, 1)
            down(TILES - 1)

        @block.scalar
        def _(act):
            def pair(r, prev, first, j):
                for p in range(2):
                    n = 2 * r + p
                    for q in range(SLOT_CHUNKS):
                        act.wait_ge(hid_ready, 8 * n + q + 1)
                        grp = q // 4
                        if q % 4 == 0 and not (first and p == 0):
                            act.wait_ge(mix_done, 4 * n + 2 * grp - 2)
                        act.activation(H[:, q, :].rearrange("p (a c) -> p a c", a=2), hp[q % 2][:, :, 0:HALF],
                                       ACT.Gelu_apprx_tanh).then_inc(gelu_done, 1)

            program(act, pair)

        @block.vector
        def _(dve):
            dve.tensor_copy(identb[:], g.ident[:]).then_inc(identb_ready, 1)
            FIN = 4

            def leave_pieces(n, p):
                dve.wait_ge(dps_ready, n + 1)
                dve.tensor_copy(dT[:, p, :], dps[0:BROWS, :]).then_inc(dT_ready, 1)

            def leave_u(n):
                dve.wait_ge(mix_done, 4 * n + 4)
                dve.tensor_copy(U[:].rearrange("p (a c) -> p a c", a=2), up[:, :, 0:HALF]).then_inc(u_ready, 1)

            def leave_ut(n, part, slot):
                dve.wait_ge(ut_ready, 2 * n + part + 1)
                dve.tensor_copy(UT[:, 3 * part:3 * part + 3, :, bass.ds(slot, 1), :],
                                tps[:, 0:3 * P].rearrange("p (c e o n) -> p c e o n", c=3, e=SLOT_E, n=32)[:, :, :, :, 0:PATCHES]
                                ).then_inc(ut_done, 1)

            def finish(t):
                c = Chain(dve, step, base=FIN * t)
                dve.wait_ge(y_ready, t + 1)
                ht = g.h[:, bass.ds(t, 1), :].rearrange("p o d -> p (o d)")
                dve.tensor_tensor(acc[:], tps[:, 0:D], ht, ALU.add).then_inc(y_done, 1)
                dve.wait_ge(y_done, t + 1)
                for e in range(SLOT_E):
                    c.after(dve.scalar_tensor_tensor(acc[:] if e < SLOT_E - 1 else ht, b2[:, e, :],
                                                     zn[:, bass.ds(t, 1), e:e + 1].rearrange("p o e -> p (o e)"),
                                                     acc[:], ALU.mult, ALU.add))

            def pair(r, prev, first, j):
                for p in range(2):
                    n = 2 * r + p
                    if first and p == 0:
                        leave_pieces(0, 0)
                    if not first:
                        leave_ut(n - 2, 1, (TILE_IMAGES - 2 + p if prev is not None else 2 * j + p - 2))
                    if not (first and p == 0):
                        leave_u(n - 1)
                    if prev is not None and p == 1:
                        finish(prev)
                    leave_pieces(n + 1, 1 - p)
                    if not (first and p == 0):
                        leave_ut(n - 1, 0, (TILE_IMAGES - 1 if prev is not None and p == 0 else 2 * j + p - 1))

            dve.wait_ge(b_in, 48)
            program(dve, pair)
            leave_ut(IMAGES - 2, 1, TILE_IMAGES - 2)
            leave_u(IMAGES - 1)
            leave_ut(IMAGES - 1, 0, TILE_IMAGES - 1)
            leave_ut(IMAGES - 1, 1, TILE_IMAGES - 1)
            finish(TILES - 1)


def soft_moe(nc, g, a):
    with Scope(nc, "smoe") as s:
        CT = s.sb("CT", [P, SLOT_CHUNKS, TOKENS])
        Dn = s.sb("Dn", [P, SLOT_CHUNKS, TOKENS])
        zn = s.sb("zn", [P, TILES, SLOT_E])
        g_dram = nc.dram_tensor("g_pieces", (3, TOKENS, SLOT_E * HID), BF16).ap()
        b_dram = nc.dram_tensor("b_pieces", (3, SLOT_E * HID), BF16).ap()
        slot_weights(nc, g, CT, Dn, zn)
        hidden_pieces(nc, g, a["b1"], g_dram, b_dram)
        slot_experts(nc, g, CT, Dn, zn, a["b2_rows"], g_dram, b_dram)


class Globals:
    pass


def route(nc, g, a, rt, xn_dram):
    with Scope(nc, "rte") as s:
        wg = s.sb("wg", [KD, NKD, G1 + EXPERTS])
        bg = s.sb("bg", [P, G1 + EXPERTS])
        tri, ones = s.sb("tri", [P, P]), s.sb("ones", [P, P])
        tie = s.sb("tie", [P, E1, E1])
        tri32 = s.sb("tri32", [P, EXPERTS, EXPERTS])
        steps = s.sb("steps", [P, TILES])
        tile_no = s.sb("tile_no", [1, MOE_TILES])
        lane, tile_lane = s.sb("lane", [P, P]), s.sb("tile_lane", [P, MOE_TILES])
        row_id, spare = s.sb("row_id", [P, TILES * TOPK]), s.sb("spare", [P, 1])
        placei, lanei, tilei = (s.sb(n, [P, TILES * TOPK], U32) for n in ("placei", "lanei", "tilei"))
        lanef, tilef = (s.sb(n, [P, TILES * TOPK]) for n in ("lanef", "tilef"))
        in_lane = s.sb("in_lane", [P, TILES * TOPK, P])
        in_tile = s.sb("in_tile", [P, TILES * TOPK, MOE_TILES])
        rows, free = s.sb("rows", [P, MOE_TILES]), s.sb("free", [P, MOE_TILES])
        lg = s.sb("lg", [P, TILES, G1 + EXPERTS])
        val = [s.sb("val0", [P, TILES, G1]), s.sb("val1", [P, TILES * G1, E1])]
        tmp = [s.sb(f"tmp{i}", [P, TILES * G1, E1 * E1]) for i in range(2)]
        rank = [s.sb("rank0", [P, TILES, G1]), s.sb("rank1", [P, TILES * G1, E1])]
        is0 = [s.sb("is00", [P, TILES, G1]), s.sb("is01", [P, TILES * G1, E1])]
        is1 = [s.sb("is10", [P, TILES, G1]), s.sb("is11", [P, TILES * G1, E1])]
        v0, v1, ev, g0, g1 = ([s.sb(f"{n}0", [P, TILES]), s.sb(f"{n}1", [P, TILES * G1])] for n in ("v0", "v1", "ev", "g0", "g1"))
        share = [s.sb("share0", [P, TILES, G1]), s.sb("share1", [P, TILES * G1, E1])]
        mask = s.sb("mask", [P, TOPK, TILES, EXPERTS])
        comb, sel, pos = (s.sb(n, [P, TILES, EXPERTS]) for n in ("comb", "sel", "pos"))
        cum = s.sb("cum", [P, TILES + 1, EXPERTS])
        cnt, need, base, incl = (s.sb(n, [P, EXPERTS]) for n in ("cnt", "need", "base", "incl"))
        placef = s.sb("placef", [P, TILES, TOPK])
        owner = s.sb("owner", [1, MOE_TILES])
        ps_lg, ps_pos, ps_cnt, ps_row = (s.ps(n, [P, 512]) for n in ("ps_lg", "ps_pos", "ps_cnt", "ps_row"))
        c_in, lg_ready, ones_ready, diff_ready, exp_ready, sel_ready, pos_ready, in_ready, step = (
            s.sem(n) for n in ("c_in", "lg_ready", "ones_ready", "diff_ready", "exp_ready", "sel_ready", "pos_ready",
                               "in_ready", "step"))
        xn_out, row_ready, slot_done = (s.sem(n) for n in ("xn_out", "row_ready", "slot_done"))
        loads = [(wg[:], a["wgate"]), (bg[:], a["bgate_rows"]), (tri[:], a["tri"]),
                 (tie[:].rearrange("p a b -> p (a b)"), a["tie8"]), (tri32[:].rearrange("p a b -> p (a b)"), a["tri32"]),
                 (steps[:], a["steps"]), (tile_no[:], a["tile_no"][0:1, :]),
                 (tile_lane[:], a["tile_no"]), (lane[:], a["lane"]), (row_id[:], a["row_id"]), (spare[:], a["spare"])]
        block = s.block()

        @block.sync
        def _(sp):
            for dst, src in loads:
                sp.dma_start(dst, src).then_inc(c_in, 16)
            sp.dma_start(xn_dram.rearrange("(i p) d -> p i d", p=P), g.xn[:]).then_inc(xn_out, 16)
            sp.wait_ge(xn_out, 16)

        @block.tensor
        def _(pe):
            pe.wait_ge(c_in, 16 * len(loads))
            for i in range(TILES):
                for k in range(NKD):
                    mm = pe.matmul(ps_lg[:, i * 36:(i + 1) * 36], g.xnT[:, k, i * P:(i + 1) * P], wg[:, k, :],
                                   start=(k == 0), stop=(k == NKD - 1))
            mm.then_inc(lg_ready, 1)
            pe.wait_ge(ones_ready, 1)
            pe.wait_ge(sel_ready, 1)
            pe.matmul(ps_pos[:, 0:TILES * EXPERTS], tri[:], sel[:].rearrange("p i e -> p (i e)"), start=True, stop=False)
            pe.matmul(ps_pos[:, 0:TILES * EXPERTS], ones[:], cum[:, 0:TILES, :].rearrange("p i e -> p (i e)"), start=False, stop=True)
            pe.matmul(ps_cnt[:, 0:EXPERTS], ones[:], cum[:, TILES, :], start=True, stop=True).then_inc(pos_ready, 1)
            for n in range(TILES * TOPK):
                if n % (TILES * TOPK // 4) == 0:
                    pe.wait_ge(in_ready, n // (TILES * TOPK // 4) + 1)
                mm = pe.matmul(ps_row[:, 0:MOE_TILES], in_lane[:, n, :], in_tile[:, n, :], start=(n == 0), stop=(n == TILES * TOPK - 1))
            mm.then_inc(row_ready, 1)

        @block.scalar
        def _(act):
            for lv in range(2):
                act.wait_ge(diff_ready, lv + 1)
                act.activation(ev[lv][:], v1[lv][:], ACT.Exp).then_inc(exp_ready, 1)

        @block.vector
        def _(dve):
            c = Chain(dve, step)
            dve.memset(ones[:], 1.0).then_inc(ones_ready, 1)
            dve.wait_ge(c_in, 16 * len(loads))
            dve.wait_ge(lg_ready, 1)
            c.after(dve.tensor_tensor(lg[:], ps_lg[:, 0:TILES * 36].rearrange("p (i n) -> p i n", i=TILES),
                                      bg[:].unsqueeze(1).to_broadcast([P, TILES, 36]), ALU.add))
            c.after(dve.tensor_copy(val[0][:], lg[:, :, 0:G1]))
            c.after(dve.tensor_copy(val[1][:].rearrange("p (i g) e -> p i (g e)", g=G1), lg[:, :, G1:]))
            for lv, (G, E) in enumerate(((TILES, G1), (TILES * G1, E1))):
                v = val[lv][:]
                gt, eq = (tmp[n][:].rearrange("p g e -> p (g e)")[:, 0:G * E * E].rearrange("p (g i j) -> p g i j", g=G, i=E) for n in range(2))
                other = v.unsqueeze(2).to_broadcast([P, G, E, E])
                own = v.unsqueeze(3).to_broadcast([P, G, E, E])
                c.after(dve.tensor_tensor(gt, other, own, ALU.is_gt))
                c.after(dve.tensor_tensor(eq, other, own, ALU.is_equal))
                c.after(dve.tensor_tensor(eq, eq, tie[:, 0:E, 0:E].unsqueeze(1).to_broadcast([P, G, E, E]), ALU.mult))
                c.after(dve.tensor_tensor(gt, gt, eq, ALU.add))
                c.after(dve.tensor_reduce(rank[lv][:], gt, AX.X, ALU.add))
                c.after(dve.tensor_scalar(is0[lv][:], rank[lv][:], 0.0, None, ALU.is_equal))
                c.after(dve.tensor_scalar(is1[lv][:], rank[lv][:], 1.0, None, ALU.is_equal))
                c.after(dve.tensor_reduce(v0[lv][:], v, AX.X, ALU.max))
                c.after(dve.tensor_tensor(share[lv][:], v, is1[lv][:], ALU.mult))
                c.after(dve.tensor_reduce(v1[lv][:], share[lv][:], AX.X, ALU.add))
                dve.tensor_tensor(v1[lv][:], v1[lv][:], v0[lv][:], ALU.subtract).then_inc(diff_ready, 1)
                dve.wait_ge(exp_ready, lv + 1)
                c.after(dve.tensor_scalar(g0[lv][:], ev[lv][:], 1.0, None, ALU.add))
                c.after(dve.reciprocal(g0[lv][:], g0[lv][:]))
                c.after(dve.tensor_tensor(g1[lv][:], ev[lv][:], g0[lv][:], ALU.mult))
                wide = lambda x: x.unsqueeze(2).to_broadcast([P, G, E])
                c.after(dve.tensor_tensor(share[lv][:], is0[lv][:], wide(g0[lv][:]), ALU.mult))
                part = tmp[0][:].rearrange("p g e -> p (g e)")[:, 0:G * E].rearrange("p (g e) -> p g e", g=G)
                c.after(dve.tensor_tensor(part, is1[lv][:], wide(g1[lv][:]), ALU.mult))
                c.after(dve.tensor_tensor(share[lv][:], share[lv][:], part, ALU.add))
            pairs = lambda x: x.rearrange("p i (g e) -> p (i g) e", g=G1)
            outer = lambda x: x.rearrange("p i g -> p (i g)").unsqueeze(2).to_broadcast([P, TILES * G1, E1])
            c.after(dve.tensor_tensor(pairs(comb[:]), share[1][:], outer(share[0][:]), ALU.mult))
            for k in range(TOPK):
                gm, em = (is0, is1)[k // 2][0], (is0, is1)[k % 2][1]
                c.after(dve.tensor_tensor(pairs(mask[:, k]), em[:], outer(gm[:]), ALU.mult))
            c.after(dve.tensor_tensor(sel[:], mask[:, 0], mask[:, 1], ALU.add))
            c.after(dve.tensor_tensor(sel[:], sel[:], mask[:, 2], ALU.add))
            c.after(dve.tensor_tensor(sel[:], sel[:], mask[:, 3], ALU.add))
            c.after(dve.memset(cum[:, 0, :], 0.0))
            for i in range(TILES):
                op = dve.tensor_tensor(cum[:, i + 1, :], cum[:, i, :], sel[:, i, :], ALU.add)
                if i < TILES - 1:
                    c.after(op)
            op.then_inc(sel_ready, 1)

            def pick(dst, x):
                for k in range(TOPK):
                    flat = tmp[k % 2][:].rearrange("p g e -> p (g e)")[:, 0:TILES * EXPERTS].rearrange("p (i e) -> p i e", i=TILES)
                    c.after(dve.tensor_tensor(flat, x, mask[:, k], ALU.mult))
                    c.after(dve.tensor_reduce(dst[:, :, k], flat, AX.X, ALU.add))

            pick(rt.gate, comb[:])
            dve.wait_ge(pos_ready, 1)
            c.after(dve.tensor_copy(cnt[:], ps_cnt[:, 0:EXPERTS]))
            flat = tmp[0][:].rearrange("p g e -> p (g e)")
            over = flat[:, 0:EXPERTS * TILES].rearrange("p (e n) -> p e n", n=TILES)
            c.after(dve.tensor_tensor(over, cnt[:].unsqueeze(2).to_broadcast([P, EXPERTS, TILES]),
                                      steps[:].unsqueeze(1).to_broadcast([P, EXPERTS, TILES]), ALU.is_gt))
            c.after(dve.tensor_reduce(need[:], over, AX.X, ALU.add))
            before = flat[:, 0:EXPERTS * EXPERTS].rearrange("p (a b) -> p a b", a=EXPERTS)
            c.after(dve.tensor_tensor(before, need[:].unsqueeze(1).to_broadcast([P, EXPERTS, EXPERTS]), tri32[:], ALU.mult))
            c.after(dve.tensor_reduce(base[:], before, AX.X, ALU.add))
            c.after(dve.tensor_tensor(incl[:], base[:], need[:], ALU.add))
            c.after(dve.tensor_scalar(base[:], base[:], float(P), None, ALU.mult))
            c.after(dve.tensor_tensor(pos[:], ps_pos[:, 0:TILES * EXPERTS].rearrange("p (i e) -> p i e", i=TILES),
                                      base[:].unsqueeze(1).to_broadcast([P, TILES, EXPERTS]), ALU.add))
            pick(placef, pos[:])
            c.after(dve.tensor_copy(placei[:], placef[:].rearrange("p i k -> p (i k)")))
            c.after(dve.tensor_scalar(lanei[:], placei[:], P - 1, None, ALU.bitwise_and))
            c.after(dve.tensor_scalar(tilei[:], placei[:], LANE_BITS, None, ALU.logical_shift_right))
            c.after(dve.tensor_copy(lanef[:], lanei[:]))
            c.after(dve.tensor_copy(tilef[:], tilei[:]))
            quarter = TILES * TOPK // 4
            for n in range(0, TILES * TOPK, quarter):
                at = slice(n, n + quarter)
                wide = lambda x, m: x[:, at].unsqueeze(2).to_broadcast([P, quarter, m])
                every = lambda x, m: x.unsqueeze(1).to_broadcast([P, quarter, m])
                c.after(dve.tensor_tensor(in_tile[:, at], every(tile_lane[:], MOE_TILES), wide(tilef, MOE_TILES), ALU.is_equal))
                c.after(dve.tensor_tensor(in_tile[:, at], in_tile[:, at], wide(row_id, MOE_TILES), ALU.mult))
                dve.tensor_tensor(in_lane[:, at], every(lane[:], P), wide(lanef, P), ALU.is_equal).then_inc(in_ready, 1)
            ended = flat[0:1, 0:MOE_TILES * EXPERTS].rearrange("p (t e) -> p t e", e=EXPERTS)
            c.after(dve.tensor_tensor(ended, incl[0:1].unsqueeze(1).to_broadcast([1, MOE_TILES, EXPERTS]),
                                      tile_no[:].unsqueeze(2).to_broadcast([1, MOE_TILES, EXPERTS]), ALU.is_le))
            c.after(dve.tensor_reduce(owner[:], ended, AX.X, ALU.add))
            c.after(dve.tensor_scalar(rt.expert[:], owner[:], float(EXPERTS - 1), None, ALU.min))
            dve.wait_ge(row_ready, 1)
            c.after(dve.tensor_scalar(free[:], ps_row[:, 0:MOE_TILES], 0.0, spare[:], ALU.is_equal, ALU.mult))
            c.after(dve.tensor_tensor(rows[:], free[:], ps_row[:, 0:MOE_TILES], ALU.add))
            c.after(dve.tensor_scalar(rt.slot[:, 1, :], rows[:], -1.0, None, ALU.add))
            dve.tensor_scalar(rt.slot[:, 0, :], rt.slot[:, 1, :], TOKENS - 1, None, ALU.bitwise_and).then_inc(slot_done, 1)
            dve.wait_ge(slot_done, 1)


def expert_tiles(nc, g, a, rt, xn_dram, y_dram):
    DEEP = 3
    ROUNDS = MOE_TILES // DEEP
    with Scope(nc, "ext") as s:
        w1 = s.sb("w1", [KD + 1, DEEP, NKD, HID])
        w2 = s.sb("w2", [P, DEEP, HC, D])
        b2 = s.sb("b2", [1, DEEP, D])
        x = s.sb("x", [P, DEEP, D])
        xT = s.sb("xT", [KD + 1, DEEP, NKD, P])
        H = s.sb("H", [P, DEEP, HC, P])
        y = s.sb("y", [P, DEEP, D])
        xi, yi = ([s.sb(f"{n}{i}", [P, 1], U32) for i in range(DEEP)] for n in ("xi", "yi"))
        ones = s.sb("ones", [1, P])
        hp = [s.ps(f"hp{i}", [P, 2, 512]) for i in range(DEEP)]
        xp, yp = s.ps("xp", [P, 512]), s.ps("yp", [P, 512])
        xi_ready, yi_ready, xp_ready, xT_done, hid_ready, gelu_done, y_ready, y_done, consts, turn = (
            s.sem(n) for n in ("xi_ready", "yi_ready", "xp_ready", "xT_done", "hid_ready", "gelu_done", "y_ready",
                               "y_done", "consts", "turn"))
        w1_in, w2_in, x_in, y_out = ([s.sem(f"{n}{i}") for i in range(DEEP)] for n in ("w1_in", "w2_in", "x_in", "y_out"))
        block = s.block()

        def program(eng, tile):
            for p in range(DEEP):
                tile(p, p, 0, True, False)
            with eng.Fori(1, ROUNDS - 1) as r:
                for p in range(DEEP):
                    tile(DEEP * r + p, p, r, False, False)
            for p in range(DEEP):
                tile(DEEP * (ROUNDS - 1) + p, p, ROUNDS - 1, False, True)

        @block.sync
        def _(sp):
            def load(t, p, r, first, last):
                e = sp.value_load(rt.expert[0:1, bass.ds(t, 1)], min_val=0, max_val=EXPERTS - 1)
                if not first:
                    sp.wait_ge(hid_ready, t - DEEP + 1)
                sp.dma_start(w1[0:KD, p], a["W1"][bass.ds(e, 1)].rearrange("o k c n -> (o k) c n")).then_inc(w1_in[p], 16)
                sp.dma_start(w1[KD:KD + 1, p, 1, :], a["B1"][bass.ds(e, 1), :]).then_inc(w1_in[p], 16)
                if not first:
                    sp.wait_ge(y_ready, t - DEEP + 1)
                sp.dma_start(w2[:, p], a["W2"][bass.ds(e, 1)].rearrange("o p c n -> (o p) c n")).then_inc(w2_in[p], 16)
                sp.dma_start(b2[:, p, :], a["B2"][bass.ds(e, 1), :]).then_inc(w2_in[p], 16)

            program(sp, load)

        @block.tensor
        def _(pe):
            pe.wait_ge(consts, 2)

            def transpose_x(t, p, r):
                pe.wait_ge(x_in[p], 16 * r + 16)
                if not isinstance(t, int) or t > 0:
                    pe.wait_ge(xT_done, t)
                for k in range(NKD):
                    tr = pe.transpose(xp[0:KD, k * P:(k + 1) * P], x[:, p, k * KD:(k + 1) * KD], g.ident[:])
                tr.then_inc(xp_ready, 1)

            def up(t, p, r, first):
                pe.wait_ge(w1_in[p], 32 * r + 32)
                pe.wait_ge(xT_done, t + 1)
                if not first:
                    pe.wait_ge(gelu_done, t - DEEP + 1)
                for c in range(HC):
                    for k in range(NKD):
                        rows = KD + k
                        mm = pe.matmul(hp[p][:, c // 3, (c % 3) * P:(c % 3 + 1) * P], w1[0:rows, p, k, c * P:(c + 1) * P],
                                       xT[0:rows, p, k, :], start=(k == 0), stop=(k == NKD - 1))
                mm.then_inc(hid_ready, 1)

            def down(t, p, r):
                pe.wait_ge(w2_in[p], 32 * r + 32)
                pe.wait_ge(gelu_done, t + 1)
                if not isinstance(t, int) or t > 0:
                    pe.wait_ge(y_done, t)
                for c in range(HC):
                    pe.matmul(yp[:, 0:D], H[:, p, c, :], w2[:, p, c, :], start=(c == 0), stop=False)
                pe.matmul(yp[:, 0:D], ones[:], b2[:, p, :], start=False, stop=True).then_inc(y_ready, 1)

            def tile(t, p, r, first, last):
                if first and p == 0:
                    transpose_x(0, 0, 0)
                if not (last and p == DEEP - 1):
                    transpose_x(t + 1, (p + 1) % DEEP, r + (p + 1) // DEEP)
                up(t, p, r, first)
                if not (first and p == 0):
                    down(t - 1, (p - 1) % DEEP, r + (p - 1) // DEEP)

            program(pe, tile)
            down(MOE_TILES - 1, DEEP - 1, ROUNDS - 1)

        @block.scalar
        def _(act):
            def gelu(t, p, r, first, last):
                act.wait_ge(hid_ready, t + 1)
                if not first:
                    act.wait_ge(y_ready, t - DEEP + 1)
                act.activation(H[:, p].rearrange("p (a c) n -> p a (c n)", a=2), hp[p][:, :, 0:3 * P], ACT.Gelu).then_inc(gelu_done, 1)

            program(act, gelu)

        @block.vector
        def _(dve):
            dve.memset(ones[:], 1.0).then_inc(consts, 1)
            dve.memset(xT[KD:KD + 1], 1.0).then_inc(consts, 1)

            def index(n, t, p):
                dve.tensor_copy((xi, yi)[n][p][:], rt.slot[:, n, bass.ds(t, 1)]).then_inc((xi_ready, yi_ready)[n], 1)

            def leave_x(t, p, first):
                dve.wait_ge(xp_ready, t + 1)
                if not first:
                    dve.wait_ge(hid_ready, t - DEEP + 1)
                dve.tensor_copy(xT[0:KD, p], xp[0:KD, 0:2 * P].rearrange("p (k c) -> p k c", k=NKD)).then_inc(xT_done, 1)

            def leave_y(t, p, r, first):
                dve.wait_ge(y_ready, t + 1)
                if not first:
                    dve.wait_ge(y_out[p], 16 * r)
                index(1, t, p)
                dve.tensor_copy(y[:, p, :], yp[:, 0:D]).then_inc(y_done, 1)

            def tile(t, p, r, first, last):
                if first and p == 0:
                    for q in range(DEEP):
                        index(0, q, q)
                    leave_x(0, 0, True)
                if not (last and p == DEEP - 1):
                    leave_x(t + 1, (p + 1) % DEEP, first and p + 1 < DEEP)
                if not last:
                    dve.wait_ge(x_in[p], 16 * r + 16)
                    index(0, t + DEEP, p)
                if not (first and p == 0):
                    leave_y(t - 1, (p - 1) % DEEP, r + (p - 1) // DEEP, first)

            program(dve, tile)
            leave_y(MOE_TILES - 1, DEEP - 1, ROUNDS - 1, False)

        @block.gpsimd
        def _(pool):
            def gather(t, p):
                pool.wait_ge(xi_ready, t + 1)
                pool.sem_inc(turn, 1)
                pool.indirect_dma_start(out=x[:, p, :], out_offset=None, in_=xn_dram,
                                        in_offset=bass.IndirectOffsetOnAxis(ap=xi[p][:], axis=0)).then_inc(x_in[p], 16)

            def scatter(t, p, r, first):
                pool.wait_ge(yi_ready, t + 1)
                pool.wait_ge(y_done, t + 1)
                if not first:
                    pool.wait_ge(y_out[(p - 1) % DEEP], 16 * (r + (p - 1) // DEEP) + 16)
                pool.sem_inc(turn, 1)
                pool.indirect_dma_start(out=y_dram, out_offset=bass.IndirectOffsetOnAxis(ap=yi[p][:], axis=0),
                                        in_=y[:, p, :], in_offset=None).then_inc(y_out[p], 16)

            def tile(t, p, r, first, last):
                if not last:
                    pool.wait_ge(xp_ready, t + 1)
                    gather(t + DEEP, p)
                if not (first and p == 0):
                    scatter(t - 1, (p - 1) % DEEP, r + (p - 1) // DEEP, first and p == 1)

            for q in range(DEEP):
                gather(q, q)
            program(pool, tile)
            scatter(MOE_TILES - 1, DEEP - 1, ROUNDS - 1, False)
            for p in range(DEEP):
                pool.wait_ge(y_out[p], 16 * ROUNDS)
            pool.wait_ge(turn, 2 * MOE_TILES)


def combine(nc, g, rt, y_dram, out):
    with Scope(nc, "cmb") as s:
        rows = s.sb("rows", [P, TILES, TOPK, D])
        row_in = [s.sem(f"row_in{i}") for i in range(TILES)]
        h_step = [s.sem(f"h_step{i}") for i in range(TILES)]
        by_choice = y_dram[0:TOPK * TOKENS].rearrange("(k i p) d -> i p k d", k=TOPK, i=TILES)
        block = s.block()

        def load(eng, i):
            eng.dma_start(rows[:, i], by_choice[i]).then_inc(row_in[i], 16)

        @block.scalar
        def _(act):
            for i in range(1, TILES, 2):
                load(act, i)

        @block.vector
        def _(dve):
            for i in range(0, TILES, 2):
                dve.wait_ge(row_in[i], 16)
                dve.wait_ge(row_in[i + 1], 16)
                for k in range(TOPK):
                    for j in (i, i + 1):
                        if k > 0:
                            dve.wait_ge(h_step[j], k)
                        dve.scalar_tensor_tensor(g.h[:, j, :], rows[:, j, k, :], rt.gate[:, j, k:k + 1], g.h[:, j, :],
                                                 ALU.mult, ALU.add).then_inc(h_step[j], 1)

        @block.sync
        def _(sp):
            for i in range(0, TILES, 2):
                load(sp, i)
            for i in range(TILES):
                sp.wait_ge(h_step[i], TOPK)
                sp.dma_start(out[i * P:(i + 1) * P, :], g.h[:, i, :]).then_inc(g.out_done, 16)
            sp.wait_ge(g.out_done, 16 * TILES)


def routed_moe(nc, g, a, out):
    with Scope(nc, "rmoe") as s:
        rt = Globals()
        rt.gate = s.sb("gate", [P, TILES, TOPK])
        rt.slot = s.sb("slot", [P, 2, MOE_TILES], U32)
        rt.expert = s.sb("expert", [1, MOE_TILES], I32)
        xn_dram = nc.dram_tensor("xn", (TOKENS, D), F32).ap()
        y_dram = nc.dram_tensor("y_by_choice", (TOPK * TOKENS + P, D), F32).ap()
        route(nc, g, a, rt, xn_dram)
        expert_tiles(nc, g, a, rt, xn_dram, y_dram)
        combine(nc, g, rt, y_dram, out)


def build(nc, a, out, upto=99, dump=None):
    Scope.ended = []
    with Scope(nc, "vit") as s:
        g = Globals()
        g.h = s.sb("h", [P, TILES, D])
        g.xn = s.sb("xn", [P, TILES, D])
        g.xnT = s.sb("xnT", [KD, NKD, TOKENS])
        g.ident = s.sb("ident", [P, P])
        g.phi = s.sb("phi", [KD, NKD, ALL_SLOTS])
        g.w1 = s.sb("w1", [KD, NKD, SLOT_E * HID])
        g.w2 = s.sb("w2", [P, SLOT_E * HC, D])
        g.d_phi, g.d_w1, g.d_w2, g.d_ident = a["phi"], a["w1"], a["w2"], a["ident"]
        g.phi_in, g.w1_in, g.w2_in, g.ident_in, g.out_done = (nc.alloc_semaphore(n) for n in ("phi_in", "w1_in", "w2_in", "ident_in", "out_done"))
        embed(nc, g, a["xT"], a["tokW"], a["pos_rows"], a["tok_b_rows"])
        if upto >= 1:
            layernorm(nc, g, "ln0")
            attention0(nc, g, a)
        if upto >= 2 and upto != 30:
            layernorm(nc, g, "ln1")
            soft_moe(nc, g, a)
        if upto >= 3:
            Scope.retire(nc)
            layernorm(nc, g, "ln2")
            attention1(nc, g, a)
        if upto >= 4:
            layernorm(nc, g, "ln3")
            routed_moe(nc, g, a, out)
            return
        block = s.block()

        @block.sync
        def _(sp):
            sp.dma_start(out.rearrange("(i p) d -> p i d", p=P), g.h[:]).then_inc(g.out_done, 16)
            sp.wait_ge(g.out_done, 16)
            for sem in (g.phi_in, g.w1_in, g.w2_in, g.ident_in):
                sp.wait_ge(sem, 16)


def layouts(x, L0_tok_W, L0_tok_b, L0_tok_pos_emb, L0_attn_W_qkv, L0_attn_b_qkv, L0_ffn_phi, L0_ffn_w1, L0_ffn_b1,
            L0_ffn_w2, L0_ffn_b2, L1_attn_qA, L1_attn_qB, L1_attn_kA, L1_attn_kB, L1_attn_vA, L1_attn_vB, L1_attn_o_w,
            L1_ffn_Wg, L1_ffn_bg, L1_ffn_Wge, L1_ffn_bge, L1_ffn_W1, L1_ffn_b1, L1_ffn_W2, L1_ffn_b2):
    c = np.ascontiguousarray
    kd = lambda w: c(np.asarray(w).reshape(NKD, KD, -1).transpose(1, 0, 2))
    rows = lambda v: c(np.broadcast_to(np.asarray(v).reshape(1, -1), (P, np.asarray(v).size)))
    x = np.asarray(x)
    patches = x.reshape(IMAGES, 4, 16, 4, 16, 3).transpose(0, 1, 3, 2, 4, 5).reshape(TOKENS, 768)
    a = {}
    a["xT"] = c(patches.T.reshape(PATCH_CHUNKS, P, TOKENS).transpose(1, 0, 2))
    a["tokW"] = c(np.asarray(L0_tok_W).reshape(PATCH_CHUNKS, P, D).transpose(1, 0, 2))
    a["pos_rows"] = c(np.tile(np.asarray(L0_tok_pos_emb), (TILE_IMAGES, 1)))
    a["tok_b_rows"] = rows(L0_tok_b)
    a["ident"] = np.eye(P, dtype=np.float32)
    a["wqkv"] = kd(L0_attn_W_qkv)
    bq = np.asarray(L0_attn_b_qkv)
    a["bqk"] = c(bq[0:2 * D].reshape(4, KD).T)
    a["bv_rows"] = rows(bq[2 * D:])
    p = np.arange(KD)
    a["head_mask0"] = (p[:, None] // 16 == np.arange(6)[None, :]).astype(np.float32)
    a["head_mask1"] = (p[:, None] // 32 == np.arange(3)[None, :]).astype(np.float32)
    q = np.arange(P)
    a["mask_q"] = c(np.tile(np.concatenate([
        (q[None, :] // PATCHES == np.arange(8)[:, None]), (q[None, :] % PATCHES == np.arange(16)[:, None])
    ]).astype(np.float32), (1, TILES)))
    mk = np.concatenate([(q[None, :] // PATCHES != np.arange(8)[:, None]),
                         (q[None, :] % PATCHES > np.arange(16)[:, None])]).astype(np.float32) * np.float32(-BIG)
    a["mask_k"] = c(np.broadcast_to(mk[:, None, :], (24, 6, P)))
    a["phi"] = kd(np.asarray(L0_ffn_phi).reshape(ALL_SLOTS, D).T)
    a["w1"] = kd(np.asarray(L0_ffn_w1).transpose(1, 0, 2).reshape(D, SLOT_E * HID))
    a["b1"] = c(np.asarray(L0_ffn_b1).reshape(P, SLOT_E * HID // P))
    a["w2"] = c(np.asarray(L0_ffn_w2).reshape(SLOT_E * HC, P, D).transpose(1, 0, 2))
    a["b2_rows"] = rows(L0_ffn_b2)
    for n, A, B in (("q", L1_attn_qA, L1_attn_qB), ("k", L1_attn_kA, L1_attn_kB), ("v", L1_attn_vA, L1_attn_vB)):
        a[n + "A"] = kd(A)
        a[n + "B"] = c(np.asarray(B))
    a["o_w"] = kd(L1_attn_o_w)
    hd = 32
    inv = np.float32(1.0) / np.float32(10000.0) ** (np.arange(0, hd, 2, dtype=np.float32) / np.float32(hd))
    fr = np.outer(np.arange(PATCHES, dtype=np.float32), inv).astype(np.float32)
    emb = np.concatenate([fr, fr], -1)
    table = lambda f: c(np.tile(f(emb).astype(np.float32).T, (3, 512 // PATCHES)))
    a["cosT"], a["sinT"] = table(np.cos), table(np.sin)
    a["wgate"] = kd(np.concatenate([np.asarray(L1_ffn_Wg), np.asarray(L1_ffn_Wge).transpose(1, 0, 2).reshape(D, EXPERTS)], 1))
    a["bgate_rows"] = rows(np.concatenate([np.asarray(L1_ffn_bg), np.asarray(L1_ffn_bge).reshape(-1)]))
    a["W1"] = c(np.asarray(L1_ffn_W1).reshape(EXPERTS, NKD, KD, HID).transpose(0, 2, 1, 3))
    a["B1"] = c(np.asarray(L1_ffn_b1))
    a["W2"] = c(np.asarray(L1_ffn_W2).reshape(EXPERTS, HC, P, D).transpose(0, 2, 1, 3))
    a["B2"] = c(np.asarray(L1_ffn_b2))
    a["tri"] = (np.arange(P)[:, None] < np.arange(P)[None, :]).astype(np.float32)
    e = np.arange(E1)
    a["tie8"] = c(np.broadcast_to((e[None, :] < e[:, None]).astype(np.float32).reshape(1, -1), (P, 64)))
    e = np.arange(EXPERTS)
    a["tri32"] = c(np.broadcast_to((e[None, :] < e[:, None]).astype(np.float32).reshape(1, -1), (P, 1024)))
    a["steps"] = rows((np.arange(8) * P).astype(np.float32))
    a["tile_no"] = rows(np.arange(MOE_TILES).astype(np.float32))
    a["lane"] = rows(np.arange(P).astype(np.float32))
    t = np.arange(P)[:, None, None] + P * np.arange(TILES)[None, :, None] + TOKENS * np.arange(TOPK)[None, None, :]
    a["row_id"] = c((t + 1).astype(np.float32).reshape(P, TILES * TOPK))
    a["spare"] = (TOPK * TOKENS + 1 + np.arange(P, dtype=np.float32))[:, None]
    return a


def kernel(**inputs):
    import concourse.bacc as bacc
    from concourse.bass_utils import run_bass_kernel_spmd

    nc = bacc.Bacc("TRN2", target_bir_lowering=False, num_devices=1)
    arrays = layouts(**inputs)
    args = {n: nc.dram_tensor(n, v.shape, mybir.dt.from_np(v.dtype), kind="ExternalInput").ap() for n, v in arrays.items()}
    out = nc.dram_tensor("out", (TOKENS, D), F32, kind="ExternalOutput").ap()
    build(nc, args, out)
    r = run_bass_kernel_spmd(nc, [arrays], core_ids=[0])
    return r.results[0]["out"].reshape(IMAGES, PATCHES, D)
```

```python
import numpy as np

import concourse.bass as bass
from concourse import mybir
from contextlib import ExitStack

F32 = mybir.dt.float32
BF16 = mybir.dt.bfloat16
U32 = mybir.dt.uint32
I32 = mybir.dt.int32
ACT = mybir.ActivationFunctionType
ALU = mybir.AluOpType
AX = mybir.AxisListType

P = 128
IMAGES, PATCHES, D = 64, 16, 192
TOKENS = IMAGES * PATCHES
TILES = TOKENS // P
TILE_IMAGES = P // PATCHES
KD, NKD = 96, 2
PATCH_CHUNKS = 768 // P
EPS = 1e-5
BIG = float(2.0 ** 100)
SLOT_E, SLOTS, HID = 4, 256, 768
ALL_SLOTS = SLOT_E * SLOTS
SLOT_CHUNKS = ALL_SLOTS // P
HC = HID // P
HALF = HID // 2
PAIRS = ((0, 0), (0, 1), (0, 2), (1, 0), (1, 1), (2, 0))
PROWS = len(PAIRS) * PATCHES
BROWS = PROWS + 3
G1, E1 = 4, 8
EXPERTS = G1 * E1
TOPK = 4
MOE_TILES = (TOPK * TOKENS + EXPERTS * (P - 1)) // P
LANE_BITS = 7


class Chain:

    def __init__(self, eng, sem, base=0, turn=None):
        self.eng, self.sem, self.base, self.n, self.turn = eng, sem, base, 0, turn

    def after(self, ins):
        self.n += 1
        ins.then_inc(self.sem, 1)
        self.eng.wait_ge(self.sem, self.base + self.n)
        if self.turn is not None:
            self.eng.sem_inc(self.turn, 1)


class Scope(ExitStack):

    ended = []

    def __init__(self, nc, stage):
        super().__init__()
        self.nc, self.stage = nc, stage

    def sb(self, name, shape, dt=F32):
        return self.enter_context(self.nc.sbuf_tensor(f"{self.stage}_{name}", shape, dt))

    def ps(self, name, shape, dt=F32):
        return self.enter_context(self.nc.psum_tensor(f"{self.stage}_{name}", shape, dt))

    def sem(self, name):
        sem = self.nc.alloc_semaphore(f"{self.stage}_{name}")
        Scope.ended.append(sem)
        return sem

    @staticmethod
    def retire(nc):
        nc.clear_and_free_semaphores(Scope.ended)
        nc.all_engine_barrier()
        Scope.ended = []

    def block(self):
        return self.enter_context(self.nc.Block())


def embed(nc, g, xT, tokW, pos_rows, tok_b_rows):
    with Scope(nc, "emb") as s:
        x_sb = s.sb("x", [P, PATCH_CHUNKS, TOKENS])
        w_sb = s.sb("w", [P, PATCH_CHUNKS, D])
        pos = s.sb("pos", [P, D])
        tokb = s.sb("tokb", [P, D])
        acc = [s.ps(f"acc{i}", [P, 512]) for i in range(TILES)]
        w_in = [s.sem(f"w_in{j}") for j in range(PATCH_CHUNKS)]
        rows_in, bias_ready, acc_ready, h_done = (s.sem(n) for n in ("rows_in", "bias_ready", "acc_ready", "h_done"))
        block = s.block()

        @block.sync
        def _(sp):
            for j in range(PATCH_CHUNKS):
                sp.dma_start(w_sb[:, j, :], tokW[:, j, :]).then_inc(w_in[j], 16)
                sp.dma_start(x_sb[:, j, :], xT[:, j, :]).then_inc(w_in[j], 16)
            sp.dma_start(g.phi[:], g.d_phi).then_inc(g.phi_in, 16)
            sp.dma_start(g.w1[:], g.d_w1).then_inc(g.w1_in, 16)

        @block.scalar
        def _(act):
            act.dma_start(pos[:], pos_rows).then_inc(rows_in, 16)
            act.dma_start(tokb[:], tok_b_rows).then_inc(rows_in, 16)
            act.dma_start(g.ident[:], g.d_ident).then_inc(g.ident_in, 16)
            act.dma_start(g.w2[:], g.d_w2).then_inc(g.w2_in, 16)

        @block.tensor
        def _(pe):
            for j in range(PATCH_CHUNKS):
                pe.wait_ge(w_in[j], 32)
                for i in range(TILES):
                    mm = pe.matmul(acc[i][:, 0:D], x_sb[:, j, i * P:(i + 1) * P], w_sb[:, j, :],
                                   start=(j == 0), stop=(j == PATCH_CHUNKS - 1))
                    if j == PATCH_CHUNKS - 1:
                        mm.then_inc(acc_ready, 1)

        @block.vector
        def _(dve):
            dve.wait_ge(rows_in, 32)
            dve.tensor_tensor(pos[:], pos[:], tokb[:], ALU.add).then_inc(bias_ready, 1)
            dve.wait_ge(bias_ready, 1)
            for i in range(TILES):
                dve.wait_ge(acc_ready, i + 1)
                dve.tensor_tensor(g.h[:, i, :], acc[i][:, 0:D], pos[:], ALU.add).then_inc(h_done, 1)
            dve.wait_ge(h_done, TILES)


def layernorm(nc, g, stage, banks=None, loads=(), loaded=None):
    with Scope(nc, stage) as s:
        stats = s.sb("stats", [P, TILES, 6])
        mv = s.sb("mv", [P, TILES, 2])
        ve, sd, r, t, nmr = (s.sb(n, [P, TILES]) for n in ("ve", "sd", "r", "t", "nmr"))
        psT = banks or [s.ps(f"psT{i}", [P, 512]) for i in range(TILES // 2)]
        step, var_ready, sd_ready, xn_ready, t_ready, xnT_done = (
            s.sem(n) for n in ("step", "var_ready", "sd_ready", "xn_ready", "t_ready", "xnT_done"))
        block = s.block()

        @block.sync
        def _(sp):
            for dst, src in loads:
                sp.dma_start(dst, src).then_inc(loaded, 16)

        @block.vector
        def _(dve):
            c = Chain(dve, step)
            for i in range(TILES):
                c.after(dve.bn_stats(stats[:, i, :], g.h[:, i, :]))
            for i in range(TILES):
                c.after(dve.bn_aggr(mv[:, i, :], stats[:, i, :]))
            dve.tensor_scalar(ve[:], mv[:, :, 1], EPS, None, ALU.add).then_inc(var_ready, 1)
            dve.wait_ge(sd_ready, 1)
            c.after(dve.reciprocal(r[:], sd[:]))
            c.after(dve.tensor_tensor(t[:], r[:], r[:], ALU.mult))
            c.after(dve.tensor_tensor(t[:], t[:], ve[:], ALU.mult))
            c.after(dve.tensor_scalar(t[:], t[:], -0.5, 1.5, ALU.mult, ALU.add))
            c.after(dve.tensor_tensor(r[:], r[:], t[:], ALU.mult))
            c.after(dve.scalar_tensor_tensor(nmr[:], mv[:, :, 0], -1.0, r[:], ALU.mult, ALU.mult))
            for i in range(TILES):
                dve.tensor_scalar(g.xn[:, i, :], g.h[:, i, :], r[:, i:i + 1], nmr[:, i:i + 1],
                                  ALU.mult, ALU.add).then_inc(xn_ready, 1)

        @block.tensor
        def _(pe):
            pe.wait_ge(g.ident_in, 16)
            for i in range(TILES):
                pe.wait_ge(xn_ready, i + 1)
                for k in range(NKD):
                    at = (i % 2 * NKD + k) * P
                    tr = pe.transpose(psT[i // 2][0:KD, at:at + P], g.xn[:, i, k * KD:(k + 1) * KD], g.ident[:])
                tr.then_inc(t_ready, 1)

        @block.scalar
        def _(act):
            act.wait_ge(var_ready, 1)
            act.activation(sd[:], ve[:], ACT.Sqrt).then_inc(sd_ready, 1)
            for j in range(TILES // 2):
                act.wait_ge(t_ready, 2 * j + 2)
                for k in range(NKD):
                    src = psT[j][0:KD, :].rearrange("p (i k c) -> p i k c", i=2, k=NKD)[:, :, k, :]
                    dst = g.xnT[:, k, 2 * j * P:(2 * j + 2) * P].rearrange("p (i c) -> p i c", i=2)
                    act.activation(dst, src, ACT.Copy).then_inc(xnT_done, 1)


HEADS_U = 6
KEYS_DEEP = 3


class Attend:

    def __init__(self, s, g, units, scale, rows, heads_per_group):
        self.s, self.g, self.units, self.scale = s, g, units, scale
        self.qT = s.sb("qT", [rows, 2, TOKENS])
        self.kT = s.sb("kT", [KD, 2, TOKENS])
        self.kTm = s.sb("kTm", [rows, KEYS_DEEP, HEADS_U, P])
        self.hm = s.sb("hm", [KD, heads_per_group])
        self.v = s.sb("v", [P, TILES, D])
        self.nmax, self.rsum, self.rinv = (s.sb(n, [P, 2, HEADS_U]) for n in ("nmax", "rsum", "rinv"))
        self.prob = s.sb("prob", [P, 2, HEADS_U, P])
        self.probT = s.sb("probT", [P, 2, HEADS_U, P])
        self.sc = [s.ps(f"sc{i}", [P, 2, 512]) for i in range(2)]
        self.pt = [s.ps(f"pt{i}", [P, 512]) for i in range(2)]
        self.av = [s.ps(f"av{i}", [P, 512]) for i in range(2)]
        (self.km_pool, self.km_dve, self.sc_ready, self.max_raw, self.max_ready, self.exp_done, self.rinv_ready,
         self.pt_ready, self.ptc_act, self.ptc_dve, self.av_ready, self.av_done) = (
            s.sem(n) for n in ("km_pool", "km_dve", "sc_ready", "max_raw", "max_ready", "exp_done", "rinv_ready",
                               "pt_ready", "ptc_act", "ptc_dve", "av_ready", "av_done"))

    def scores(self, pe, u, operands):
        pe.wait_ge(self.km_pool, u + 1)
        pe.wait_ge(self.km_dve, u + 1)
        if u >= 2:
            pe.wait_ge(self.exp_done, HEADS_U * (u - 1))
        for b in range(2):
            q, k = operands(u, b)
            mm = pe.matmul(self.sc[u % 2][:, b, 0:3 * P], q, k, start=True, stop=True)
        mm.then_inc(self.sc_ready, 1)

    def transposes(self, pe, u):
        if u >= 1:
            pe.wait_ge(self.ptc_act, u)
            pe.wait_ge(self.ptc_dve, u)
        for hd in range(HEADS_U):
            tr = pe.transpose(self.pt[hd // 4][:, (hd % 4) * P:(hd % 4 + 1) * P], self.prob[:, u % 2, hd, :], self.g.ident[:])
        tr.then_inc(self.pt_ready, 1)

    def wait_values(self, pe, u):
        pe.wait_ge(self.ptc_act, u + 1)
        pe.wait_ge(self.ptc_dve, u + 1)
        if u >= 2:
            pe.wait_ge(self.av_done, u - 1)

    def exps(self, act, u, heads):
        if heads[0] == 0:
            act.wait_ge(self.max_ready, u + 1)
            if u >= 2:
                act.wait_ge(self.pt_ready, u - 1)
                act.wait_ge(self.rinv_ready, u - 1)
        for hd in heads:
            act.activation(self.prob[:, u % 2, hd, :], self.sc[u % 2][:, hd // 3, (hd % 3) * P:(hd % 3 + 1) * P], ACT.Exp,
                           bias=self.nmax[:, u % 2, hd:hd + 1], scale=self.scale,
                           accum_out=self.rsum[:, u % 2, hd:hd + 1]).then_inc(self.exp_done, 1)

    def leave_act(self, act, u):
        act.wait_ge(self.pt_ready, u + 1)
        if u >= 2:
            act.wait_ge(self.av_ready, u - 1)
        act.activation(self.probT[:, u % 2, 0:4, :], self.pt[0][:].rearrange("p (h c) -> p h c", h=4), ACT.Copy
                       ).then_inc(self.ptc_act, 1)

    def leave_dve(self, dve, u):
        dve.wait_ge(self.pt_ready, u + 1)
        if u >= 2:
            dve.wait_ge(self.av_ready, u - 1)
        dve.tensor_copy(self.probT[:, u % 2, 4:6, :], self.pt[1][:, 0:2 * P].rearrange("p (h c) -> p h c", h=2)
                        ).then_inc(self.ptc_dve, 1)

    def maximum(self, dve, u):
        dve.wait_ge(self.sc_ready, u + 1)
        if u >= 2:
            dve.wait_ge(self.exp_done, HEADS_U * (u - 1))
        b = u % 2
        dve.tensor_reduce(self.nmax[:, b, :].rearrange("p (a h) -> p a h", a=2),
                          self.sc[b][:, :, 0:3 * P].rearrange("p a (h c) -> p a h c", h=3), AX.X, ALU.max, negate=True
                          ).then_inc(self.max_raw, 1)
        dve.wait_ge(self.max_raw, u + 1)
        dve.tensor_scalar(self.nmax[:, b, :], self.nmax[:, b, :], self.scale, None, ALU.mult).then_inc(self.max_ready, 1)

    def inverse(self, dve, u):
        dve.wait_ge(self.exp_done, HEADS_U * (u + 1))
        dve.reciprocal(self.rinv[:, u % 2, :], self.rsum[:, u % 2, :]).then_inc(self.rinv_ready, 1)
        dve.wait_ge(self.rinv_ready, u + 1)


def attention0(nc, g, a):
    DH, GH = 16, 6
    KM = KD + TILE_IMAGES
    UNITS = 2 * TILES
    with Scope(nc, "at0") as s:
        w = s.sb("w", [KD, NKD, 3 * D])
        bias = s.sb("bias", [KD, 4])
        bv = s.sb("bv", [P, D])
        o = s.sb("o", [P, 2, D // 2])
        t = Attend(s, g, UNITS, 1.0, KM, GH)
        w_in, qk_ready, qk_done, v_ready, v_done, step = (
            s.sem(n) for n in ("w_in", "qk_ready", "qk_done", "v_ready", "v_done", "step"))
        banks = [t.sc[0][:, 0], t.sc[0][:, 1], t.sc[1][:, 0], t.sc[1][:, 1], t.pt[0][:], t.pt[1][:], t.av[0][:], t.av[1][:]]
        loads = [(w[:], a["wqkv"]), (bias[:], a["bqk"]), (bv[:], a["bv_rows"]), (t.hm[:], a["head_mask0"])]
        loads += [(t.qT[KD:KM, b, :], a["mask_q"][0:TILE_IMAGES]) for b in range(2)]
        loads += [(t.kTm[KD:KM, b, :, :], a["mask_k"][0:TILE_IMAGES]) for b in range(KEYS_DEEP)]
        layernorm(nc, g, "ln0", banks[0:4], loads, w_in)
        block = s.block()

        def keys(eng, u, heads, sem):
            i, grp = u // 2, u % 2
            if u >= KEYS_DEEP:
                eng.wait_ge(t.sc_ready, u - KEYS_DEEP + 1)
            for hd in heads:
                op = eng.tensor_scalar(t.kTm[0:KD, u % KEYS_DEEP, hd, :], t.kT[:, grp, i * P:(i + 1) * P],
                                       t.hm[:, hd:hd + 1], None, ALU.mult)
            op.then_inc(sem, 1)

        @block.tensor
        def _(pe):
            pe.wait_ge(w_in, 16 * len(loads))
            for n in range(8):
                part, half = n // 2, n % 2
                for k in range(NKD):
                    mm = pe.matmul(banks[n][0:KD, :], w[:, k, part * KD:(part + 1) * KD],
                                   g.xnT[:, k, half * 512:(half + 1) * 512], start=(k == 0), stop=(k == NKD - 1))
                mm.then_inc(qk_ready, 1)
            for i in range(TILES):
                pe.wait_ge(qk_done, i + 1)
                for k in range(NKD):
                    mm = pe.matmul(banks[i][:, 0:D], g.xnT[:, k, i * P:(i + 1) * P], w[:, k, 2 * D:3 * D],
                                   start=(k == 0), stop=(k == NKD - 1))
                mm.then_inc(v_ready, 1)

            def operands(u, b):
                i, grp = u // 2, u % 2
                return t.qT[:, grp, i * P:(i + 1) * P], t.kTm[:, u % KEYS_DEEP, 3 * b:3 * b + 3, :]

            def values(u):
                i, grp = u // 2, u % 2
                t.wait_values(pe, u)
                for hd in range(GH):
                    at = (grp * GH + hd) * DH
                    mm = pe.matmul(t.av[u % 2][:, hd * DH:(hd + 1) * DH], t.probT[:, u % 2, hd, :], t.v[:, i, at:at + DH],
                                   start=True, stop=True)
                mm.then_inc(t.av_ready, 1)

            pe.wait_ge(v_done, TILES)
            t.scores(pe, 0, operands)
            t.scores(pe, 1, operands)
            for u in range(UNITS):
                pe.wait_ge(t.exp_done, HEADS_U * (u + 1))
                t.transposes(pe, u)
                if u + 2 < UNITS:
                    t.scores(pe, u + 2, operands)
                if u >= 1:
                    values(u - 1)
            values(UNITS - 1)

        @block.scalar
        def _(act):
            act.wait_ge(w_in, 16 * len(loads))
            for n in range(8):
                part, half = n // 2, n % 2
                act.wait_ge(qk_ready, n + 1)
                dst = (t.qT[0:KD] if part < 2 else t.kT[:])[:, part % 2, half * 512:(half + 1) * 512]
                act.activation(dst, banks[n][0:KD, :], ACT.Identity, bias=bias[:, part:part + 1]).then_inc(qk_done, 1)
            t.exps(act, 0, range(HEADS_U))
            for u in range(UNITS):
                if u + 1 < UNITS:
                    t.exps(act, u + 1, range(HEADS_U // 2))
                t.leave_act(act, u)
                if u + 1 < UNITS:
                    t.exps(act, u + 1, range(HEADS_U // 2, HEADS_U))

        @block.gpsimd
        def _(pool):
            pool.wait_ge(qk_done, 8)
            pool.wait_ge(w_in, 16 * len(loads))
            for u in range(UNITS):
                keys(pool, u, range(GH // 2), t.km_pool)

        @block.vector
        def _(dve):
            c = Chain(dve, step)
            dve.wait_ge(w_in, 16 * len(loads))
            for i in range(TILES):
                dve.wait_ge(v_ready, i + 1)
                dve.tensor_tensor(t.v[:, i, :], banks[i][:, 0:D], bv[:], ALU.add).then_inc(v_done, 1)

            def finish(u):
                i, grp = u // 2, u % 2
                hs = g.h[:, i, grp * 96:(grp + 1) * 96]
                dve.wait_ge(t.av_ready, u + 1)
                dve.tensor_tensor(o[:, u % 2, :].rearrange("p (h d) -> p h d", h=GH),
                                  t.av[u % 2][:, 0:GH * DH].rearrange("p (h d) -> p h d", h=GH),
                                  t.rinv[:, u % 2, :].unsqueeze(2).to_broadcast([P, GH, DH]), ALU.mult).then_inc(t.av_done, 1)
                dve.wait_ge(t.av_done, u + 1)
                c.after(dve.tensor_tensor(hs, hs, o[:, u % 2, :], ALU.add))

            dve.wait_ge(qk_done, 8)
            for u in range(KEYS_DEEP):
                keys(dve, u, range(GH // 2, GH), t.km_dve)
            t.maximum(dve, 0)
            t.maximum(dve, 1)
            for u in range(UNITS):
                if u + KEYS_DEEP < UNITS:
                    keys(dve, u + KEYS_DEEP, range(GH // 2, GH), t.km_dve)
                t.inverse(dve, u)
                t.leave_dve(dve, u)
                if u + 2 < UNITS:
                    t.maximum(dve, u + 2)
                if u >= 1:
                    finish(u - 1)
            finish(UNITS - 1)


def attention1(nc, g, a):
    DH, GH, RANK = 32, 3, 48
    KM = KD + TILE_IMAGES + PATCHES
    UNITS = TILES
    with Scope(nc, "at1") as s:
        wa = s.sb("wa", [KD, NKD, 3, RANK])
        wb = s.sb("wb", [RANK, 3, D])
        wr = s.sb("wr", [RANK, 2, D])
        ow = s.sb("ow", [KD, NKD, D])
        low = s.sb("low", [RANK, 3, TOKENS])
        cosT, sinT = (s.sb(n, [KD, 512]) for n in ("cosT", "sinT"))
        rope = s.sb("rope", [KD, 2, 2, 512])
        oT = s.sb("oT", [KD, 2, 2, P])
        t = Attend(s, g, UNITS, 1.0 / float(np.sqrt(DH)), KM, GH)
        w_in, rot_ready, low_ready, low_done, qk_ready, cs_done, rope_done, v_ready, v_done, oT_ready, o_ready, prob_ready, step = (
            s.sem(n) for n in ("w_in", "rot_ready", "low_ready", "low_done", "qk_ready", "cs_done", "rope_done", "v_ready",
                               "v_done", "oT_ready", "o_ready", "prob_ready", "step"))
        banks = [t.sc[0][:, 0], t.sc[0][:, 1], t.sc[1][:, 0], t.sc[1][:, 1], t.pt[0][:], t.pt[1][:], t.av[0][:], t.av[1][:]]
        loads = [(ow[:], a["o_w"]), (t.hm[:], a["head_mask1"]), (cosT[:], a["cosT"]), (sinT[:], a["sinT"])]
        for n, x in enumerate("qkv"):
            loads += [(wa[:, :, n, :], a[x + "A"]), (wb[:, n, :], a[x + "B"])]
        loads += [(t.qT[KD:KM, b, :], a["mask_q"]) for b in range(2)]
        loads += [(t.kTm[KD:KM, b, :, :], a["mask_k"]) for b in range(KEYS_DEEP)]
        layernorm(nc, g, "ln2", banks[0:4], loads, w_in)
        block = s.block()

        def keys(eng, u, heads, sem):
            if u >= KEYS_DEEP:
                eng.wait_ge(t.sc_ready, u - KEYS_DEEP + 1)
            for j in heads:
                op = eng.tensor_scalar(t.kTm[0:KD, u % KEYS_DEEP].rearrange("p (g h) c -> p g h c", g=2)[:, :, j, :],
                                       t.kT[:, :, u * P:(u + 1) * P], t.hm[:, j:j + 1], None, ALU.mult)
            op.then_inc(sem, 1)

        parts = [(x, grp, half) for x in range(2) for grp in range(2) for half in range(2)]

        @block.tensor
        def _(pe):
            pe.wait_ge(w_in, 16 * len(loads))
            for n in range(6):
                x, half = n // 2, n % 2
                for k in range(NKD):
                    mm = pe.matmul(banks[n][0:RANK, :], wa[:, k, x, :], g.xnT[:, k, half * 512:(half + 1) * 512],
                                   start=(k == 0), stop=(k == NKD - 1))
                mm.then_inc(low_ready, 1)
            pe.wait_ge(low_done, 6)
            pe.wait_ge(rot_ready, 4)
            for n, (x, grp, half) in enumerate(parts):
                if n >= 4:
                    pe.wait_ge(cs_done, 2 * (n - 3))
                for r, m in enumerate((wb, wr)):
                    mm = pe.matmul(banks[2 * (n % 4) + r][0:KD, :], m[:, x, grp * KD:(grp + 1) * KD],
                                   low[:, x, half * 512:(half + 1) * 512], start=True, stop=True)
                mm.then_inc(qk_ready, 1)
            for i in range(TILES):
                pe.wait_ge(cs_done, 2 * (5 + i // 2))
                pe.matmul(banks[i][:, 0:D], low[:, 2, i * P:(i + 1) * P], wb[:, 2, :], start=True, stop=True).then_inc(v_ready, 1)

            def operands(u, b):
                return t.qT[:, b, u * P:(u + 1) * P], t.kTm[:, u % KEYS_DEEP, 3 * b:3 * b + 3, :]

            def values(u):
                t.wait_values(pe, u)
                for hd in range(HEADS_U):
                    grp, j = hd // GH, hd % GH
                    mm = pe.matmul(t.av[u % 2][j * DH:(j + 1) * DH, grp * P:(grp + 1) * P], t.v[:, u, hd * DH:(hd + 1) * DH],
                                   t.probT[:, u % 2, hd, :], start=True, stop=True)
                mm.then_inc(t.av_ready, 1)

            def project(u):
                pe.wait_ge(oT_ready, u + 1)
                for k in range(NKD):
                    mm = pe.matmul(t.av[u % 2][:, 256:256 + D], oT[:, u % 2, k, :], ow[:, k, :],
                                   start=(k == 0), stop=(k == NKD - 1))
                mm.then_inc(o_ready, 1)

            pe.wait_ge(v_done, TILES)
            t.scores(pe, 0, operands)
            t.scores(pe, 1, operands)
            for u in range(UNITS):
                if u + 2 < UNITS:
                    t.scores(pe, u + 2, operands)
                pe.wait_ge(prob_ready, u + 1)
                t.transposes(pe, u)
                if u >= 2:
                    project(u - 2)
                if u >= 1:
                    values(u - 1)
            project(UNITS - 2)
            values(UNITS - 1)
            project(UNITS - 1)

        @block.scalar
        def _(act):
            for n in range(6):
                x, half = n // 2, n % 2
                act.wait_ge(low_ready, n + 1)
                act.activation(low[:, x, half * 512:(half + 1) * 512], banks[n][0:RANK, :], ACT.Copy).then_inc(low_done, 1)

            def leave_values(u):
                act.wait_ge(t.av_ready, u + 1)
                if u >= 2:
                    act.wait_ge(o_ready, u - 1)
                act.activation(oT[:, u % 2, :, :], t.av[u % 2][0:KD, 0:2 * P].rearrange("p (g c) -> p g c", g=2), ACT.Copy
                               ).then_inc(oT_ready, 1)

            t.exps(act, 0, range(HEADS_U))
            for u in range(UNITS):
                if u >= 2:
                    leave_values(u - 2)
                if u + 1 < UNITS:
                    t.exps(act, u + 1, range(HEADS_U // 2))
                t.leave_act(act, u)
                if u + 1 < UNITS:
                    t.exps(act, u + 1, range(HEADS_U // 2, HEADS_U))
            leave_values(UNITS - 2)
            leave_values(UNITS - 1)

        @block.gpsimd
        def _(pool):
            pool.wait_ge(rope_done, len(parts))
            pool.wait_ge(w_in, 16 * len(loads))
            for u in range(UNITS):
                keys(pool, u, (0,), t.km_pool)

        @block.vector
        def _(dve):
            c = Chain(dve, step)
            dve.wait_ge(w_in, 16 * len(loads))
            for x in range(2):
                src = wb[:, x, :].rearrange("p (h r d) -> p h r d", h=HEADS_U, r=2)
                dst = wr[:, x, :].rearrange("p (h r d) -> p h r d", h=HEADS_U, r=2)
                dve.tensor_scalar(dst[:, :, 0, :], src[:, :, 1, :], -1.0, None, ALU.mult).then_inc(rot_ready, 1)
                dve.tensor_copy(dst[:, :, 1, :], src[:, :, 0, :]).then_inc(rot_ready, 1)
            for n, (x, grp, half) in enumerate(parts):
                dst = (t.qT[0:KD] if x == 0 else t.kT[:])[:, grp, half * 512:(half + 1) * 512]
                dve.wait_ge(qk_ready, n + 1)
                if n >= 2:
                    dve.wait_ge(rope_done, n - 1)
                dve.tensor_tensor(rope[:, n % 2, 0, :], banks[2 * (n % 4)][0:KD, :], cosT[:], ALU.mult).then_inc(cs_done, 1)
                dve.tensor_tensor(rope[:, n % 2, 1, :], banks[2 * (n % 4) + 1][0:KD, :], sinT[:], ALU.mult).then_inc(cs_done, 1)
                dve.wait_ge(cs_done, 2 * n + 2)
                dve.tensor_tensor(dst, rope[:, n % 2, 0, :], rope[:, n % 2, 1, :], ALU.add).then_inc(rope_done, 1)
            for i in range(TILES):
                dve.wait_ge(v_ready, i + 1)
                dve.tensor_copy(t.v[:, i, :], banks[i][:, 0:D]).then_inc(v_done, 1)

            def finish(u):
                dve.wait_ge(o_ready, u + 1)
                dve.tensor_tensor(g.h[:, u, :], g.h[:, u, :], t.av[u % 2][:, 256:256 + D], ALU.add).then_inc(t.av_done, 1)

            dve.wait_ge(rope_done, len(parts))
            for u in range(KEYS_DEEP):
                keys(dve, u, (1, 2), t.km_dve)
            t.maximum(dve, 0)
            t.maximum(dve, 1)
            for u in range(UNITS):
                if u + KEYS_DEEP < UNITS:
                    keys(dve, u + KEYS_DEEP, (1, 2), t.km_dve)
                t.inverse(dve, u)
                dve.tensor_tensor(t.prob[:, u % 2], t.prob[:, u % 2], t.rinv[:, u % 2, :].unsqueeze(2).to_broadcast([P, HEADS_U, P]),
                                  ALU.mult).then_inc(prob_ready, 1)
                if u + 2 < UNITS:
                    t.maximum(dve, u + 2)
                t.leave_dve(dve, u)
                if u >= 2:
                    finish(u - 2)
            finish(UNITS - 2)
            finish(UNITS - 1)
            dve.wait_ge(t.av_done, UNITS)


def slot_weights(nc, g, CT, Dn, zn):
    with Scope(nc, "slw") as s:
        nmax, zsum, rz = (s.sb(n, [P, 2]) for n in ("nmax", "zsum", "rz"))
        ze = s.sb("ze", [P, 2, SLOT_E])
        ex = s.sb("ex", [P, 2, ALL_SLOTS])
        dmax, dsum = (s.sb(n, [P, 2, IMAGES]) for n in ("dmax", "dsum"))
        cl = s.ps("cl", [P, 2, 512])
        dl = s.ps("dl", [P, 2, 2, 512])
        tp = s.ps("tp", [P, 2, 512])
        step, cl_ready, cmax_ready, cexp_ready, cw_ready, tp_ready, ct_done, dl_ready, dsub_ready, dexp_ready = (
            s.sem(n) for n in ("step", "cl_ready", "cmax_ready", "cexp_ready", "cw_ready", "tp_ready", "ct_done",
                               "dl_ready", "dsub_ready", "dexp_ready"))
        block = s.block()

        @block.tensor
        def _(pe):
            pe.wait_ge(g.phi_in, 16)

            def combine_transposed(i):
                pe.wait_ge(cw_ready, i + 1)
                if i >= 1:
                    pe.wait_ge(ct_done, i)
                for c in range(SLOT_CHUNKS):
                    tr = pe.transpose(tp[:, c // 4, (c % 4) * P:(c % 4 + 1) * P], ex[:, i % 2, c * P:(c + 1) * P], g.ident[:])
                tr.then_inc(tp_ready, 1)

            for i in range(TILES):
                if i >= 1:
                    pe.wait_ge(cexp_ready, SLOT_E * i)
                for half in range(2):
                    for k in range(NKD):
                        mm = pe.matmul(cl[:, half, :], g.xnT[:, k, i * P:(i + 1) * P], g.phi[:, k, half * 512:(half + 1) * 512],
                                       start=(k == 0), stop=(k == NKD - 1))
                mm.then_inc(cl_ready, 1)
                if i >= 2:
                    pe.wait_ge(dsub_ready, i - 1)
                for half in range(2):
                    for k in range(NKD):
                        mm = pe.matmul(dl[:, i % 2, half, :], g.phi[:, k, i * P:(i + 1) * P], g.xnT[:, k, half * 512:(half + 1) * 512],
                                       start=(k == 0), stop=(k == NKD - 1))
                mm.then_inc(dl_ready, 1)
                if i >= 1:
                    combine_transposed(i - 1)
            combine_transposed(TILES - 1)

        @block.scalar
        def _(act):
            def leave(i):
                act.wait_ge(tp_ready, i + 1)
                act.activation(CT[:, :, i * P:(i + 1) * P], tp[:].rearrange("p a (c t) -> p (a c) t", c=4), ACT.Copy).then_inc(ct_done, 1)

            for i in range(TILES):
                act.wait_ge(cmax_ready, i + 1)
                if i >= 2:
                    act.wait_ge(tp_ready, i - 1)
                for e in range(SLOT_E):
                    act.activation(ex[:, i % 2, e * SLOTS:(e + 1) * SLOTS], cl[:, e // 2, (e % 2) * SLOTS:(e % 2 + 1) * SLOTS],
                                   ACT.Exp, bias=nmax[:, i % 2:i % 2 + 1], accum_out=ze[:, i % 2, e:e + 1]).then_inc(cexp_ready, 1)
                act.wait_ge(dsub_ready, i + 1)
                act.activation(Dn[:, i, :], Dn[:, i, :], ACT.Exp).then_inc(dexp_ready, 1)
                if i >= 1:
                    leave(i - 1)
            leave(TILES - 1)

        @block.vector
        def _(dve):
            c = Chain(dve, step)

            def by_image(x):
                return x.rearrange("p (b n) -> p b n", n=PATCHES)

            def spread(x):
                return x.unsqueeze(2).to_broadcast([P, IMAGES, PATCHES])

            def normalise(i):
                b = i % 2
                dve.wait_ge(dexp_ready, i + 1)
                c.after(dve.tensor_reduce(dsum[:, b, :], by_image(Dn[:, i, :]), AX.X, ALU.add))
                c.after(dve.reciprocal(dsum[:, b, :], dsum[:, b, :]))
                c.after(dve.tensor_tensor(by_image(Dn[:, i, :]), by_image(Dn[:, i, :]), spread(dsum[:, b, :]), ALU.mult))

            for i in range(TILES):
                b = i % 2
                dve.wait_ge(cl_ready, i + 1)
                dve.tensor_reduce(nmax[:, b:b + 1], cl[:], AX.XY, ALU.max, negate=True).then_inc(cmax_ready, 1)
                dve.wait_ge(dl_ready, i + 1)
                for half in range(2):
                    c.after(dve.tensor_reduce(dmax[:, b, 32 * half:32 * half + 32], by_image(dl[:, b, half, :]), AX.X, ALU.max))
                for half in range(2):
                    op = dve.tensor_tensor(by_image(Dn[:, i, half * 512:(half + 1) * 512]), by_image(dl[:, b, half, :]),
                                           dmax[:, b, 32 * half:32 * half + 32].unsqueeze(2).to_broadcast([P, 32, PATCHES]),
                                           ALU.subtract)
                op.then_inc(dsub_ready, 1)
                dve.wait_ge(cexp_ready, SLOT_E * (i + 1))
                c.after(dve.tensor_reduce(zsum[:, b:b + 1], ze[:, b, :], AX.X, ALU.add))
                c.after(dve.reciprocal(rz[:, b:b + 1], zsum[:, b:b + 1]))
                c.after(dve.tensor_scalar(zn[:, i, :], ze[:, b, :], rz[:, b:b + 1], None, ALU.mult))
                dve.tensor_scalar(ex[:, b, :], ex[:, b, :], rz[:, b:b + 1], None, ALU.mult).then_inc(cw_ready, 1)
                if i >= 1:
                    normalise(i - 1)
            normalise(TILES - 1)


def hidden_pieces(nc, g, b1, g_dram, b_dram):
    WIDE = SLOT_E * HID
    with Scope(nc, "hid") as s:
        gp = s.sb("gp", [P, 2, 3, WIDE], BF16)
        rest = s.sb("rest", [P, 2, HID])
        b1f = s.sb("b1f", [P, 2, WIDE // P])
        bp = s.sb("bp", [P, 3, WIDE // P], BF16)
        gps = [s.ps(f"gps{i}", [P, 2, 512]) for i in range(4)]
        b_in, step, g_ready, one, rest1, two, three, b_done, g_out = (
            s.sem(n) for n in ("b_in", "step", "g_ready", "one", "rest1", "two", "three", "b_done", "g_out"))
        out_done = [s.sem(f"out_done{i}") for i in range(2)]
        block = s.block()
        steps = [(i, e) for i in range(TILES) for e in range(SLOT_E)]

        @block.sync
        def _(sp):
            sp.dma_start(b1f[:, 0, :], b1).then_inc(b_in, 16)
            for i in range(TILES):
                sp.wait_ge(three, SLOT_E * (i + 1))
                for k in range(3):
                    sp.dma_start(g_dram[k, i * P:(i + 1) * P, :], gp[:, i % 2, k, :]).then_inc(out_done[i % 2], 16)
            sp.wait_ge(b_done, 1)
            sp.dma_start(b_dram.rearrange("k (p c) -> p k c", p=P), bp[:]).then_inc(g_out, 16)
            sp.wait_ge(g_out, 16)
            for k in range(2):
                sp.wait_ge(out_done[k], 48 * TILES // 2)

        @block.tensor
        def _(pe):
            pe.wait_ge(g.w1_in, 16)
            for n, (i, e) in enumerate(steps):
                if n >= 4:
                    pe.wait_ge(rest1, n - 3)
                for half in range(2):
                    for k in range(NKD):
                        at = e * HID + half * HALF
                        mm = pe.matmul(gps[n % 4][:, half, 0:HALF], g.xnT[:, k, i * P:(i + 1) * P],
                                       g.w1[:, k, at:at + HALF], start=(k == 0), stop=(k == NKD - 1))
                mm.then_inc(g_ready, 1)

        def piece(buf, k, e):
            return gp[:, buf, k, e * HID:(e + 1) * HID].rearrange("p (a c) -> p a c", a=2)

        def halves(x):
            return x.rearrange("p (a c) -> p a c", a=2)

        @block.scalar
        def _(act):
            def second(n):
                i, e = steps[n]
                act.wait_ge(rest1, n + 1)
                act.activation(piece(i % 2, 1, e), halves(rest[:, n % 2, :]), ACT.Copy).then_inc(two, 1)

            for n, (i, e) in enumerate(steps):
                act.wait_ge(g_ready, n + 1)
                if i >= 2:
                    act.wait_ge(out_done[i % 2], 48 * (i // 2))
                act.activation(piece(i % 2, 0, e), gps[n % 4][:, :, 0:HALF], ACT.Copy).then_inc(one, 1)
                if n >= 1:
                    second(n - 1)
            second(len(steps) - 1)

        @block.vector
        def _(dve):
            c = Chain(dve, step)
            dve.wait_ge(b_in, 16)
            c.after(dve.tensor_copy(bp[:, 0, :], b1f[:, 0, :]))
            c.after(dve.tensor_tensor(b1f[:, 1, :], b1f[:, 0, :], bp[:, 0, :], ALU.subtract))
            c.after(dve.tensor_copy(bp[:, 1, :], b1f[:, 1, :]))
            dve.tensor_tensor(bp[:, 2, :], b1f[:, 1, :], bp[:, 1, :], ALU.subtract).then_inc(b_done, 1)

            def third(n):
                i, e = steps[n]
                dve.wait_ge(two, n + 1)
                dve.tensor_tensor(piece(i % 2, 2, e), halves(rest[:, n % 2, :]), piece(i % 2, 1, e), ALU.subtract).then_inc(three, 1)

            for n, (i, e) in enumerate(steps):
                dve.wait_ge(one, n + 1)
                if n >= 2:
                    dve.wait_ge(three, n - 1)
                dve.tensor_tensor(halves(rest[:, n % 2, :]), gps[n % 4][:, :, 0:HALF], piece(i % 2, 0, e), ALU.subtract).then_inc(rest1, 1)
                if n >= 1:
                    third(n - 1)
            third(len(steps) - 1)


def slot_experts(nc, g, CT, Dn, zn, b2_rows, g_dram, b_dram):
    TP = TILE_IMAGES // 2
    with Scope(nc, "sle") as s:
        G = s.sb("G", [BROWS, 2, SLOT_E * HID], BF16)
        dp = s.sb("dp", [P, 2, SLOT_CHUNKS, BROWS], BF16)
        rest = s.sb("rest", [P, 2, SLOT_CHUNKS, PATCHES])
        dT = s.sb("dT", [BROWS, 2, ALL_SLOTS], BF16)
        cw = s.sb("cw", [P, 2, SLOT_CHUNKS, 2 * PATCHES])
        H = s.sb("H", [P, 8, HID])
        U = s.sb("U", [P, HID])
        UT = s.sb("UT", [P, HC, SLOT_E, TILE_IMAGES, PATCHES])
        b2 = s.sb("b2", [P, SLOT_E, D])
        acc = s.sb("acc", [P, D])
        identb = s.sb("identb", [P, P], BF16)
        hp = [s.ps(f"hp{i}", [P, 2, 512]) for i in range(2)]
        up = s.ps("up", [P, 2, 512])
        dps = s.ps("dps", [P, 1024], BF16)
        tps = s.ps("tps", [P, 512])
        b_in, consts, identb_ready, turn, step, pstep, pieces_ready, cw_ready, dps_ready, dT_ready, hid_ready, gelu_done, mix_done, \
            u_ready, ut_ready, ut_done, y_ready, y_done = (s.sem(n) for n in (
                "b_in", "consts", "identb_ready", "turn", "step", "pstep", "pieces_ready", "cw_ready", "dps_ready", "dT_ready", "hid_ready",
                "gelu_done", "mix_done", "u_ready", "ut_ready", "ut_done", "y_ready", "y_done"))
        g_in = [s.sem(f"g_in{i}") for i in range(2)]
        block = s.block()
        ORDER = [0, 2, 4, 6, 1, 3, 5, 7]
        BEFORE = [[], [(1, 0)], [], [(1, 1)], [], [], [], []]
        OWN = [[], [], [], [], [], [(0, 0)], [], [(0, 1)]]
        POOL_STEPS = 5

        def program(eng, pair):
            pair(0, None, True, 0, None)
            with eng.Fori(1, TP) as j:
                pair(j, None, False, j, None)
            with eng.Fori(1, TILES) as t:
                pair(TP * t, t - 1, False, 0, None)
                with eng.Fori(1, TP) as j:
                    pair(TP * t + j, None, False, j, t)

        @block.sync
        def _(sp):
            sp.dma_start(b2[:].rearrange("p e d -> p (e d)"), b2_rows).then_inc(b_in, 16)
            for p in range(2):
                sp.dma_start(G[PROWS:BROWS, p, :], b_dram).then_inc(b_in, 16)

            def pair(r, prev, first, j, tile):
                for p in range(2):
                    n = 2 * r + p
                    if not first:
                        sp.wait_ge(hid_ready, 8 * n - 8)
                    row = 0
                    for k, copies in ((0, 3), (1, 2), (2, 1)):
                        src = g_dram[k, bass.ds(n * PATCHES, PATCHES), :]
                        for c in range(copies):
                            sp.dma_start(G[row:row + PATCHES, p, :], src).then_inc(g_in[p], 16)
                            row += PATCHES

            program(sp, pair)

        @block.gpsimd
        def _(pool):
            pool.memset(dp[:], 1.0).then_inc(consts, 1)
            pool.memset(cw[:], 0.0).then_inc(consts, 1)
            pool.wait_ge(consts, 2)

            def pieces(n, p, first, image):
                c = Chain(pool, pstep, base=POOL_STEPS * n, turn=turn)
                if not first:
                    pool.wait_ge(dps_ready, n - 1)
                    pool.sem_inc(turn, 1)
                q = PATCHES
                src = Dn[:, :, bass.ds(image * PATCHES, PATCHES)]
                d = dp[:, p]
                c.after(pool.tensor_copy(d[:, :, 0:q], src))
                c.after(pool.tensor_tensor(rest[:, p], src, d[:, :, 0:q], ALU.subtract))
                c.after(pool.tensor_copy(d[:, :, q:2 * q], rest[:, p]))
                c.after(pool.tensor_tensor(d[:, :, 2 * q:3 * q], rest[:, p], d[:, :, q:2 * q], ALU.subtract))
                c.after(pool.tensor_copy(d[:, :, 3 * q:5 * q], d[:, :, 0:2 * q]))
                pool.tensor_copy(d[:, :, 5 * q:6 * q], d[:, :, 0:q]).then_inc(pieces_ready, 1)

            def pair(r, prev, first, j, tile):
                for p in range(2):
                    n = 2 * r + p
                    pieces(n, p, first, n)
                    if not first:
                        pool.wait_ge(mix_done, 4 * n - 4)
                        pool.sem_inc(turn, 1)
                    pool.tensor_copy(cw[:, p, :, p * PATCHES:(p + 1) * PATCHES], CT[:, :, bass.ds(n * PATCHES, PATCHES)]).then_inc(cw_ready, 1)

            program(pool, pair)
            pieces(IMAGES, 0, False, IMAGES - 1)

        @block.tensor
        def _(pe):
            pe.wait_ge(b_in, 48)
            pe.wait_ge(identb_ready, 1)
            pe.wait_ge(g.w2_in, 16)

            def transpose_pieces(n, p, chunks):
                if chunks[0] == 0:
                    pe.wait_ge(pieces_ready, n + 1)
                    pe.wait_ge(dT_ready, n)
                for c in chunks:
                    tr = pe.transpose(dps[0:BROWS, c * P:(c + 1) * P], dp[:, p, c, :], identb[:])
                if chunks[-1] == SLOT_CHUNKS - 1:
                    tr.then_inc(dps_ready, 1)

            def mix(n, p, r, grp, half):
                pe.wait_ge(gelu_done, 8 * n + 4 * grp + 4)
                if half == 0 and grp == 0:
                    pe.wait_ge(cw_ready, n + 1)
                if p == 0 and grp == 0 and not (isinstance(r, int) and r == 0):
                    pe.wait_ge(u_ready, 2 * r - 1 + half)
                for e in range(SLOT_E):
                    mm = pe.matmul(up[32 * e:32 * e + 32, half, 0:HALF], cw[:, p, 2 * e + grp, :],
                                   H[:, 4 * grp + e, half * HALF:(half + 1) * HALF],
                                   start=(p == 0 and grp == 0), stop=(p == 1 and grp == 1))
                mm.then_inc(mix_done, 1)

            def transpose_u(r, part):
                pe.wait_ge(u_ready, 2 * r + part + 1)
                pe.wait_ge(ut_done, 2 * r + part + 1)
                for c in range(3):
                    at = (3 * part + c) * P
                    tr = pe.transpose(tps[:, c * P:(c + 1) * P], U[:, at:at + P], g.ident[:])
                tr.then_inc(ut_ready, 1)

            def down(t):
                pe.wait_ge(ut_done, 2 * TP * (t + 1) + 1)
                for e in range(SLOT_E):
                    for c in range(HC):
                        mm = pe.matmul(tps[:, 0:D], UT[:, c, e, :, :], g.w2[:, e * HC + c, :],
                                       start=(e == 0 and c == 0), stop=(e == SLOT_E - 1 and c == HC - 1))
                mm.then_inc(y_ready, 1)

            def pair(r, prev, first, j, tile):
                for p in range(2):
                    n = 2 * r + p
                    start = first and p == 0
                    if start:
                        transpose_pieces(0, 0, range(SLOT_CHUNKS))
                    pe.wait_ge(dT_ready, n + 1)
                    pe.wait_ge(g_in[p], 96 * r + 96)
                    for q in range(SLOT_CHUNKS):
                        c = ORDER[q]
                        if not (start and q < 2):
                            pe.wait_ge(gelu_done, 8 * n + q - 1)
                        for half in range(2):
                            at = (c // 2) * HID + half * HALF
                            mm = pe.matmul(hp[q % 2][:, half, 0:HALF], dT[:, p, c * P:(c + 1) * P],
                                           G[:, p, at:at + HALF], start=True, stop=True)
                        mm.then_inc(hid_ready, 1)
                        if not start:
                            for grp, half in BEFORE[q]:
                                mix(n - 1, 1 - p, r - 1 + p, grp, half)
                        for grp, half in OWN[q]:
                            mix(n, p, r, grp, half)
                        if q in (2, 4):
                            transpose_pieces(n + 1, 1 - p, range(2 * q - 4, 2 * q))
                        if q == (6, 0)[p] and not first:
                            if tile is not None and p == 0:
                                pe.wait_ge(y_done, tile)
                            transpose_u(r - 1, p)
                        if q == 6 and prev is not None and p == 1:
                            down(prev)

            program(pe, pair)
            for grp, half in sum(BEFORE, []):
                mix(IMAGES - 1, 1, IMAGES // 2 - 1, grp, half)
            transpose_u(IMAGES // 2 - 1, 0)
            transpose_u(IMAGES // 2 - 1, 1)
            down(TILES - 1)

        @block.scalar
        def _(act):
            def pair(r, prev, first, j, tile):
                for p in range(2):
                    n = 2 * r + p
                    for q in range(SLOT_CHUNKS):
                        act.wait_ge(hid_ready, 8 * n + q + 1)
                        grp = q // 4
                        if q % 4 == 0 and not (first and p == 0):
                            act.wait_ge(mix_done, 4 * n + 2 * grp - 2)
                        act.activation(H[:, q, :].rearrange("p (a c) -> p a c", a=2), hp[q % 2][:, :, 0:HALF],
                                       ACT.Gelu_apprx_tanh).then_inc(gelu_done, 1)

            program(act, pair)

        @block.vector
        def _(dve):
            dve.tensor_copy(identb[:], g.ident[:]).then_inc(identb_ready, 1)
            dve.sem_inc(ut_done, 1)
            FIN = 4

            def leave_pieces(n, p):
                dve.wait_ge(dps_ready, n + 1)
                dve.tensor_copy(dT[:, p, :], dps[0:BROWS, :]).then_inc(dT_ready, 1)

            def leave_u(r, half):
                dve.wait_ge(mix_done, 8 * r + 7 + half)
                dve.tensor_copy(U[:, half * HALF:(half + 1) * HALF], up[:, half, 0:HALF]).then_inc(u_ready, 1)

            def leave_ut(r, part, j):
                dve.wait_ge(ut_ready, 2 * r + part + 1)
                dve.tensor_copy(UT[:, 3 * part:3 * part + 3, :, bass.ds(2 * j, 2), :],
                                tps[:, 0:3 * P].rearrange("p (c e o n) -> p c e o n", c=3, e=SLOT_E, n=PATCHES)).then_inc(ut_done, 1)

            def finish(t):
                c = Chain(dve, step, base=FIN * t)
                dve.wait_ge(y_ready, t + 1)
                ht = g.h[:, bass.ds(t, 1), :].rearrange("p o d -> p (o d)")
                dve.tensor_tensor(acc[:], tps[:, 0:D], ht, ALU.add).then_inc(y_done, 1)
                dve.wait_ge(y_done, t + 1)
                for e in range(SLOT_E):
                    op = dve.scalar_tensor_tensor(acc[:] if e < SLOT_E - 1 else ht, b2[:, e, :],
                                                  zn[:, bass.ds(t, 1), e:e + 1].rearrange("p o e -> p (o e)"),
                                                  acc[:], ALU.mult, ALU.add)
                    if e < SLOT_E - 1:
                        c.after(op)
                op.then_inc(step, 1)

            def pair(r, prev, first, j, tile):
                if first:
                    leave_pieces(0, 0)
                j_before = TP - 1 if prev is not None else j - 1
                if not first:
                    leave_u(r - 1, 0)
                    leave_u(r - 1, 1)
                leave_pieces(2 * r + 1, 1)
                if not first:
                    leave_ut(r - 1, 0, j_before)
                    leave_ut(r - 1, 1, j_before)
                leave_pieces(2 * r + 2, 0)
                if prev is not None:
                    finish(prev)

            dve.wait_ge(b_in, 48)
            program(dve, pair)
            for half in range(2):
                leave_u(IMAGES // 2 - 1, half)
            for part in range(2):
                leave_ut(IMAGES // 2 - 1, part, TP - 1)
            finish(TILES - 1)
            dve.wait_ge(step, FIN * TILES)


def soft_moe(nc, g, a):
    with Scope(nc, "smoe") as s:
        CT = s.sb("CT", [P, SLOT_CHUNKS, TOKENS])
        Dn = s.sb("Dn", [P, SLOT_CHUNKS, TOKENS])
        zn = s.sb("zn", [P, TILES, SLOT_E])
        g_dram = nc.dram_tensor("g_pieces", (3, TOKENS, SLOT_E * HID), BF16).ap()
        b_dram = nc.dram_tensor("b_pieces", (3, SLOT_E * HID), BF16).ap()
        slot_weights(nc, g, CT, Dn, zn)
        hidden_pieces(nc, g, a["b1"], g_dram, b_dram)
        slot_experts(nc, g, CT, Dn, zn, a["b2_rows"], g_dram, b_dram)


class Globals:
    pass


def route(nc, g, a, rt, xn_dram):
    with Scope(nc, "rte") as s:
        wg = s.sb("wg", [KD, NKD, G1 + EXPERTS])
        bg = s.sb("bg", [P, G1 + EXPERTS])
        tri, ones = s.sb("tri", [P, P]), s.sb("ones", [P, P])
        tie = s.sb("tie", [P, E1, E1])
        tri32 = s.sb("tri32", [P, EXPERTS, EXPERTS])
        steps = s.sb("steps", [P, TILES])
        tile_no = s.sb("tile_no", [1, MOE_TILES])
        lane, tile_lane = s.sb("lane", [P, P]), s.sb("tile_lane", [P, MOE_TILES])
        row_id, spare = s.sb("row_id", [P, TILES * TOPK]), s.sb("spare", [P, 1])
        placei, lanei, tilei = (s.sb(n, [P, TILES * TOPK], U32) for n in ("placei", "lanei", "tilei"))
        lanef, tilef = (s.sb(n, [P, TILES * TOPK]) for n in ("lanef", "tilef"))
        in_lane = s.sb("in_lane", [P, TILES * TOPK, P])
        in_tile = s.sb("in_tile", [P, TILES * TOPK, MOE_TILES])
        rows, free = s.sb("rows", [P, MOE_TILES]), s.sb("free", [P, MOE_TILES])
        lg = s.sb("lg", [P, TILES, G1 + EXPERTS])
        val = [s.sb("val0", [P, TILES, G1]), s.sb("val1", [P, TILES * G1, E1])]
        tmp = [s.sb(f"tmp{i}", [P, TILES * G1, E1 * E1]) for i in range(2)]
        rank = [s.sb("rank0", [P, TILES, G1]), s.sb("rank1", [P, TILES * G1, E1])]
        is0 = [s.sb("is00", [P, TILES, G1]), s.sb("is01", [P, TILES * G1, E1])]
        is1 = [s.sb("is10", [P, TILES, G1]), s.sb("is11", [P, TILES * G1, E1])]
        v0, v1, ev, g0, g1 = ([s.sb(f"{n}0", [P, TILES]), s.sb(f"{n}1", [P, TILES * G1])] for n in ("v0", "v1", "ev", "g0", "g1"))
        share = [s.sb("share0", [P, TILES, G1]), s.sb("share1", [P, TILES * G1, E1])]
        mask = s.sb("mask", [P, TOPK, TILES, EXPERTS])
        comb, sel, pos = (s.sb(n, [P, TILES, EXPERTS]) for n in ("comb", "sel", "pos"))
        cum = s.sb("cum", [P, TILES + 1, EXPERTS])
        cnt, need, base, incl = (s.sb(n, [P, EXPERTS]) for n in ("cnt", "need", "base", "incl"))
        placef = s.sb("placef", [P, TILES, TOPK])
        owner = s.sb("owner", [1, MOE_TILES])
        ps_lg, ps_pos, ps_cnt, ps_row = (s.ps(n, [P, 512]) for n in ("ps_lg", "ps_pos", "ps_cnt", "ps_row"))
        c_in, lg_ready, ones_ready, diff_ready, exp_ready, sel_ready, pos_ready, in_ready, step = (
            s.sem(n) for n in ("c_in", "lg_ready", "ones_ready", "diff_ready", "exp_ready", "sel_ready", "pos_ready",
                               "in_ready", "step"))
        xn_out, row_ready, slot_done = (s.sem(n) for n in ("xn_out", "row_ready", "slot_done"))
        loads = [(wg[:], a["wgate"]), (bg[:], a["bgate_rows"]), (tri[:], a["tri"]),
                 (tie[:].rearrange("p a b -> p (a b)"), a["tie8"]), (tri32[:].rearrange("p a b -> p (a b)"), a["tri32"]),
                 (steps[:], a["steps"]), (tile_no[:], a["tile_no"][0:1, :]),
                 (tile_lane[:], a["tile_no"]), (lane[:], a["lane"]), (row_id[:], a["row_id"]), (spare[:], a["spare"])]
        layernorm(nc, g, "ln3", None, loads, c_in)
        block = s.block()

        @block.sync
        def _(sp):
            sp.dma_start(xn_dram.rearrange("(i p) d -> p i d", p=P), g.xn[:]).then_inc(xn_out, 16)
            sp.wait_ge(xn_out, 16)

        @block.tensor
        def _(pe):
            pe.wait_ge(c_in, 16 * len(loads))
            for i in range(TILES):
                for k in range(NKD):
                    mm = pe.matmul(ps_lg[:, i * 36:(i + 1) * 36], g.xnT[:, k, i * P:(i + 1) * P], wg[:, k, :],
                                   start=(k == 0), stop=(k == NKD - 1))
            mm.then_inc(lg_ready, 1)
            pe.wait_ge(ones_ready, 1)
            pe.wait_ge(sel_ready, 1)
            pe.matmul(ps_pos[:, 0:TILES * EXPERTS], tri[:], sel[:].rearrange("p i e -> p (i e)"), start=True, stop=False)
            pe.matmul(ps_pos[:, 0:TILES * EXPERTS], ones[:], cum[:, 0:TILES, :].rearrange("p i e -> p (i e)"), start=False, stop=True)
            pe.matmul(ps_cnt[:, 0:EXPERTS], ones[:], cum[:, TILES, :], start=True, stop=True).then_inc(pos_ready, 1)
            for n in range(TILES * TOPK):
                if n % (TILES * TOPK // 4) == 0:
                    pe.wait_ge(in_ready, n // (TILES * TOPK // 4) + 1)
                mm = pe.matmul(ps_row[:, 0:MOE_TILES], in_lane[:, n, :], in_tile[:, n, :], start=(n == 0), stop=(n == TILES * TOPK - 1))
            mm.then_inc(row_ready, 1)

        @block.scalar
        def _(act):
            for lv in range(2):
                act.wait_ge(diff_ready, lv + 1)
                act.activation(ev[lv][:], v1[lv][:], ACT.Exp).then_inc(exp_ready, 1)

        @block.vector
        def _(dve):
            c = Chain(dve, step)
            dve.memset(ones[:], 1.0).then_inc(ones_ready, 1)
            dve.wait_ge(c_in, 16 * len(loads))
            dve.wait_ge(lg_ready, 1)
            c.after(dve.tensor_tensor(lg[:], ps_lg[:, 0:TILES * 36].rearrange("p (i n) -> p i n", i=TILES),
                                      bg[:].unsqueeze(1).to_broadcast([P, TILES, 36]), ALU.add))
            c.after(dve.tensor_copy(val[0][:], lg[:, :, 0:G1]))
            c.after(dve.tensor_copy(val[1][:].rearrange("p (i g) e -> p i (g e)", g=G1), lg[:, :, G1:]))
            for lv, (G, E) in enumerate(((TILES, G1), (TILES * G1, E1))):
                v = val[lv][:]
                gt, eq = (tmp[n][:].rearrange("p g e -> p (g e)")[:, 0:G * E * E].rearrange("p (g i j) -> p g i j", g=G, i=E) for n in range(2))
                other = v.unsqueeze(2).to_broadcast([P, G, E, E])
                own = v.unsqueeze(3).to_broadcast([P, G, E, E])
                c.after(dve.tensor_tensor(gt, other, own, ALU.is_gt))
                c.after(dve.tensor_tensor(eq, other, own, ALU.is_equal))
                c.after(dve.tensor_tensor(eq, eq, tie[:, 0:E, 0:E].unsqueeze(1).to_broadcast([P, G, E, E]), ALU.mult))
                c.after(dve.tensor_tensor(gt, gt, eq, ALU.add))
                c.after(dve.tensor_reduce(rank[lv][:], gt, AX.X, ALU.add))
                c.after(dve.tensor_scalar(is0[lv][:], rank[lv][:], 0.0, None, ALU.is_equal))
                c.after(dve.tensor_scalar(is1[lv][:], rank[lv][:], 1.0, None, ALU.is_equal))
                c.after(dve.tensor_reduce(v0[lv][:], v, AX.X, ALU.max))
                c.after(dve.tensor_tensor(share[lv][:], v, is1[lv][:], ALU.mult))
                c.after(dve.tensor_reduce(v1[lv][:], share[lv][:], AX.X, ALU.add))
                dve.tensor_tensor(v1[lv][:], v1[lv][:], v0[lv][:], ALU.subtract).then_inc(diff_ready, 1)
                dve.wait_ge(exp_ready, lv + 1)
                c.after(dve.tensor_scalar(g0[lv][:], ev[lv][:], 1.0, None, ALU.add))
                c.after(dve.reciprocal(g0[lv][:], g0[lv][:]))
                c.after(dve.tensor_tensor(g1[lv][:], ev[lv][:], g0[lv][:], ALU.mult))
                wide = lambda x: x.unsqueeze(2).to_broadcast([P, G, E])
                c.after(dve.tensor_tensor(share[lv][:], is0[lv][:], wide(g0[lv][:]), ALU.mult))
                part = tmp[0][:].rearrange("p g e -> p (g e)")[:, 0:G * E].rearrange("p (g e) -> p g e", g=G)
                c.after(dve.tensor_tensor(part, is1[lv][:], wide(g1[lv][:]), ALU.mult))
                c.after(dve.tensor_tensor(share[lv][:], share[lv][:], part, ALU.add))
            pairs = lambda x: x.rearrange("p i (g e) -> p (i g) e", g=G1)
            outer = lambda x: x.rearrange("p i g -> p (i g)").unsqueeze(2).to_broadcast([P, TILES * G1, E1])
            c.after(dve.tensor_tensor(pairs(comb[:]), share[1][:], outer(share[0][:]), ALU.mult))
            for k in range(TOPK):
                gm, em = (is0, is1)[k // 2][0], (is0, is1)[k % 2][1]
                c.after(dve.tensor_tensor(pairs(mask[:, k]), em[:], outer(gm[:]), ALU.mult))
            c.after(dve.tensor_tensor(sel[:], mask[:, 0], mask[:, 1], ALU.add))
            c.after(dve.tensor_tensor(sel[:], sel[:], mask[:, 2], ALU.add))
            c.after(dve.tensor_tensor(sel[:], sel[:], mask[:, 3], ALU.add))
            c.after(dve.memset(cum[:, 0, :], 0.0))
            for i in range(TILES):
                op = dve.tensor_tensor(cum[:, i + 1, :], cum[:, i, :], sel[:, i, :], ALU.add)
                if i < TILES - 1:
                    c.after(op)
            op.then_inc(sel_ready, 1)

            def pick(dst, x):
                for k in range(TOPK):
                    flat = tmp[k % 2][:].rearrange("p g e -> p (g e)")[:, 0:TILES * EXPERTS].rearrange("p (i e) -> p i e", i=TILES)
                    c.after(dve.tensor_tensor(flat, x, mask[:, k], ALU.mult))
                    c.after(dve.tensor_reduce(dst[:, :, k], flat, AX.X, ALU.add))

            pick(rt.gate, comb[:])
            dve.wait_ge(pos_ready, 1)
            c.after(dve.tensor_copy(cnt[:], ps_cnt[:, 0:EXPERTS]))
            flat = tmp[0][:].rearrange("p g e -> p (g e)")
            over = flat[:, 0:EXPERTS * TILES].rearrange("p (e n) -> p e n", n=TILES)
            c.after(dve.tensor_tensor(over, cnt[:].unsqueeze(2).to_broadcast([P, EXPERTS, TILES]),
                                      steps[:].unsqueeze(1).to_broadcast([P, EXPERTS, TILES]), ALU.is_gt))
            c.after(dve.tensor_reduce(need[:], over, AX.X, ALU.add))
            before = flat[:, 0:EXPERTS * EXPERTS].rearrange("p (a b) -> p a b", a=EXPERTS)
            c.after(dve.tensor_tensor(before, need[:].unsqueeze(1).to_broadcast([P, EXPERTS, EXPERTS]), tri32[:], ALU.mult))
            c.after(dve.tensor_reduce(base[:], before, AX.X, ALU.add))
            c.after(dve.tensor_tensor(incl[:], base[:], need[:], ALU.add))
            c.after(dve.tensor_scalar(base[:], base[:], float(P), None, ALU.mult))
            c.after(dve.tensor_tensor(pos[:], ps_pos[:, 0:TILES * EXPERTS].rearrange("p (i e) -> p i e", i=TILES),
                                      base[:].unsqueeze(1).to_broadcast([P, TILES, EXPERTS]), ALU.add))
            pick(placef, pos[:])
            c.after(dve.tensor_copy(placei[:], placef[:].rearrange("p i k -> p (i k)")))
            c.after(dve.tensor_scalar(lanei[:], placei[:], P - 1, None, ALU.bitwise_and))
            c.after(dve.tensor_scalar(tilei[:], placei[:], LANE_BITS, None, ALU.logical_shift_right))
            c.after(dve.tensor_copy(lanef[:], lanei[:]))
            c.after(dve.tensor_copy(tilef[:], tilei[:]))
            quarter = TILES * TOPK // 4
            for n in range(0, TILES * TOPK, quarter):
                at = slice(n, n + quarter)
                wide = lambda x, m: x[:, at].unsqueeze(2).to_broadcast([P, quarter, m])
                every = lambda x, m: x.unsqueeze(1).to_broadcast([P, quarter, m])
                c.after(dve.tensor_tensor(in_tile[:, at], every(tile_lane[:], MOE_TILES), wide(tilef, MOE_TILES), ALU.is_equal))
                c.after(dve.tensor_tensor(in_tile[:, at], in_tile[:, at], wide(row_id, MOE_TILES), ALU.mult))
                dve.tensor_tensor(in_lane[:, at], every(lane[:], P), wide(lanef, P), ALU.is_equal).then_inc(in_ready, 1)
            ended = flat[0:1, 0:MOE_TILES * EXPERTS].rearrange("p (t e) -> p t e", e=EXPERTS)
            c.after(dve.tensor_tensor(ended, incl[0:1].unsqueeze(1).to_broadcast([1, MOE_TILES, EXPERTS]),
                                      tile_no[:].unsqueeze(2).to_broadcast([1, MOE_TILES, EXPERTS]), ALU.is_le))
            c.after(dve.tensor_reduce(owner[:], ended, AX.X, ALU.add))
            c.after(dve.tensor_scalar(rt.expert[:], owner[:], float(EXPERTS - 1), None, ALU.min))
            dve.wait_ge(row_ready, 1)
            c.after(dve.tensor_scalar(free[:], ps_row[:, 0:MOE_TILES], 0.0, spare[:], ALU.is_equal, ALU.mult))
            c.after(dve.tensor_tensor(rows[:], free[:], ps_row[:, 0:MOE_TILES], ALU.add))
            c.after(dve.tensor_scalar(rt.slot[:, 1, :], rows[:], -1.0, None, ALU.add))
            dve.tensor_scalar(rt.slot[:, 0, :], rt.slot[:, 1, :], TOKENS - 1, None, ALU.bitwise_and).then_inc(slot_done, 1)
            dve.wait_ge(slot_done, 1)


def expert_tiles(nc, g, a, rt, xn_dram, y_dram):
    DEEP = 3
    ROUNDS = MOE_TILES // DEEP
    with Scope(nc, "ext") as s:
        w1 = s.sb("w1", [KD + 1, DEEP, NKD, HID])
        w2 = s.sb("w2", [P, DEEP, HC, D])
        b2 = s.sb("b2", [1, DEEP, D])
        x = s.sb("x", [P, DEEP, D])
        xT = s.sb("xT", [KD + 1, DEEP, NKD, P])
        H = s.sb("H", [P, DEEP, HC, P])
        y = s.sb("y", [P, DEEP, D])
        xi, yi = ([s.sb(f"{n}{i}", [P, 1], U32) for i in range(DEEP)] for n in ("xi", "yi"))
        ones = s.sb("ones", [1, P])
        hp = [s.ps(f"hp{i}", [P, 2, 512]) for i in range(DEEP)]
        xp, yp = s.ps("xp", [P, 512]), s.ps("yp", [P, 512])
        xi_ready, yi_ready, xp_ready, xT_done, hid_ready, gelu_done, y_ready, y_done, consts, turn = (
            s.sem(n) for n in ("xi_ready", "yi_ready", "xp_ready", "xT_done", "hid_ready", "gelu_done", "y_ready",
                               "y_done", "consts", "turn"))
        w1_in, w2_in, x_in, y_out = ([s.sem(f"{n}{i}") for i in range(DEEP)] for n in ("w1_in", "w2_in", "x_in", "y_out"))
        block = s.block()

        def program(eng, tile):
            for p in range(DEEP):
                tile(p, p, 0, True, False)
            with eng.Fori(1, ROUNDS - 1) as r:
                for p in range(DEEP):
                    tile(DEEP * r + p, p, r, False, False)
            for p in range(DEEP):
                tile(DEEP * (ROUNDS - 1) + p, p, ROUNDS - 1, False, True)

        @block.sync
        def _(sp):
            def load(t, p, r, first, last):
                e = sp.value_load(rt.expert[0:1, bass.ds(t, 1)], min_val=0, max_val=EXPERTS - 1)
                if not first:
                    sp.wait_ge(hid_ready, t - DEEP + 1)
                sp.dma_start(w1[0:KD, p], a["W1"][bass.ds(e, 1)].rearrange("o k c n -> (o k) c n")).then_inc(w1_in[p], 16)
                sp.dma_start(w1[KD:KD + 1, p, 1, :], a["B1"][bass.ds(e, 1), :]).then_inc(w1_in[p], 16)
                if not first:
                    sp.wait_ge(y_ready, t - DEEP + 1)
                sp.dma_start(w2[:, p], a["W2"][bass.ds(e, 1)].rearrange("o p c n -> (o p) c n")).then_inc(w2_in[p], 16)
                sp.dma_start(b2[:, p, :], a["B2"][bass.ds(e, 1), :]).then_inc(w2_in[p], 16)

            program(sp, load)

        @block.tensor
        def _(pe):
            pe.wait_ge(consts, 2)

            def transpose_x(t, p, r):
                pe.wait_ge(x_in[p], 16 * r + 16)
                if not isinstance(t, int) or t > 0:
                    pe.wait_ge(xT_done, t)
                for k in range(NKD):
                    tr = pe.transpose(xp[0:KD, k * P:(k + 1) * P], x[:, p, k * KD:(k + 1) * KD], g.ident[:])
                tr.then_inc(xp_ready, 1)

            def up(t, p, r, first):
                pe.wait_ge(w1_in[p], 32 * r + 32)
                pe.wait_ge(xT_done, t + 1)
                if not first:
                    pe.wait_ge(gelu_done, t - DEEP + 1)
                for c in range(HC):
                    for k in range(NKD):
                        rows = KD + k
                        mm = pe.matmul(hp[p][:, c // 3, (c % 3) * P:(c % 3 + 1) * P], w1[0:rows, p, k, c * P:(c + 1) * P],
                                       xT[0:rows, p, k, :], start=(k == 0), stop=(k == NKD - 1))
                mm.then_inc(hid_ready, 1)

            def down(t, p, r):
                pe.wait_ge(w2_in[p], 32 * r + 32)
                pe.wait_ge(gelu_done, t + 1)
                if not isinstance(t, int) or t > 0:
                    pe.wait_ge(y_done, t)
                for c in range(HC):
                    pe.matmul(yp[:, 0:D], H[:, p, c, :], w2[:, p, c, :], start=(c == 0), stop=False)
                pe.matmul(yp[:, 0:D], ones[:], b2[:, p, :], start=False, stop=True).then_inc(y_ready, 1)

            def tile(t, p, r, first, last):
                if first and p == 0:
                    transpose_x(0, 0, 0)
                if not (last and p == DEEP - 1):
                    transpose_x(t + 1, (p + 1) % DEEP, r + (p + 1) // DEEP)
                up(t, p, r, first)
                if not (first and p == 0):
                    down(t - 1, (p - 1) % DEEP, r + (p - 1) // DEEP)

            program(pe, tile)
            down(MOE_TILES - 1, DEEP - 1, ROUNDS - 1)

        @block.scalar
        def _(act):
            def gelu(t, p, r, first, last):
                act.wait_ge(hid_ready, t + 1)
                if not first:
                    act.wait_ge(y_ready, t - DEEP + 1)
                act.activation(H[:, p].rearrange("p (a c) n -> p a (c n)", a=2), hp[p][:, :, 0:3 * P], ACT.Gelu).then_inc(gelu_done, 1)

            program(act, gelu)

        @block.vector
        def _(dve):
            dve.memset(ones[:], 1.0).then_inc(consts, 1)
            dve.memset(xT[KD:KD + 1], 1.0).then_inc(consts, 1)

            def index(n, t, p):
                dve.tensor_copy((xi, yi)[n][p][:], rt.slot[:, n, bass.ds(t, 1)]).then_inc((xi_ready, yi_ready)[n], 1)

            def leave_x(t, p, first):
                dve.wait_ge(xp_ready, t + 1)
                if not first:
                    dve.wait_ge(hid_ready, t - DEEP + 1)
                dve.tensor_copy(xT[0:KD, p], xp[0:KD, 0:2 * P].rearrange("p (k c) -> p k c", k=NKD)).then_inc(xT_done, 1)

            def leave_y(t, p, r, first):
                dve.wait_ge(y_ready, t + 1)
                if not first:
                    dve.wait_ge(y_out[p], 16 * r)
                index(1, t, p)
                dve.tensor_copy(y[:, p, :], yp[:, 0:D]).then_inc(y_done, 1)

            def tile(t, p, r, first, last):
                if first and p == 0:
                    for q in range(DEEP):
                        index(0, q, q)
                    leave_x(0, 0, True)
                if not (last and p == DEEP - 1):
                    leave_x(t + 1, (p + 1) % DEEP, first and p + 1 < DEEP)
                if not last:
                    dve.wait_ge(x_in[p], 16 * r + 16)
                    index(0, t + DEEP, p)
                if not (first and p == 0):
                    leave_y(t - 1, (p - 1) % DEEP, r + (p - 1) // DEEP, first)

            program(dve, tile)
            leave_y(MOE_TILES - 1, DEEP - 1, ROUNDS - 1, False)

        @block.gpsimd
        def _(pool):
            def gather(t, p):
                pool.wait_ge(xi_ready, t + 1)
                pool.sem_inc(turn, 1)
                pool.indirect_dma_start(out=x[:, p, :], out_offset=None, in_=xn_dram,
                                        in_offset=bass.IndirectOffsetOnAxis(ap=xi[p][:], axis=0)).then_inc(x_in[p], 16)

            def scatter(t, p, r, first):
                pool.wait_ge(yi_ready, t + 1)
                pool.wait_ge(y_done, t + 1)
                if not first:
                    pool.wait_ge(y_out[(p - 1) % DEEP], 16 * (r + (p - 1) // DEEP) + 16)
                pool.sem_inc(turn, 1)
                pool.indirect_dma_start(out=y_dram, out_offset=bass.IndirectOffsetOnAxis(ap=yi[p][:], axis=0),
                                        in_=y[:, p, :], in_offset=None).then_inc(y_out[p], 16)

            def tile(t, p, r, first, last):
                if not last:
                    pool.wait_ge(xp_ready, t + 1)
                    gather(t + DEEP, p)
                if not (first and p == 0):
                    scatter(t - 1, (p - 1) % DEEP, r + (p - 1) // DEEP, first and p == 1)

            for q in range(DEEP):
                gather(q, q)
            program(pool, tile)
            scatter(MOE_TILES - 1, DEEP - 1, ROUNDS - 1, False)
            for p in range(DEEP):
                pool.wait_ge(y_out[p], 16 * ROUNDS)
            pool.wait_ge(turn, 2 * MOE_TILES)


def combine(nc, g, rt, y_dram, out):
    with Scope(nc, "cmb") as s:
        rows = s.sb("rows", [P, TILES, TOPK, D])
        row_in = [s.sem(f"row_in{i}") for i in range(TILES)]
        h_step = [s.sem(f"h_step{i}") for i in range(TILES)]
        by_choice = y_dram[0:TOPK * TOKENS].rearrange("(k i p) d -> i p k d", k=TOPK, i=TILES)
        block = s.block()

        def load(eng, i):
            eng.dma_start(rows[:, i], by_choice[i]).then_inc(row_in[i], 16)

        @block.scalar
        def _(act):
            for i in range(1, TILES, 2):
                load(act, i)

        @block.vector
        def _(dve):
            for i in range(0, TILES, 2):
                dve.wait_ge(row_in[i], 16)
                dve.wait_ge(row_in[i + 1], 16)
                for k in range(TOPK):
                    for j in (i, i + 1):
                        if k > 0:
                            dve.wait_ge(h_step[j], k)
                        dve.scalar_tensor_tensor(g.h[:, j, :], rows[:, j, k, :], rt.gate[:, j, k:k + 1], g.h[:, j, :],
                                                 ALU.mult, ALU.add).then_inc(h_step[j], 1)

        @block.sync
        def _(sp):
            for i in range(0, TILES, 2):
                load(sp, i)
            for i in range(TILES):
                sp.wait_ge(h_step[i], TOPK)
                sp.dma_start(out[i * P:(i + 1) * P, :], g.h[:, i, :]).then_inc(g.out_done, 16)
            sp.wait_ge(g.out_done, 16 * TILES)


def routed_moe(nc, g, a, out):
    with Scope(nc, "rmoe") as s:
        rt = Globals()
        rt.gate = s.sb("gate", [P, TILES, TOPK])
        rt.slot = s.sb("slot", [P, 2, MOE_TILES], U32)
        rt.expert = s.sb("expert", [1, MOE_TILES], I32)
        xn_dram = nc.dram_tensor("xn", (TOKENS, D), F32).ap()
        y_dram = nc.dram_tensor("y_by_choice", (TOPK * TOKENS + P, D), F32).ap()
        route(nc, g, a, rt, xn_dram)
        expert_tiles(nc, g, a, rt, xn_dram, y_dram)
        combine(nc, g, rt, y_dram, out)


def build(nc, a, out, upto=99, dump=None):
    Scope.ended = []
    with Scope(nc, "vit") as s:
        g = Globals()
        g.h = s.sb("h", [P, TILES, D])
        g.xn = s.sb("xn", [P, TILES, D])
        g.xnT = s.sb("xnT", [KD, NKD, TOKENS])
        g.ident = s.sb("ident", [P, P])
        g.phi = s.sb("phi", [KD, NKD, ALL_SLOTS])
        g.w1 = s.sb("w1", [KD, NKD, SLOT_E * HID])
        g.w2 = s.sb("w2", [P, SLOT_E * HC, D])
        g.d_phi, g.d_w1, g.d_w2, g.d_ident = a["phi"], a["w1"], a["w2"], a["ident"]
        g.phi_in, g.w1_in, g.w2_in, g.ident_in, g.out_done = (nc.alloc_semaphore(n) for n in ("phi_in", "w1_in", "w2_in", "ident_in", "out_done"))
        embed(nc, g, a["xT"], a["tokW"], a["pos_rows"], a["tok_b_rows"])
        if upto >= 1:
            attention0(nc, g, a)
        if upto >= 2 and upto != 30:
            layernorm(nc, g, "ln1")
            soft_moe(nc, g, a)
        if upto >= 3:
            Scope.retire(nc)
            attention1(nc, g, a)
        if upto >= 4:
            routed_moe(nc, g, a, out)
            return
        block = s.block()

        @block.sync
        def _(sp):
            sp.dma_start(out.rearrange("(i p) d -> p i d", p=P), g.h[:]).then_inc(g.out_done, 16)
            sp.wait_ge(g.out_done, 16)
            for sem in (g.phi_in, g.w1_in, g.w2_in, g.ident_in):
                sp.wait_ge(sem, 16)


def layouts(x, L0_tok_W, L0_tok_b, L0_tok_pos_emb, L0_attn_W_qkv, L0_attn_b_qkv, L0_ffn_phi, L0_ffn_w1, L0_ffn_b1,
            L0_ffn_w2, L0_ffn_b2, L1_attn_qA, L1_attn_qB, L1_attn_kA, L1_attn_kB, L1_attn_vA, L1_attn_vB, L1_attn_o_w,
            L1_ffn_Wg, L1_ffn_bg, L1_ffn_Wge, L1_ffn_bge, L1_ffn_W1, L1_ffn_b1, L1_ffn_W2, L1_ffn_b2):
    c = np.ascontiguousarray
    kd = lambda w: c(np.asarray(w).reshape(NKD, KD, -1).transpose(1, 0, 2))
    rows = lambda v: c(np.broadcast_to(np.asarray(v).reshape(1, -1), (P, np.asarray(v).size)))
    x = np.asarray(x)
    patches = x.reshape(IMAGES, 4, 16, 4, 16, 3).transpose(0, 1, 3, 2, 4, 5).reshape(TOKENS, 768)
    a = {}
    a["xT"] = c(patches.T.reshape(PATCH_CHUNKS, P, TOKENS).transpose(1, 0, 2))
    a["tokW"] = c(np.asarray(L0_tok_W).reshape(PATCH_CHUNKS, P, D).transpose(1, 0, 2))
    a["pos_rows"] = c(np.tile(np.asarray(L0_tok_pos_emb), (TILE_IMAGES, 1)))
    a["tok_b_rows"] = rows(L0_tok_b)
    a["ident"] = np.eye(P, dtype=np.float32)
    a["wqkv"] = kd(L0_attn_W_qkv)
    bq = np.asarray(L0_attn_b_qkv)
    a["bqk"] = c(bq[0:2 * D].reshape(4, KD).T)
    a["bv_rows"] = rows(bq[2 * D:])
    p = np.arange(KD)
    a["head_mask0"] = (p[:, None] // 16 == np.arange(6)[None, :]).astype(np.float32)
    a["head_mask1"] = (p[:, None] // 32 == np.arange(3)[None, :]).astype(np.float32)
    q = np.arange(P)
    a["mask_q"] = c(np.tile(np.concatenate([
        (q[None, :] // PATCHES == np.arange(8)[:, None]), (q[None, :] % PATCHES == np.arange(16)[:, None])
    ]).astype(np.float32), (1, TILES)))
    mk = np.concatenate([(q[None, :] // PATCHES != np.arange(8)[:, None]),
                         (q[None, :] % PATCHES > np.arange(16)[:, None])]).astype(np.float32) * np.float32(-BIG)
    a["mask_k"] = c(np.broadcast_to(mk[:, None, :], (24, 6, P)))
    a["phi"] = kd(np.asarray(L0_ffn_phi).reshape(ALL_SLOTS, D).T)
    a["w1"] = kd(np.asarray(L0_ffn_w1).transpose(1, 0, 2).reshape(D, SLOT_E * HID))
    a["b1"] = c(np.asarray(L0_ffn_b1).reshape(P, SLOT_E * HID // P))
    a["w2"] = c(np.asarray(L0_ffn_w2).reshape(SLOT_E * HC, P, D).transpose(1, 0, 2))
    a["b2_rows"] = rows(L0_ffn_b2)
    for n, A, B in (("q", L1_attn_qA, L1_attn_qB), ("k", L1_attn_kA, L1_attn_kB), ("v", L1_attn_vA, L1_attn_vB)):
        a[n + "A"] = kd(A)
        a[n + "B"] = c(np.asarray(B))
    a["o_w"] = kd(L1_attn_o_w)
    hd = 32
    inv = np.float32(1.0) / np.float32(10000.0) ** (np.arange(0, hd, 2, dtype=np.float32) / np.float32(hd))
    fr = np.outer(np.arange(PATCHES, dtype=np.float32), inv).astype(np.float32)
    emb = np.concatenate([fr, fr], -1)
    table = lambda f: c(np.tile(f(emb).astype(np.float32).T, (3, 512 // PATCHES)))
    a["cosT"], a["sinT"] = table(np.cos), table(np.sin)
    a["wgate"] = kd(np.concatenate([np.asarray(L1_ffn_Wg), np.asarray(L1_ffn_Wge).transpose(1, 0, 2).reshape(D, EXPERTS)], 1))
    a["bgate_rows"] = rows(np.concatenate([np.asarray(L1_ffn_bg), np.asarray(L1_ffn_bge).reshape(-1)]))
    a["W1"] = c(np.asarray(L1_ffn_W1).reshape(EXPERTS, NKD, KD, HID).transpose(0, 2, 1, 3))
    a["B1"] = c(np.asarray(L1_ffn_b1))
    a["W2"] = c(np.asarray(L1_ffn_W2).reshape(EXPERTS, HC, P, D).transpose(0, 2, 1, 3))
    a["B2"] = c(np.asarray(L1_ffn_b2))
    a["tri"] = (np.arange(P)[:, None] < np.arange(P)[None, :]).astype(np.float32)
    e = np.arange(E1)
    a["tie8"] = c(np.broadcast_to((e[None, :] < e[:, None]).astype(np.float32).reshape(1, -1), (P, 64)))
    e = np.arange(EXPERTS)
    a["tri32"] = c(np.broadcast_to((e[None, :] < e[:, None]).astype(np.float32).reshape(1, -1), (P, 1024)))
    a["steps"] = rows((np.arange(8) * P).astype(np.float32))
    a["tile_no"] = rows(np.arange(MOE_TILES).astype(np.float32))
    a["lane"] = rows(np.arange(P).astype(np.float32))
    t = np.arange(P)[:, None, None] + P * np.arange(TILES)[None, :, None] + TOKENS * np.arange(TOPK)[None, None, :]
    a["row_id"] = c((t + 1).astype(np.float32).reshape(P, TILES * TOPK))
    a["spare"] = (TOPK * TOKENS + 1 + np.arange(P, dtype=np.float32))[:, None]
    return a


def kernel(**inputs):
    import concourse.bacc as bacc
    from concourse.bass_utils import run_bass_kernel_spmd

    nc = bacc.Bacc("TRN2", target_bir_lowering=False, num_devices=1)
    arrays = layouts(**inputs)
    args = {n: nc.dram_tensor(n, v.shape, mybir.dt.from_np(v.dtype), kind="ExternalInput").ap() for n, v in arrays.items()}
    out = nc.dram_tensor("out", (TOKENS, D), F32, kind="ExternalOutput").ap()
    build(nc, args, out)
    r = run_bass_kernel_spmd(nc, [arrays], core_ids=[0])
    return r.results[0]["out"].reshape(IMAGES, PATCHES, D)
```

```python
import numpy as np

import concourse.bass as bass
from concourse import mybir
from contextlib import ExitStack

F32 = mybir.dt.float32
BF16 = mybir.dt.bfloat16
U32 = mybir.dt.uint32
I32 = mybir.dt.int32
ACT = mybir.ActivationFunctionType
ALU = mybir.AluOpType
AX = mybir.AxisListType

P = 128
IMAGES, PATCHES, D = 64, 16, 192
TOKENS = IMAGES * PATCHES
TILES = TOKENS // P
TILE_IMAGES = P // PATCHES
KD, NKD = 96, 2
PATCH_CHUNKS = 768 // P
EPS = 1e-5
BIG = float(2.0 ** 100)
SLOT_E, SLOTS, HID = 4, 256, 768
ALL_SLOTS = SLOT_E * SLOTS
SLOT_CHUNKS = ALL_SLOTS // P
HC = HID // P
HALF = HID // 2
PAIRS = ((0, 0), (0, 1), (0, 2), (1, 0), (1, 1), (2, 0))
PROWS = len(PAIRS) * PATCHES
BROWS = PROWS + 3
G1, E1 = 4, 8
EXPERTS = G1 * E1
TOPK = 4
MOE_TILES = (TOPK * TOKENS + EXPERTS * (P - 1)) // P
LANE_BITS = 7


class Chain:

    def __init__(self, eng, sem, base=0, turn=None):
        self.eng, self.sem, self.base, self.n, self.turn = eng, sem, base, 0, turn

    def after(self, ins):
        self.n += 1
        ins.then_inc(self.sem, 1)
        self.eng.wait_ge(self.sem, self.base + self.n)
        if self.turn is not None:
            self.eng.sem_inc(self.turn, 1)


class Scope(ExitStack):

    ended = []

    def __init__(self, nc, stage):
        super().__init__()
        self.nc, self.stage = nc, stage

    def sb(self, name, shape, dt=F32):
        return self.enter_context(self.nc.sbuf_tensor(f"{self.stage}_{name}", shape, dt))

    def ps(self, name, shape, dt=F32):
        return self.enter_context(self.nc.psum_tensor(f"{self.stage}_{name}", shape, dt))

    def sem(self, name):
        sem = self.nc.alloc_semaphore(f"{self.stage}_{name}")
        Scope.ended.append(sem)
        return sem

    @staticmethod
    def retire(nc):
        nc.clear_and_free_semaphores(Scope.ended)
        nc.all_engine_barrier()
        Scope.ended = []

    def block(self):
        return self.enter_context(self.nc.Block())


def keep_busy(pe, g, bank, products):
    for _ in range(products):
        pe.matmul(bank[:, 0:P], g.ident[:], g.ident[:], start=True, stop=True)


def embed(nc, g, xT, tokW, pos_rows, tok_b_rows):
    with Scope(nc, "emb") as s:
        x_sb = s.sb("x", [P, PATCH_CHUNKS, TOKENS])
        w_sb = s.sb("w", [P, PATCH_CHUNKS, D])
        pos = s.sb("pos", [P, D])
        tokb = s.sb("tokb", [P, D])
        acc = [s.ps(f"acc{i}", [P, 512]) for i in range(TILES)]
        w_in = [s.sem(f"w_in{j}") for j in range(PATCH_CHUNKS)]
        rows_in, bias_ready, acc_ready, h_done = (s.sem(n) for n in ("rows_in", "bias_ready", "acc_ready", "h_done"))
        block = s.block()

        @block.sync
        def _(sp):
            for j in range(PATCH_CHUNKS):
                sp.dma_start(w_sb[:, j, :], tokW[:, j, :]).then_inc(w_in[j], 16)
                sp.dma_start(x_sb[:, j, :], xT[:, j, :]).then_inc(w_in[j], 16)
            sp.dma_start(g.phi[:], g.d_phi).then_inc(g.phi_in, 16)
            sp.dma_start(g.w1[:], g.d_w1).then_inc(g.w1_in, 16)
            sp.dma_start(g.w2[:], g.d_w2).then_inc(g.w2_in, 16)

        @block.scalar
        def _(act):
            act.dma_start(g.ident[:], g.d_ident).then_inc(g.ident_in, 16)
            act.dma_start(pos[:], pos_rows).then_inc(rows_in, 16)
            act.dma_start(tokb[:], tok_b_rows).then_inc(rows_in, 16)

        @block.tensor
        def _(pe):
            pe.wait_ge(g.ident_in, 16)
            keep_busy(pe, g, acc[-1], 6)
            for j in range(PATCH_CHUNKS):
                pe.wait_ge(w_in[j], 32)
                for i in range(TILES):
                    mm = pe.matmul(acc[i][:, 0:D], x_sb[:, j, i * P:(i + 1) * P], w_sb[:, j, :],
                                   start=(j == 0), stop=(j == PATCH_CHUNKS - 1))
                    if j == PATCH_CHUNKS - 1:
                        mm.then_inc(acc_ready, 1)

        @block.vector
        def _(dve):
            dve.wait_ge(rows_in, 32)
            dve.tensor_tensor(pos[:], pos[:], tokb[:], ALU.add).then_inc(bias_ready, 1)
            dve.wait_ge(bias_ready, 1)
            for i in range(TILES):
                dve.wait_ge(acc_ready, i + 1)
                dve.tensor_tensor(g.h[:, i, :], acc[i][:, 0:D], pos[:], ALU.add).then_inc(h_done, 1)
            dve.wait_ge(h_done, TILES)


def layernorm(nc, g, stage, banks=None, loads=(), loaded=None):
    with Scope(nc, stage) as s:
        stats = s.sb("stats", [P, TILES, 6])
        mv = s.sb("mv", [P, TILES, 2])
        ve, sd, r, t, nmr = (s.sb(n, [P, TILES]) for n in ("ve", "sd", "r", "t", "nmr"))
        psT = banks or [s.ps(f"psT{i}", [P, 512]) for i in range(TILES // 2)]
        stats_ready, mv_ready, step, var_ready, sd_ready, xn_ready, t_ready, xnT_done = (
            s.sem(n) for n in ("stats_ready", "mv_ready", "step", "var_ready", "sd_ready", "xn_ready", "t_ready", "xnT_done"))
        block = s.block()

        @block.sync
        def _(sp):
            for dst, src in loads:
                sp.dma_start(dst, src).then_inc(loaded, 16)

        @block.vector
        def _(dve):
            c = Chain(dve, step)
            for i in range(TILES):
                dve.bn_stats(stats[:, i, :], g.h[:, i, :]).then_inc(stats_ready, 1)
            for i in range(TILES):
                dve.wait_ge(stats_ready, i + 1)
                dve.bn_aggr(mv[:, i, :], stats[:, i, :]).then_inc(mv_ready, 1)
            dve.wait_ge(mv_ready, TILES)
            dve.tensor_scalar(ve[:], mv[:, :, 1], EPS, None, ALU.add).then_inc(var_ready, 1)
            dve.wait_ge(sd_ready, 1)
            c.after(dve.reciprocal(r[:], sd[:]))
            c.after(dve.tensor_tensor(t[:], r[:], r[:], ALU.mult))
            c.after(dve.tensor_tensor(t[:], t[:], ve[:], ALU.mult))
            c.after(dve.tensor_scalar(t[:], t[:], -0.5, 1.5, ALU.mult, ALU.add))
            c.after(dve.tensor_tensor(r[:], r[:], t[:], ALU.mult))
            c.after(dve.scalar_tensor_tensor(nmr[:], mv[:, :, 0], -1.0, r[:], ALU.mult, ALU.mult))
            for i in range(TILES):
                dve.tensor_scalar(g.xn[:, i, :], g.h[:, i, :], r[:, i:i + 1], nmr[:, i:i + 1],
                                  ALU.mult, ALU.add).then_inc(xn_ready, 1)

        @block.tensor
        def _(pe):
            pe.wait_ge(g.ident_in, 16)
            keep_busy(pe, g, psT[-1], 16)
            for i in range(TILES):
                pe.wait_ge(xn_ready, i + 1)
                for k in range(NKD):
                    at = (i % 2 * NKD + k) * P
                    tr = pe.transpose(psT[i // 2][0:KD, at:at + P], g.xn[:, i, k * KD:(k + 1) * KD], g.ident[:])
                tr.then_inc(t_ready, 1)

        @block.scalar
        def _(act):
            act.wait_ge(var_ready, 1)
            act.activation(sd[:], ve[:], ACT.Sqrt).then_inc(sd_ready, 1)
            for j in range(TILES // 2):
                act.wait_ge(t_ready, 2 * j + 2)
                for k in range(NKD):
                    src = psT[j][0:KD, :].rearrange("p (i k c) -> p i k c", i=2, k=NKD)[:, :, k, :]
                    dst = g.xnT[:, k, 2 * j * P:(2 * j + 2) * P].rearrange("p (i c) -> p i c", i=2)
                    act.activation(dst, src, ACT.Copy).then_inc(xnT_done, 1)


HEADS_U = 6
KEYS_DEEP = 3


class Attend:

    def __init__(self, s, g, units, scale, rows, heads_per_group):
        self.s, self.g, self.units, self.scale = s, g, units, scale
        self.qT = s.sb("qT", [rows, 2, TOKENS])
        self.kT = s.sb("kT", [KD, 2, TOKENS])
        self.kTm = s.sb("kTm", [rows, KEYS_DEEP, HEADS_U, P])
        self.hm = s.sb("hm", [KD, heads_per_group])
        self.v = s.sb("v", [P, TILES, D])
        self.nmax, self.rsum, self.rinv = (s.sb(n, [P, 2, HEADS_U]) for n in ("nmax", "rsum", "rinv"))
        self.prob = s.sb("prob", [P, 2, HEADS_U, P])
        self.probT = s.sb("probT", [P, 2, HEADS_U, P])
        self.sc = [s.ps(f"sc{i}", [P, 2, 512]) for i in range(2)]
        self.pt = [s.ps(f"pt{i}", [P, 512]) for i in range(2)]
        self.av = [s.ps(f"av{i}", [P, 512]) for i in range(2)]
        (self.km_pool, self.km_dve, self.sc_ready, self.max_raw, self.max_ready, self.exp_done, self.rinv_ready,
         self.pt_ready, self.ptc_act, self.ptc_dve, self.av_ready, self.av_done) = (
            s.sem(n) for n in ("km_pool", "km_dve", "sc_ready", "max_raw", "max_ready", "exp_done", "rinv_ready",
                               "pt_ready", "ptc_act", "ptc_dve", "av_ready", "av_done"))

    def scores(self, pe, u, operands):
        pe.wait_ge(self.km_pool, u + 1)
        pe.wait_ge(self.km_dve, u + 1)
        if u >= 2:
            pe.wait_ge(self.exp_done, HEADS_U * (u - 1))
        for b in range(2):
            q, k = operands(u, b)
            mm = pe.matmul(self.sc[u % 2][:, b, 0:3 * P], q, k, start=True, stop=True)
        mm.then_inc(self.sc_ready, 1)

    def transposes(self, pe, u):
        if u >= 1:
            pe.wait_ge(self.ptc_act, u)
            pe.wait_ge(self.ptc_dve, u)
        for hd in range(HEADS_U):
            tr = pe.transpose(self.pt[hd // 4][:, (hd % 4) * P:(hd % 4 + 1) * P], self.prob[:, u % 2, hd, :], self.g.ident[:])
        tr.then_inc(self.pt_ready, 1)

    def wait_values(self, pe, u):
        pe.wait_ge(self.ptc_act, u + 1)
        pe.wait_ge(self.ptc_dve, u + 1)
        if u >= 2:
            pe.wait_ge(self.av_done, u - 1)

    def exps(self, act, u, heads):
        if heads[0] == 0:
            act.wait_ge(self.max_ready, u + 1)
            if u >= 2:
                act.wait_ge(self.pt_ready, u - 1)
                act.wait_ge(self.rinv_ready, u - 1)
        for hd in heads:
            act.activation(self.prob[:, u % 2, hd, :], self.sc[u % 2][:, hd // 3, (hd % 3) * P:(hd % 3 + 1) * P], ACT.Exp,
                           bias=self.nmax[:, u % 2, hd:hd + 1], scale=self.scale,
                           accum_out=self.rsum[:, u % 2, hd:hd + 1]).then_inc(self.exp_done, 1)

    def leave_act(self, act, u):
        act.wait_ge(self.pt_ready, u + 1)
        if u >= 2:
            act.wait_ge(self.av_ready, u - 1)
        act.activation(self.probT[:, u % 2, 0:4, :], self.pt[0][:].rearrange("p (h c) -> p h c", h=4), ACT.Copy
                       ).then_inc(self.ptc_act, 1)

    def leave_dve(self, dve, u):
        dve.wait_ge(self.pt_ready, u + 1)
        if u >= 2:
            dve.wait_ge(self.av_ready, u - 1)
        dve.tensor_copy(self.probT[:, u % 2, 4:6, :], self.pt[1][:, 0:2 * P].rearrange("p (h c) -> p h c", h=2)
                        ).then_inc(self.ptc_dve, 1)

    def maximum(self, dve, u):
        dve.wait_ge(self.sc_ready, u + 1)
        if u >= 2:
            dve.wait_ge(self.exp_done, HEADS_U * (u - 1))
        b = u % 2
        dve.tensor_reduce(self.nmax[:, b, :].rearrange("p (a h) -> p a h", a=2),
                          self.sc[b][:, :, 0:3 * P].rearrange("p a (h c) -> p a h c", h=3), AX.X, ALU.max, negate=True
                          ).then_inc(self.max_raw, 1)
        dve.wait_ge(self.max_raw, u + 1)
        dve.tensor_scalar(self.nmax[:, b, :], self.nmax[:, b, :], self.scale, None, ALU.mult).then_inc(self.max_ready, 1)

    def inverse(self, dve, u):
        dve.wait_ge(self.exp_done, HEADS_U * (u + 1))
        dve.reciprocal(self.rinv[:, u % 2, :], self.rsum[:, u % 2, :]).then_inc(self.rinv_ready, 1)
        dve.wait_ge(self.rinv_ready, u + 1)


def attention0(nc, g, a):
    DH, GH = 16, 6
    KM = KD + TILE_IMAGES
    UNITS = 2 * TILES
    with Scope(nc, "at0") as s:
        w = s.sb("w", [KD, NKD, 3 * D])
        bias = s.sb("bias", [KD, 4])
        bv = s.sb("bv", [P, D])
        o = s.sb("o", [P, 2, D // 2])
        t = Attend(s, g, UNITS, 1.0, KM, GH)
        w_in, qk_ready, qk_done, v_ready, v_done, step = (
            s.sem(n) for n in ("w_in", "qk_ready", "qk_done", "v_ready", "v_done", "step"))
        banks = [t.sc[0][:, 0], t.sc[0][:, 1], t.sc[1][:, 0], t.sc[1][:, 1], t.pt[0][:], t.pt[1][:], t.av[0][:], t.av[1][:]]
        loads = [(w[:], a["wqkv"]), (bias[:], a["bqk"]), (bv[:], a["bv_rows"]), (t.hm[:], a["head_mask0"])]
        loads += [(t.qT[KD:KM, b, :], a["mask_q"][0:TILE_IMAGES]) for b in range(2)]
        loads += [(t.kTm[KD:KM, b, :, :], a["mask_k"][0:TILE_IMAGES]) for b in range(KEYS_DEEP)]
        layernorm(nc, g, "ln0", banks[0:4], loads, w_in)
        block = s.block()

        def keys(eng, u, heads, sem):
            i, grp = u // 2, u % 2
            if u >= KEYS_DEEP:
                eng.wait_ge(t.sc_ready, u - KEYS_DEEP + 1)
            for hd in heads:
                op = eng.tensor_scalar(t.kTm[0:KD, u % KEYS_DEEP, hd, :], t.kT[:, grp, i * P:(i + 1) * P],
                                       t.hm[:, hd:hd + 1], None, ALU.mult)
            op.then_inc(sem, 1)

        @block.tensor
        def _(pe):
            pe.wait_ge(w_in, 16 * len(loads))
            for n in range(8):
                part, half = n // 2, n % 2
                for k in range(NKD):
                    mm = pe.matmul(banks[n][0:KD, :], w[:, k, part * KD:(part + 1) * KD],
                                   g.xnT[:, k, half * 512:(half + 1) * 512], start=(k == 0), stop=(k == NKD - 1))
                mm.then_inc(qk_ready, 1)
            for i in range(TILES):
                pe.wait_ge(qk_done, i + 1)
                for k in range(NKD):
                    mm = pe.matmul(banks[i][:, 0:D], g.xnT[:, k, i * P:(i + 1) * P], w[:, k, 2 * D:3 * D],
                                   start=(k == 0), stop=(k == NKD - 1))
                mm.then_inc(v_ready, 1)

            def operands(u, b):
                i, grp = u // 2, u % 2
                return t.qT[:, grp, i * P:(i + 1) * P], t.kTm[:, u % KEYS_DEEP, 3 * b:3 * b + 3, :]

            def values(u):
                i, grp = u // 2, u % 2
                t.wait_values(pe, u)
                for hd in range(GH):
                    at = (grp * GH + hd) * DH
                    mm = pe.matmul(t.av[u % 2][:, hd * DH:(hd + 1) * DH], t.probT[:, u % 2, hd, :], t.v[:, i, at:at + DH],
                                   start=True, stop=True)
                mm.then_inc(t.av_ready, 1)

            pe.wait_ge(v_done, TILES)
            t.scores(pe, 0, operands)
            t.scores(pe, 1, operands)
            for u in range(UNITS):
                pe.wait_ge(t.exp_done, HEADS_U * (u + 1))
                t.transposes(pe, u)
                if u + 2 < UNITS:
                    t.scores(pe, u + 2, operands)
                if u >= 1:
                    values(u - 1)
            values(UNITS - 1)

        @block.scalar
        def _(act):
            act.wait_ge(w_in, 16 * len(loads))
            for n in range(8):
                part, half = n // 2, n % 2
                act.wait_ge(qk_ready, n + 1)
                dst = (t.qT[0:KD] if part < 2 else t.kT[:])[:, part % 2, half * 512:(half + 1) * 512]
                act.activation(dst, banks[n][0:KD, :], ACT.Identity, bias=bias[:, part:part + 1]).then_inc(qk_done, 1)
            t.exps(act, 0, range(HEADS_U))
            for u in range(UNITS):
                if u + 1 < UNITS:
                    t.exps(act, u + 1, range(HEADS_U // 2))
                t.leave_act(act, u)
                if u + 1 < UNITS:
                    t.exps(act, u + 1, range(HEADS_U // 2, HEADS_U))

        @block.gpsimd
        def _(pool):
            pool.wait_ge(qk_done, 8)
            pool.wait_ge(w_in, 16 * len(loads))
            for u in range(UNITS):
                keys(pool, u, range(GH // 2), t.km_pool)

        @block.vector
        def _(dve):
            c = Chain(dve, step)
            dve.wait_ge(w_in, 16 * len(loads))
            for i in range(TILES):
                dve.wait_ge(v_ready, i + 1)
                dve.tensor_tensor(t.v[:, i, :], banks[i][:, 0:D], bv[:], ALU.add).then_inc(v_done, 1)
                if i % 2 == 1 and i // 2 < KEYS_DEEP:
                    dve.wait_ge(qk_done, 8)
                    keys(dve, i // 2, range(GH // 2, GH), t.km_dve)

            def finish(u):
                i, grp = u // 2, u % 2
                hs = g.h[:, i, grp * 96:(grp + 1) * 96]
                dve.wait_ge(t.av_ready, u + 1)
                dve.tensor_tensor(o[:, u % 2, :].rearrange("p (h d) -> p h d", h=GH),
                                  t.av[u % 2][:, 0:GH * DH].rearrange("p (h d) -> p h d", h=GH),
                                  t.rinv[:, u % 2, :].unsqueeze(2).to_broadcast([P, GH, DH]), ALU.mult).then_inc(t.av_done, 1)
                dve.wait_ge(t.av_done, u + 1)
                c.after(dve.tensor_tensor(hs, hs, o[:, u % 2, :], ALU.add))

            t.maximum(dve, 0)
            t.maximum(dve, 1)
            for u in range(UNITS):
                if u + KEYS_DEEP < UNITS:
                    keys(dve, u + KEYS_DEEP, range(GH // 2, GH), t.km_dve)
                t.inverse(dve, u)
                t.leave_dve(dve, u)
                if u + 2 < UNITS:
                    t.maximum(dve, u + 2)
                if u >= 1:
                    finish(u - 1)
            finish(UNITS - 1)


def attention1(nc, g, a):
    DH, GH, RANK = 32, 3, 48
    QK_RANK = 64 + RANK
    KM = KD + TILE_IMAGES + PATCHES
    UNITS = TILES
    with Scope(nc, "at1") as s:
        wa, wva = s.sb("wa", [KD, NKD, QK_RANK]), s.sb("wva", [KD, NKD, RANK])
        wb, wvb = s.sb("wb", [QK_RANK, 2, D]), s.sb("wvb", [RANK, D])
        wr = s.sb("wr", [QK_RANK, 2, D])
        ow = s.sb("ow", [KD, NKD, D])
        low, low_v = s.sb("low", [QK_RANK, TOKENS]), s.sb("low_v", [RANK, TOKENS])
        cosT, sinT = (s.sb(n, [KD, 512]) for n in ("cosT", "sinT"))
        rope = s.sb("rope", [KD, 2, 2, 512])
        oT = s.sb("oT", [KD, 2, 2, P])
        t = Attend(s, g, UNITS, 1.0 / float(np.sqrt(DH)), KM, GH)
        w_in, rot_ready, low_ready, low_done, qk_ready, cs_done, rope_done, v_ready, v_done, oT_ready, o_ready, prob_ready, step = (
            s.sem(n) for n in ("w_in", "rot_ready", "low_ready", "low_done", "qk_ready", "cs_done", "rope_done", "v_ready",
                               "v_done", "oT_ready", "o_ready", "prob_ready", "step"))
        banks = [t.sc[0][:, 0], t.sc[0][:, 1], t.sc[1][:, 0], t.sc[1][:, 1], t.pt[0][:], t.pt[1][:], t.av[0][:], t.av[1][:]]
        loads = [(ow[:], a["o_w"]), (t.hm[:], a["head_mask1"]), (cosT[:], a["cosT"]), (sinT[:], a["sinT"])]
        loads += [(wa[:], a["qkA"]), (wb[:], a["qkB"]), (wva[:], a["vA"]), (wvb[:], a["vB"])]
        loads += [(t.qT[KD:KM, b, :], a["mask_q"]) for b in range(2)]
        loads += [(t.kTm[KD:KM, b, :, :], a["mask_k"]) for b in range(KEYS_DEEP)]
        layernorm(nc, g, "ln2", banks[0:4], loads, w_in)
        block = s.block()

        def keys(eng, u, heads, sem):
            if u >= KEYS_DEEP:
                eng.wait_ge(t.sc_ready, u - KEYS_DEEP + 1)
            for j in heads:
                op = eng.tensor_scalar(t.kTm[0:KD, u % KEYS_DEEP].rearrange("p (g h) c -> p g h c", g=2)[:, :, j, :],
                                       t.kT[:, :, u * P:(u + 1) * P], t.hm[:, j:j + 1], None, ALU.mult)
            op.then_inc(sem, 1)

        parts = [(x, grp, half) for x in range(2) for grp in range(2) for half in range(2)]

        @block.tensor
        def _(pe):
            pe.wait_ge(w_in, 16 * len(loads))
            for n in range(4):
                first, half = (wa, wva)[n // 2], n % 2
                for k in range(NKD):
                    mm = pe.matmul(banks[n][0:first.shape[2], :], first[:, k, :], g.xnT[:, k, half * 512:(half + 1) * 512],
                                   start=(k == 0), stop=(k == NKD - 1))
                mm.then_inc(low_ready, 1)
            pe.wait_ge(rot_ready, 4)
            for n, (x, grp, half) in enumerate(parts):
                pe.wait_ge(low_done, min(2 * n + 2, 4))
                if n >= 4:
                    pe.wait_ge(cs_done, 2 * (n - 3))
                for r, m in enumerate((wb, wr)):
                    mm = pe.matmul(banks[2 * (n % 4) + r][0:KD, :], m[:, x, grp * KD:(grp + 1) * KD],
                                   low[:, half * 512:(half + 1) * 512], start=True, stop=True)
                mm.then_inc(qk_ready, 1)
            for i in range(TILES):
                pe.wait_ge(cs_done, 2 * (5 + i // 2))
                pe.matmul(banks[i][:, 0:D], low_v[:, i * P:(i + 1) * P], wvb[:], start=True, stop=True).then_inc(v_ready, 1)

            def operands(u, b):
                return t.qT[:, b, u * P:(u + 1) * P], t.kTm[:, u % KEYS_DEEP, 3 * b:3 * b + 3, :]

            def values(u):
                t.wait_values(pe, u)
                for hd in range(HEADS_U):
                    grp, j = hd // GH, hd % GH
                    mm = pe.matmul(t.av[u % 2][j * DH:(j + 1) * DH, grp * P:(grp + 1) * P], t.v[:, u, hd * DH:(hd + 1) * DH],
                                   t.probT[:, u % 2, hd, :], start=True, stop=True)
                mm.then_inc(t.av_ready, 1)

            def project(u):
                pe.wait_ge(oT_ready, u + 1)
                for k in range(NKD):
                    mm = pe.matmul(t.av[u % 2][:, 256:256 + D], oT[:, u % 2, k, :], ow[:, k, :],
                                   start=(k == 0), stop=(k == NKD - 1))
                mm.then_inc(o_ready, 1)

            pe.wait_ge(v_done, TILES)
            t.scores(pe, 0, operands)
            t.scores(pe, 1, operands)
            for u in range(UNITS):
                if u + 2 < UNITS:
                    t.scores(pe, u + 2, operands)
                pe.wait_ge(prob_ready, u + 1)
                t.transposes(pe, u)
                if u >= 2:
                    project(u - 2)
                if u >= 1:
                    values(u - 1)
            project(UNITS - 2)
            values(UNITS - 1)
            project(UNITS - 1)

        @block.scalar
        def _(act):
            for n in range(4):
                dst, half = (low, low_v)[n // 2], n % 2
                act.wait_ge(low_ready, n + 1)
                act.activation(dst[:, half * 512:(half + 1) * 512], banks[n][0:dst.shape[0], :], ACT.Copy).then_inc(low_done, 1)

            for i in range(TILES):
                act.wait_ge(v_ready, i + 1)
                act.activation(t.v[:, i, :], banks[i][:, 0:D], ACT.Copy).then_inc(v_done, 1)

            def leave_values(u):
                act.wait_ge(t.av_ready, u + 1)
                if u >= 2:
                    act.wait_ge(o_ready, u - 1)
                act.activation(oT[:, u % 2, :, :], t.av[u % 2][0:KD, 0:2 * P].rearrange("p (g c) -> p g c", g=2), ACT.Copy
                               ).then_inc(oT_ready, 1)

            t.exps(act, 0, range(HEADS_U))
            for u in range(UNITS):
                if u >= 2:
                    leave_values(u - 2)
                if u + 1 < UNITS:
                    t.exps(act, u + 1, range(HEADS_U // 2))
                t.leave_act(act, u)
                if u + 1 < UNITS:
                    t.exps(act, u + 1, range(HEADS_U // 2, HEADS_U))
            leave_values(UNITS - 2)
            leave_values(UNITS - 1)

        @block.gpsimd
        def _(pool):
            pool.wait_ge(rope_done, len(parts))
            pool.wait_ge(w_in, 16 * len(loads))
            for u in range(UNITS):
                keys(pool, u, (0,), t.km_pool)

        @block.vector
        def _(dve):
            c = Chain(dve, step)
            dve.wait_ge(w_in, 16 * len(loads))
            for x in range(2):
                src = wb[:, x, :].rearrange("p (h r d) -> p h r d", h=HEADS_U, r=2)
                dst = wr[:, x, :].rearrange("p (h r d) -> p h r d", h=HEADS_U, r=2)
                dve.tensor_scalar(dst[:, :, 0, :], src[:, :, 1, :], -1.0, None, ALU.mult).then_inc(rot_ready, 1)
                dve.tensor_copy(dst[:, :, 1, :], src[:, :, 0, :]).then_inc(rot_ready, 1)
            for n, (x, grp, half) in enumerate(parts):
                dst = (t.qT[0:KD] if x == 0 else t.kT[:])[:, grp, half * 512:(half + 1) * 512]
                dve.wait_ge(qk_ready, n + 1)
                if n >= 2:
                    dve.wait_ge(rope_done, n - 1)
                dve.tensor_tensor(rope[:, n % 2, 0, :], banks[2 * (n % 4)][0:KD, :], cosT[:], ALU.mult).then_inc(cs_done, 1)
                dve.tensor_tensor(rope[:, n % 2, 1, :], banks[2 * (n % 4) + 1][0:KD, :], sinT[:], ALU.mult).then_inc(cs_done, 1)
                dve.wait_ge(cs_done, 2 * n + 2)
                dve.tensor_tensor(dst, rope[:, n % 2, 0, :], rope[:, n % 2, 1, :], ALU.add).then_inc(rope_done, 1)
            def finish(u):
                dve.wait_ge(o_ready, u + 1)
                dve.tensor_tensor(g.h[:, u, :], g.h[:, u, :], t.av[u % 2][:, 256:256 + D], ALU.add).then_inc(t.av_done, 1)

            dve.wait_ge(rope_done, len(parts))
            for u in range(KEYS_DEEP):
                keys(dve, u, (1, 2), t.km_dve)
                if u >= 1:
                    t.maximum(dve, u - 1)
            for u in range(UNITS):
                if u + KEYS_DEEP < UNITS:
                    keys(dve, u + KEYS_DEEP, (1, 2), t.km_dve)
                t.inverse(dve, u)
                dve.tensor_tensor(t.prob[:, u % 2], t.prob[:, u % 2], t.rinv[:, u % 2, :].unsqueeze(2).to_broadcast([P, HEADS_U, P]),
                                  ALU.mult).then_inc(prob_ready, 1)
                if u + 2 < UNITS:
                    t.maximum(dve, u + 2)
                t.leave_dve(dve, u)
                if u >= 2:
                    finish(u - 2)
            finish(UNITS - 2)
            finish(UNITS - 1)
            dve.wait_ge(t.av_done, UNITS)


def slot_weights(nc, g, CT, Dn, zn):
    with Scope(nc, "slw") as s:
        nmax, zsum, rz = (s.sb(n, [P, 2]) for n in ("nmax", "zsum", "rz"))
        ze = s.sb("ze", [P, 2, SLOT_E])
        lg, ex = (s.sb(n, [P, 2, ALL_SLOTS]) for n in ("lg", "ex"))
        dmax, dsum = (s.sb(n, [P, 2, SLOT_CHUNKS, TILE_IMAGES]) for n in ("dmax", "dsum"))
        cl = s.ps("cl", [P, 2, 2, 512])
        dl = s.ps("dl", [P, 2, 512])
        tp = s.ps("tp", [P, 2, 512])
        step, cl_ready, lg_ready, cmax_ready, cexp_ready, rz_ready, cw_ready, tp_ready, ct_done, dl_ready, dsub_ready, dexp_ready, \
            dsum_ready, dn_done = (
            s.sem(n) for n in ("step", "cl_ready", "lg_ready", "cmax_ready", "cexp_ready", "rz_ready", "cw_ready", "tp_ready",
                               "ct_done", "dl_ready", "dsub_ready", "dexp_ready", "dsum_ready", "dn_done"))
        block = s.block()

        def chunks(bank):
            return bank[:].rearrange("p a (c t) -> p (a c) t", c=SLOT_CHUNKS // 2)

        def tile(x, i):
            return x[:, :, i * P:(i + 1) * P]

        def by_image(x):
            return x.rearrange("p c (b n) -> p c b n", n=PATCHES)

        def spread(x):
            return x.unsqueeze(3).to_broadcast([P, SLOT_CHUNKS, TILE_IMAGES, PATCHES])

        @block.tensor
        def _(pe):
            pe.wait_ge(g.phi_in, 16)

            def transposed(bank, src, ready):
                for c in range(SLOT_CHUNKS):
                    tr = pe.transpose(chunks(bank)[:, c, :], src[:, c * P:(c + 1) * P], g.ident[:])
                tr.then_inc(ready, 1)

            def logits(i):
                if i >= 2:
                    pe.wait_ge(lg_ready, i - 1)
                for half in range(2):
                    for k in range(NKD):
                        mm = pe.matmul(cl[:, i % 2, half, :], g.xnT[:, k, i * P:(i + 1) * P],
                                       g.phi[:, k, half * 512:(half + 1) * 512], start=(k == 0), stop=(k == NKD - 1))
                mm.then_inc(cl_ready, 1)

            logits(0)
            logits(1)
            for i in range(TILES + 1):
                if i < TILES:
                    pe.wait_ge(lg_ready, i + 1)
                    if i >= 1:
                        pe.wait_ge(dsub_ready, i)
                    transposed(dl, lg[:, i % 2], dl_ready)
                if i >= 1:
                    pe.wait_ge(cw_ready, i)
                    if i >= 2:
                        pe.wait_ge(ct_done, i - 1)
                    transposed(tp, ex[:, (i - 1) % 2], tp_ready)
                if i + 2 < TILES:
                    logits(i + 2)

        @block.scalar
        def _(act):
            def leave(i):
                act.wait_ge(cl_ready, i + 1)
                if i >= 2:
                    act.wait_ge(dl_ready, i - 1)
                    act.wait_ge(cmax_ready, i - 1)
                act.activation(lg[:, i % 2, :].rearrange("p (a c) -> p a c", a=2), cl[:, i % 2], ACT.Copy).then_inc(lg_ready, 1)

            leave(0)
            for i in range(TILES + 1):
                b = i % 2
                if i < TILES:
                    act.wait_ge(cmax_ready, i + 1)
                    if i >= 2:
                        act.wait_ge(tp_ready, i - 1)
                    for e in range(SLOT_E):
                        act.activation(ex[:, b, e * SLOTS:(e + 1) * SLOTS], lg[:, b, e * SLOTS:(e + 1) * SLOTS],
                                       ACT.Exp, bias=nmax[:, b:b + 1], accum_out=ze[:, b, e:e + 1]).then_inc(cexp_ready, 1)
                if i + 1 < TILES:
                    leave(i + 1)
                if i < TILES:
                    act.wait_ge(rz_ready, i + 1)
                    act.activation(ex[:, b, :], ex[:, b, :], ACT.Copy, scale=rz[:, b:b + 1]).then_inc(cw_ready, 1)
                if i >= 1:
                    act.wait_ge(tp_ready, i)
                    act.activation(tile(CT, i - 1), chunks(tp), ACT.Copy).then_inc(ct_done, 1)
                if i < TILES:
                    act.wait_ge(dsub_ready, i + 1)
                    act.activation(tile(Dn, i), tile(Dn, i), ACT.Exp).then_inc(dexp_ready, 1)

        @block.vector
        def _(dve):
            c = Chain(dve, step)

            def sums(i):
                dve.wait_ge(dexp_ready, i + 1)
                if i >= 2:
                    dve.wait_ge(dn_done, i - 1)
                c.after(dve.tensor_reduce(dsum[:, i % 2], by_image(tile(Dn, i)), AX.X, ALU.add))
                dve.reciprocal(dsum[:, i % 2], dsum[:, i % 2]).then_inc(dsum_ready, 1)

            def maximum(i):
                dve.wait_ge(lg_ready, i + 1)
                dve.tensor_reduce(nmax[:, i % 2:i % 2 + 1], lg[:, i % 2], AX.X, ALU.max, negate=True).then_inc(cmax_ready, 1)

            maximum(0)
            for i in range(TILES):
                b = i % 2
                dve.wait_ge(dl_ready, i + 1)
                c.after(dve.tensor_reduce(dmax[:, b], by_image(chunks(dl)), AX.X, ALU.max))
                dve.tensor_tensor(by_image(tile(Dn, i)), by_image(chunks(dl)), spread(dmax[:, b]), ALU.subtract
                                  ).then_inc(dsub_ready, 1)
                dve.wait_ge(cexp_ready, SLOT_E * (i + 1))
                c.after(dve.tensor_reduce(zsum[:, b:b + 1], ze[:, b, :], AX.X, ALU.add))
                dve.reciprocal(rz[:, b:b + 1], zsum[:, b:b + 1]).then_inc(rz_ready, 1)
                if i + 1 < TILES:
                    maximum(i + 1)
                dve.wait_ge(rz_ready, i + 1)
                c.after(dve.tensor_scalar(zn[:, i, :], ze[:, b, :], rz[:, b:b + 1], None, ALU.mult))
                if i >= 1:
                    sums(i - 1)
            sums(TILES - 1)

        @block.gpsimd
        def _(pool):
            for i in range(TILES):
                pool.wait_ge(dsum_ready, i + 1)
                pool.tensor_tensor(by_image(tile(Dn, i)), by_image(tile(Dn, i)), spread(dsum[:, i % 2]), ALU.mult).then_inc(dn_done, 1)
            pool.wait_ge(dn_done, TILES)


def hidden_pieces(nc, g, b1, g_dram, b_dram):
    WIDE = SLOT_E * HID
    with Scope(nc, "hid") as s:
        gp = s.sb("gp", [P, 2, 3, WIDE], BF16)
        rest = s.sb("rest", [P, 2, HID])
        b1f = s.sb("b1f", [P, 2, WIDE // P])
        bp = s.sb("bp", [P, 3, WIDE // P], BF16)
        gps = [s.ps(f"gps{i}", [P, 2, 512]) for i in range(4)]
        b_in, step, g_ready, one, rest1, two, three, b_done, g_out = (
            s.sem(n) for n in ("b_in", "step", "g_ready", "one", "rest1", "two", "three", "b_done", "g_out"))
        out_done = g.g_out
        block = s.block()
        steps = [(i, e) for i in range(TILES) for e in range(SLOT_E)]

        @block.sync
        def _(sp):
            sp.dma_start(b1f[:, 0, :], b1).then_inc(b_in, 16)
            sp.wait_ge(b_done, 1)
            sp.dma_start(b_dram.rearrange("k (p c) -> p k c", p=P), bp[:]).then_inc(g_out, 16)
            for i in range(TILES):
                for half in range(2):
                    at = slice(half * WIDE // 2, (half + 1) * WIDE // 2)
                    sp.wait_ge(three, SLOT_E * i + 2 * half + 2)
                    for k in range(3):
                        sp.dma_start(g_dram[k, i * P:(i + 1) * P, at], gp[:, i % 2, k, at]).then_inc(out_done[i % 2], 16)
            sp.wait_ge(g_out, 16)

        @block.tensor
        def _(pe):
            pe.wait_ge(g.w1_in, 16)
            for n, (i, e) in enumerate(steps):
                if n >= 4:
                    pe.wait_ge(rest1, n - 3)
                for half in range(2):
                    for k in range(NKD):
                        at = e * HID + half * HALF
                        mm = pe.matmul(gps[n % 4][:, half, 0:HALF], g.xnT[:, k, i * P:(i + 1) * P],
                                       g.w1[:, k, at:at + HALF], start=(k == 0), stop=(k == NKD - 1))
                mm.then_inc(g_ready, 1)

        def piece(buf, k, e):
            return gp[:, buf, k, e * HID:(e + 1) * HID].rearrange("p (a c) -> p a c", a=2)

        def halves(x):
            return x.rearrange("p (a c) -> p a c", a=2)

        @block.scalar
        def _(act):
            def second(n):
                i, e = steps[n]
                act.wait_ge(rest1, n + 1)
                act.activation(piece(i % 2, 1, e), halves(rest[:, n % 2, :]), ACT.Copy).then_inc(two, 1)

            for n, (i, e) in enumerate(steps):
                act.wait_ge(g_ready, n + 1)
                if i >= 2:
                    act.wait_ge(out_done[i % 2], 96 * (i // 2))
                act.activation(piece(i % 2, 0, e), gps[n % 4][:, :, 0:HALF], ACT.Copy).then_inc(one, 1)
                if n >= 1:
                    second(n - 1)
            second(len(steps) - 1)

        @block.vector
        def _(dve):
            c = Chain(dve, step)
            dve.wait_ge(b_in, 16)
            c.after(dve.tensor_copy(bp[:, 0, :], b1f[:, 0, :]))
            c.after(dve.tensor_tensor(b1f[:, 1, :], b1f[:, 0, :], bp[:, 0, :], ALU.subtract))
            c.after(dve.tensor_copy(bp[:, 1, :], b1f[:, 1, :]))
            dve.tensor_tensor(bp[:, 2, :], b1f[:, 1, :], bp[:, 1, :], ALU.subtract).then_inc(b_done, 1)

            def third(n):
                i, e = steps[n]
                dve.wait_ge(two, n + 1)
                dve.tensor_tensor(piece(i % 2, 2, e), halves(rest[:, n % 2, :]), piece(i % 2, 1, e), ALU.subtract).then_inc(three, 1)

            for n, (i, e) in enumerate(steps):
                dve.wait_ge(one, n + 1)
                if n >= 2:
                    dve.wait_ge(three, n - 1)
                dve.tensor_tensor(halves(rest[:, n % 2, :]), gps[n % 4][:, :, 0:HALF], piece(i % 2, 0, e), ALU.subtract).then_inc(rest1, 1)
                if n >= 1:
                    third(n - 1)
            third(len(steps) - 1)


def slot_experts(nc, g, CT, Dn, zn, b2_rows, g_dram, b_dram):
    TP = TILE_IMAGES // 2
    with Scope(nc, "sle") as s:
        UT = s.sb("UT", [P, HC, SLOT_E, TILE_IMAGES, PATCHES])
        H = s.sb("H", [P, 8, HID])
        G = s.sb("G", [BROWS, 2, SLOT_E * HID], BF16)
        dp = s.sb("dp", [P, 2, SLOT_CHUNKS, BROWS], BF16)
        rest = s.sb("rest", [P, 2, SLOT_CHUNKS, PATCHES])
        dT = s.sb("dT", [BROWS, 2, ALL_SLOTS], BF16)
        cw = s.sb("cw", [P, 2, SLOT_CHUNKS, 2 * PATCHES])
        U = s.sb("U", [P, HID])
        b2 = s.sb("b2", [P, SLOT_E, D])
        acc = s.sb("acc", [P, D])
        identb = s.sb("identb", [P, P], BF16)
        hp = [s.ps(f"hp{i}", [P, 2, 512]) for i in range(2)]
        up = s.ps("up", [P, 2, 512])
        dps = s.ps("dps", [P, 1024], BF16)
        tps = s.ps("tps", [P, 512])
        b_in, consts, identb_ready, turn, step, pstep, pieces_ready, cw_ready, dps_ready, dT_ready, hid_ready, gelu_done, mix_done, \
            u_ready, ut_ready, ut_done, y_ready, y_done = (s.sem(n) for n in (
                "b_in", "consts", "identb_ready", "turn", "step", "pstep", "pieces_ready", "cw_ready", "dps_ready", "dT_ready", "hid_ready",
                "gelu_done", "mix_done", "u_ready", "ut_ready", "ut_done", "y_ready", "y_done"))
        g_in = [s.sem(f"g_in{i}") for i in range(2)]
        cw_zero = s.sem("cw_zero")
        block = s.block()
        G_STORED = 16 * 3 * 2 * TILES // 2
        ORDER = [0, 2, 4, 6, 1, 3, 5, 7]
        BEFORE = [[], [(1, 0)], [], [(1, 1)], [], [], [], []]
        OWN = [[], [], [], [], [], [(0, 0)], [], [(0, 1)]]
        POOL_STEPS = 5

        def program(eng, pair):
            pair(0, None, True, 0, None)
            with eng.Fori(1, TP) as j:
                pair(j, None, False, j, None)
            with eng.Fori(1, TILES) as t:
                pair(TP * t, t - 1, False, 0, None)
                with eng.Fori(1, TP) as j:
                    pair(TP * t + j, None, False, j, t)

        @block.sync
        def _(sp):
            sp.dma_start(b2[:].rearrange("p e d -> p (e d)"), b2_rows).then_inc(b_in, 16)
            for p in range(2):
                sp.dma_start(G[PROWS:BROWS, p, :], b_dram).then_inc(b_in, 16)
            sp.wait_ge(g.g_out[0], G_STORED)

            def pair(r, prev, first, j, tile):
                if prev is not None:
                    sp.wait_ge(g.g_out[1], G_STORED)
                for p in range(2):
                    n = 2 * r + p
                    if not first:
                        sp.wait_ge(hid_ready, 8 * n - 8)
                    row = 0
                    for k, copies in ((0, 3), (1, 2), (2, 1)):
                        src = g_dram[k, bass.ds(n * PATCHES, PATCHES), :]
                        for c in range(copies):
                            sp.dma_start(G[row:row + PATCHES, p, :], src).then_inc(g_in[p], 16)
                            row += PATCHES

            program(sp, pair)

        @block.gpsimd
        def _(pool):
            pool.memset(dp[:, :, :, PROWS:], 1.0).then_inc(consts, 1)
            pool.wait_ge(consts, 1)
            pool.wait_ge(cw_zero, 1)

            def pieces(n, p, first, image):
                c = Chain(pool, pstep, base=POOL_STEPS * n, turn=turn)
                if not first:
                    pool.wait_ge(dps_ready, n - 1)
                    pool.sem_inc(turn, 1)
                q = PATCHES
                src = Dn[:, :, bass.ds(image * PATCHES, PATCHES)]
                d = dp[:, p]
                c.after(pool.tensor_copy(d[:, :, 0:q], src))
                c.after(pool.tensor_tensor(rest[:, p], src, d[:, :, 0:q], ALU.subtract))
                c.after(pool.tensor_copy(d[:, :, q:2 * q], rest[:, p]))
                c.after(pool.tensor_tensor(d[:, :, 2 * q:3 * q], rest[:, p], d[:, :, q:2 * q], ALU.subtract))
                c.after(pool.tensor_copy(d[:, :, 3 * q:5 * q], d[:, :, 0:2 * q]))
                pool.tensor_copy(d[:, :, 5 * q:6 * q], d[:, :, 0:q]).then_inc(pieces_ready, 1)

            def pair(r, prev, first, j, tile):
                for p in range(2):
                    n = 2 * r + p
                    pieces(n, p, first, n)
                    if not first:
                        pool.wait_ge(mix_done, 4 * n - 4)
                        pool.sem_inc(turn, 1)
                    pool.tensor_copy(cw[:, p, :, p * PATCHES:(p + 1) * PATCHES], CT[:, :, bass.ds(n * PATCHES, PATCHES)]).then_inc(cw_ready, 1)

            program(pool, pair)
            pieces(IMAGES, 0, False, IMAGES - 1)

        @block.tensor
        def _(pe):
            pe.wait_ge(b_in, 48)
            pe.wait_ge(identb_ready, 1)
            pe.wait_ge(g.w2_in, 16)

            def transpose_pieces(n, p, chunks):
                if chunks[0] == 0:
                    pe.wait_ge(pieces_ready, n + 1)
                    pe.wait_ge(dT_ready, n)
                for c in chunks:
                    tr = pe.transpose(dps[0:BROWS, c * P:(c + 1) * P], dp[:, p, c, :], identb[:])
                if chunks[-1] == SLOT_CHUNKS - 1:
                    tr.then_inc(dps_ready, 1)

            def mix(n, p, r, grp, half):
                pe.wait_ge(gelu_done, 8 * n + 4 * grp + 4)
                if half == 0 and grp == 0:
                    pe.wait_ge(cw_ready, n + 1)
                if p == 0 and grp == 0 and not (isinstance(r, int) and r == 0):
                    pe.wait_ge(u_ready, 2 * r - 1 + half)
                for e in range(SLOT_E):
                    mm = pe.matmul(up[32 * e:32 * e + 32, half, 0:HALF], cw[:, p, 2 * e + grp, :],
                                   H[:, 4 * grp + e, half * HALF:(half + 1) * HALF],
                                   start=(p == 0 and grp == 0), stop=(p == 1 and grp == 1))
                mm.then_inc(mix_done, 1)

            def transpose_u(r, part):
                pe.wait_ge(u_ready, 2 * r + part + 1)
                pe.wait_ge(ut_done, 2 * r + part + 1)
                for c in range(3):
                    at = (3 * part + c) * P
                    tr = pe.transpose(tps[:, c * P:(c + 1) * P], U[:, at:at + P], g.ident[:])
                tr.then_inc(ut_ready, 1)

            def down(t):
                pe.wait_ge(ut_done, 2 * TP * (t + 1) + 1)
                for e in range(SLOT_E):
                    for c in range(HC):
                        mm = pe.matmul(tps[:, 0:D], UT[:, c, e, :, :], g.w2[:, e * HC + c, :],
                                       start=(e == 0 and c == 0), stop=(e == SLOT_E - 1 and c == HC - 1))
                mm.then_inc(y_ready, 1)

            def pair(r, prev, first, j, tile):
                for p in range(2):
                    n = 2 * r + p
                    start = first and p == 0
                    if start:
                        transpose_pieces(0, 0, range(SLOT_CHUNKS))
                    pe.wait_ge(dT_ready, n + 1)
                    pe.wait_ge(g_in[p], 96 * r + 96)
                    for q in range(SLOT_CHUNKS):
                        c = ORDER[q]
                        if not (start and q < 2):
                            pe.wait_ge(gelu_done, 8 * n + q - 1)
                        for half in range(2):
                            at = (c // 2) * HID + half * HALF
                            mm = pe.matmul(hp[q % 2][:, half, 0:HALF], dT[:, p, c * P:(c + 1) * P],
                                           G[:, p, at:at + HALF], start=True, stop=True)
                        mm.then_inc(hid_ready, 1)
                        if not start:
                            for grp, half in BEFORE[q]:
                                mix(n - 1, 1 - p, r - 1 + p, grp, half)
                        for grp, half in OWN[q]:
                            mix(n, p, r, grp, half)
                        if q in (2, 4):
                            transpose_pieces(n + 1, 1 - p, range(2 * q - 4, 2 * q))
                        if q == (6, 0)[p] and not first:
                            if tile is not None and p == 0:
                                pe.wait_ge(y_done, tile)
                            transpose_u(r - 1, p)
                        if q == 6 and prev is not None and p == 1:
                            down(prev)

            program(pe, pair)
            for grp, half in sum(BEFORE, []):
                mix(IMAGES - 1, 1, IMAGES // 2 - 1, grp, half)
            transpose_u(IMAGES // 2 - 1, 0)
            transpose_u(IMAGES // 2 - 1, 1)
            down(TILES - 1)

        @block.scalar
        def _(act):
            for k in range(2):
                act.wait_ge(g.g_out[k], G_STORED)

            def pair(r, prev, first, j, tile):
                for p in range(2):
                    n = 2 * r + p
                    for q in range(SLOT_CHUNKS):
                        act.wait_ge(hid_ready, 8 * n + q + 1)
                        grp = q // 4
                        if q % 4 == 0 and not (first and p == 0):
                            act.wait_ge(mix_done, 4 * n + 2 * grp - 2)
                        act.activation(H[:, q, :].rearrange("p (a c) -> p a c", a=2), hp[q % 2][:, :, 0:HALF],
                                       ACT.Gelu_apprx_tanh).then_inc(gelu_done, 1)

            program(act, pair)

        @block.vector
        def _(dve):
            dve.memset(cw[:], 0.0).then_inc(cw_zero, 1)
            dve.tensor_copy(identb[:], g.ident[:]).then_inc(identb_ready, 1)
            dve.sem_inc(ut_done, 1)
            FIN = 4

            def leave_pieces(n, p):
                dve.wait_ge(dps_ready, n + 1)
                dve.tensor_copy(dT[:, p, :], dps[0:BROWS, :]).then_inc(dT_ready, 1)

            def leave_u(r, half):
                dve.wait_ge(mix_done, 8 * r + 7 + half)
                dve.tensor_copy(U[:, half * HALF:(half + 1) * HALF], up[:, half, 0:HALF]).then_inc(u_ready, 1)

            def leave_ut(r, part, j):
                dve.wait_ge(ut_ready, 2 * r + part + 1)
                dve.tensor_copy(UT[:, 3 * part:3 * part + 3, :, bass.ds(2 * j, 2), :],
                                tps[:, 0:3 * P].rearrange("p (c e o n) -> p c e o n", c=3, e=SLOT_E, n=PATCHES)).then_inc(ut_done, 1)

            def finish(t):
                c = Chain(dve, step, base=FIN * t)
                dve.wait_ge(y_ready, t + 1)
                ht = g.h[:, bass.ds(t, 1), :].rearrange("p o d -> p (o d)")
                dve.tensor_tensor(acc[:], tps[:, 0:D], ht, ALU.add).then_inc(y_done, 1)
                dve.wait_ge(y_done, t + 1)
                for e in range(SLOT_E):
                    op = dve.scalar_tensor_tensor(acc[:] if e < SLOT_E - 1 else ht, b2[:, e, :],
                                                  zn[:, bass.ds(t, 1), e:e + 1].rearrange("p o e -> p (o e)"),
                                                  acc[:], ALU.mult, ALU.add)
                    if e < SLOT_E - 1:
                        c.after(op)
                op.then_inc(step, 1)

            def pair(r, prev, first, j, tile):
                if first:
                    leave_pieces(0, 0)
                j_before = TP - 1 if prev is not None else j - 1
                if not first:
                    leave_u(r - 1, 0)
                    leave_u(r - 1, 1)
                leave_pieces(2 * r + 1, 1)
                if not first:
                    leave_ut(r - 1, 0, j_before)
                    leave_ut(r - 1, 1, j_before)
                leave_pieces(2 * r + 2, 0)
                if prev is not None:
                    finish(prev)

            dve.wait_ge(b_in, 48)
            program(dve, pair)
            for half in range(2):
                leave_u(IMAGES // 2 - 1, half)
            for part in range(2):
                leave_ut(IMAGES // 2 - 1, part, TP - 1)
            finish(TILES - 1)
            dve.wait_ge(step, FIN * TILES)


def soft_moe(nc, g, a):
    with Scope(nc, "smoe") as s:
        CT = s.sb("CT", [P, SLOT_CHUNKS, TOKENS])
        Dn = s.sb("Dn", [P, SLOT_CHUNKS, TOKENS])
        zn = s.sb("zn", [P, TILES, SLOT_E])
        g_dram = nc.dram_tensor("g_pieces", (3, TOKENS, SLOT_E * HID), BF16).ap()
        b_dram = nc.dram_tensor("b_pieces", (3, SLOT_E * HID), BF16).ap()
        slot_weights(nc, g, CT, Dn, zn)
        hidden_pieces(nc, g, a["b1"], g_dram, b_dram)
        slot_experts(nc, g, CT, Dn, zn, a["b2_rows"], g_dram, b_dram)


class Globals:
    pass


def route(nc, g, a, rt, xn_dram):
    SETS = TILES * G1 + TILES
    LOWEST = float(np.finfo(np.float32).min)
    with Scope(nc, "rte") as s:
        wg = s.sb("wg", [KD, NKD, G1 + EXPERTS])
        bg = s.sb("bg", [P, G1 + EXPERTS])
        tri, ones = s.sb("tri", [P, P]), s.sb("ones", [P, P])
        tri32 = s.sb("tri32", [P, EXPERTS, EXPERTS])
        steps = s.sb("steps", [P, TILES])
        lane, tile_lane = s.sb("lane", [P, P]), s.sb("tile_lane", [P, MOE_TILES])
        row_tile, row_lane = (s.sb(n, [P, TILES * TOPK]) for n in ("row_tile", "row_lane"))
        spare, own_tile = s.sb("spare", [P, 1]), s.sb("own_tile", [P, 1])
        placei, lanei, tilei = (s.sb(n, [P, TILES * TOPK], U32) for n in ("placei", "lanei", "tilei"))
        lanef, tilef = (s.sb(n, [P, TILES * TOPK]) for n in ("lanef", "tilef"))
        in_lane = s.sb("in_lane", [P, TILES * TOPK, P], BF16)
        in_tile = s.sb("in_tile", [P, TILES * TOPK, MOE_TILES])
        row_in = s.sb("row_in", [P, TILES * TOPK, 2, MOE_TILES], BF16)
        rows, free, row_sum = s.sb("rows", [P, MOE_TILES]), s.sb("free", [P, MOE_TILES]), s.sb("row_sum", [P, 2 * MOE_TILES])
        lg = s.sb("lg", [P, TILES, G1 + EXPERTS])
        val = s.sb("val", [P, SETS, E1])
        best = s.sb("best", [P, 2, SETS])
        took = s.sb("took", [P, 2, SETS, E1])
        equal, order = s.sb("equal", [P, SETS, E1]), s.sb("order", [P, E1])
        top = s.sb("top", [P, SETS])
        ev = s.sb("ev", [P, SETS])
        share = s.sb("share", [P, 2, SETS])
        part = s.sb("part", [P, 2, 2, TILES, G1])
        gate = s.sb("gate", [P, 2, 2, TILES])
        both = s.sb("both", [P, SETS, E1])
        work = s.sb("work", [P, TOPK * TILES * EXPERTS])
        mask = s.sb("mask", [P, TOPK, TILES, EXPERTS])
        sel, pos = (s.sb(n, [P, TILES, EXPERTS]) for n in ("sel", "pos"))
        cum = s.sb("cum", [P, TILES + 1, EXPERTS])
        cnt, need, base, incl = (s.sb(n, [P, EXPERTS]) for n in ("cnt", "need", "base", "incl"))
        placef = s.sb("placef", [P, TILES, TOPK])
        owner = s.sb("owner", [P, 1])
        ps_lg, ps_pos, ps_cnt, ps_row = (s.ps(n, [P, 512]) for n in ("ps_lg", "ps_pos", "ps_cnt", "ps_row"))
        val_ready, mask_ready, tile_ready, row_in_ready = (s.sem(n) for n in ("val_ready", "mask_ready", "tile_ready", "row_in_ready"))
        quarter = TILES * TOPK // 4
        c_in, lg_ready, ones_ready, diff_ready, exp_ready, sel_ready, pos_ready, in_ready, step = (
            s.sem(n) for n in ("c_in", "lg_ready", "ones_ready", "diff_ready", "exp_ready", "sel_ready", "pos_ready",
                               "in_ready", "step"))
        xn_out, row_ready, owner_ready, owner_out, slot_done = (
            s.sem(n) for n in ("xn_out", "row_ready", "owner_ready", "owner_out", "slot_done"))
        loads = [(wg[:], a["wgate"]), (bg[:], a["bgate_rows"]), (tri[:], a["tri"]),
                 (order[:], a["order8"]), (tri32[:].rearrange("p a b -> p (a b)"), a["tri32"]), (steps[:], a["steps"]),
                 (tile_lane[:], a["tile_no"]), (lane[:], a["lane"]), (row_tile[:], a["row_tile"]), (row_lane[:], a["row_lane"]),
                 (spare[:], a["spare"]), (own_tile[:], a["own_tile"])]
        layernorm(nc, g, "ln3", None, loads, c_in)
        block = s.block()

        @block.sync
        def _(sp):
            sp.dma_start(xn_dram.rearrange("(i p) d -> p i d", p=P), g.xn[:]).then_inc(xn_out, 16)
            sp.wait_ge(xn_out, 16)

        @block.gpsimd
        def _(pool):
            for n in range(0, TILES * TOPK, quarter):
                pool.wait_ge(tile_ready, n // quarter + 1)
                for part, number in enumerate((row_tile, row_lane)):
                    pool.tensor_tensor(row_in[:, n:n + quarter, part], in_tile[:, n:n + quarter],
                                       number[:, n:n + quarter].unsqueeze(2).to_broadcast([P, quarter, MOE_TILES]), ALU.mult
                                       ).then_inc(row_in_ready, 1)

        @block.tensor
        def _(pe):
            pe.wait_ge(c_in, 16 * len(loads))
            for i in range(TILES):
                for k in range(NKD):
                    mm = pe.matmul(ps_lg[:, i * 36:(i + 1) * 36], g.xnT[:, k, i * P:(i + 1) * P], wg[:, k, :],
                                   start=(k == 0), stop=(k == NKD - 1))
            mm.then_inc(lg_ready, 1)
            pe.wait_ge(ones_ready, 1)
            pe.wait_ge(sel_ready, 1)
            pe.matmul(ps_pos[:, 0:TILES * EXPERTS], tri[:], sel[:].rearrange("p i e -> p (i e)"), start=True, stop=False)
            pe.matmul(ps_pos[:, 0:TILES * EXPERTS], ones[:], cum[:, 0:TILES, :].rearrange("p i e -> p (i e)"), start=False, stop=True)
            pe.matmul(ps_cnt[:, 0:EXPERTS], ones[:], cum[:, TILES, :], start=True, stop=True).then_inc(pos_ready, 1)
            pe.wait_ge(owner_ready, 1)
            pe.matmul(ps_cnt[0:1, P:P + MOE_TILES], owner[:], g.ident[:, 0:MOE_TILES], start=True, stop=True).then_inc(owner_out, 1)
            for n in range(TILES * TOPK):
                if n % quarter == 0:
                    pe.wait_ge(in_ready, n // quarter + 1)
                    pe.wait_ge(row_in_ready, 2 * (n // quarter + 1))
                mm = pe.matmul(ps_row[:, 0:2 * MOE_TILES], in_lane[:, n, :], row_in[:, n].rearrange("p a t -> p (a t)"), start=(n == 0), stop=(n == TILES * TOPK - 1))
            mm.then_inc(row_ready, 1)

        @block.scalar
        def _(act):
            act.wait_ge(diff_ready, 1)
            act.activation(ev[:], ev[:], ACT.Exp).then_inc(exp_ready, 1)

        @block.vector
        def _(dve):
            c = Chain(dve, step)
            dve.memset(ones[:], 1.0).then_inc(ones_ready, 1)
            c.after(dve.memset(val[:], LOWEST))
            dve.wait_ge(c_in, 16 * len(loads))
            dve.wait_ge(lg_ready, 1)
            c.after(dve.tensor_tensor(lg[:], ps_lg[:, 0:TILES * 36].rearrange("p (i n) -> p i n", i=TILES),
                                      bg[:].unsqueeze(1).to_broadcast([P, TILES, 36]), ALU.add))
            GROUPS = TILES * G1
            dve.tensor_copy(val[:, GROUPS:, 0:G1], lg[:, :, 0:G1]).then_inc(val_ready, 1)
            dve.tensor_copy(val[:, 0:GROUPS].rearrange("p (i g) e -> p i (g e)", g=G1), lg[:, :, G1:]).then_inc(val_ready, 1)
            dve.wait_ge(val_ready, 2)
            wide = lambda x: x.unsqueeze(2).to_broadcast([P, SETS, E1])
            for n in range(2):
                c.after(dve.tensor_reduce(best[:, n], val[:], AX.X, ALU.max))
                c.after(dve.tensor_tensor(equal[:], val[:], wide(best[:, n]), ALU.is_equal))
                c.after(dve.tensor_tensor(equal[:], equal[:], order[:].unsqueeze(1).to_broadcast([P, SETS, E1]), ALU.mult))
                c.after(dve.tensor_reduce(top[:], equal[:], AX.X, ALU.max))
                c.after(dve.tensor_tensor(took[:, n], equal[:], wide(top[:]), ALU.is_equal))
                if n == 0:
                    c.after(dve.scalar_tensor_tensor(val[:], took[:, 0], LOWEST, val[:], ALU.mult, ALU.add))
            dve.tensor_tensor(ev[:], best[:, 1], best[:, 0], ALU.subtract).then_inc(diff_ready, 1)
            c.after(dve.tensor_tensor(both[:], took[:, 0], took[:, 1], ALU.add))
            groups = lambda x: x[:, GROUPS:, 0:G1].unsqueeze(3).to_broadcast([P, TILES, G1, E1])
            experts = lambda x: x[:, 0:GROUPS].rearrange("p (i g) e -> p i g e", g=G1)
            split = lambda x: x.rearrange("p i (g e) -> p i g e", g=G1)
            c.after(dve.tensor_tensor(split(sel[:]), experts(both), groups(both), ALU.mult))
            c.after(dve.memset(cum[:, 0, :], 0.0))
            for i in range(TILES):
                op = dve.tensor_tensor(cum[:, i + 1, :], cum[:, i, :], sel[:, i, :], ALU.add)
                if i < TILES - 1:
                    c.after(op)
            op.then_inc(sel_ready, 1)

            for k in range(TOPK):
                dve.tensor_tensor(split(mask[:, k]), experts(took[:, k % 2]), groups(took[:, k // 2]), ALU.mult).then_inc(mask_ready, 1)
            dve.wait_ge(exp_ready, 1)
            c.after(dve.tensor_scalar(share[:, 0], ev[:], 1.0, None, ALU.add))
            c.after(dve.reciprocal(share[:, 0], share[:, 0]))
            c.after(dve.tensor_tensor(share[:, 1], ev[:], share[:, 0], ALU.mult))
            for n in range(2):
                c.after(dve.tensor_tensor(part[:, n], took[:, n, GROUPS:, 0:G1].unsqueeze(1).to_broadcast([P, 2, TILES, G1]),
                                          share[:, :, 0:GROUPS].rearrange("p b (i g) -> p b i g", g=G1), ALU.mult))
            c.after(dve.tensor_reduce(gate[:].rearrange("p a b i -> p (a b i)"), part[:].rearrange("p a b i g -> p (a b i) g"), AX.X, ALU.add))
            for n in range(2):
                c.after(dve.tensor_tensor(rt.gate[:, :, 2 * n:2 * n + 2].rearrange("p i b -> p b i"), gate[:, n],
                                          share[:, n, GROUPS:].unsqueeze(1).to_broadcast([P, 2, TILES]), ALU.mult))
            dve.wait_ge(mask_ready, TOPK)
            dve.wait_ge(pos_ready, 1)
            c.after(dve.tensor_copy(cnt[:], ps_cnt[:, 0:EXPERTS]))
            flat = work[:]
            over = flat[:, 0:EXPERTS * TILES].rearrange("p (e n) -> p e n", n=TILES)
            c.after(dve.tensor_tensor(over, cnt[:].unsqueeze(2).to_broadcast([P, EXPERTS, TILES]),
                                      steps[:].unsqueeze(1).to_broadcast([P, EXPERTS, TILES]), ALU.is_gt))
            c.after(dve.tensor_reduce(need[:], over, AX.X, ALU.add))
            before = flat[:, 0:EXPERTS * EXPERTS].rearrange("p (a b) -> p a b", a=EXPERTS)
            c.after(dve.tensor_tensor(before, need[:].unsqueeze(1).to_broadcast([P, EXPERTS, EXPERTS]), tri32[:], ALU.mult))
            c.after(dve.tensor_reduce(base[:], before, AX.X, ALU.add))
            c.after(dve.tensor_tensor(incl[:], base[:], need[:], ALU.add))
            c.after(dve.tensor_scalar(incl[:], incl[:], own_tile[:], None, ALU.is_le))
            dve.tensor_reduce(owner[:], incl[:], AX.X, ALU.add).then_inc(owner_ready, 1)
            c.after(dve.tensor_scalar(base[:], base[:], float(P), None, ALU.mult))
            c.after(dve.tensor_tensor(pos[:], ps_pos[:, 0:TILES * EXPERTS].rearrange("p (i e) -> p i e", i=TILES),
                                      base[:].unsqueeze(1).to_broadcast([P, TILES, EXPERTS]), ALU.add))
            product = flat.rearrange("p (k i e) -> p k i e", k=TOPK, i=TILES)
            c.after(dve.tensor_tensor(product, mask[:], pos[:].unsqueeze(1).to_broadcast([P, TOPK, TILES, EXPERTS]), ALU.mult))
            c.after(dve.tensor_reduce(placef[:].rearrange("p i k -> p k i"), product, AX.X, ALU.add))
            c.after(dve.tensor_copy(placei[:], placef[:].rearrange("p i k -> p (i k)")))
            c.after(dve.tensor_scalar(lanei[:], placei[:], P - 1, None, ALU.bitwise_and))
            c.after(dve.tensor_scalar(tilei[:], placei[:], LANE_BITS, None, ALU.logical_shift_right))
            c.after(dve.tensor_copy(lanef[:], lanei[:]))
            c.after(dve.tensor_copy(tilef[:], tilei[:]))
            for n in range(0, TILES * TOPK, quarter):
                at = slice(n, n + quarter)
                every = lambda x, m: x.unsqueeze(1).to_broadcast([P, quarter, m])
                wide = lambda x, m: x[:, at].unsqueeze(2).to_broadcast([P, quarter, m])
                dve.tensor_tensor(in_tile[:, at], every(tile_lane[:], MOE_TILES), wide(tilef, MOE_TILES), ALU.is_equal).then_inc(tile_ready, 1)
                dve.tensor_tensor(in_lane[:, at], every(lane[:], P), wide(lanef, P), ALU.is_equal).then_inc(in_ready, 1)
            dve.wait_ge(row_ready, 1)
            c.after(dve.tensor_copy(row_sum[:], ps_row[:, 0:2 * MOE_TILES]))
            c.after(dve.scalar_tensor_tensor(rows[:], row_sum[:, 0:MOE_TILES], float(P), row_sum[:, MOE_TILES:], ALU.mult, ALU.add))
            c.after(dve.tensor_scalar(free[:], rows[:], 0.0, spare[:], ALU.is_equal, ALU.mult))
            c.after(dve.tensor_tensor(rows[:], free[:], rows[:], ALU.add))
            c.after(dve.tensor_scalar(rt.slot[:, 1, :], rows[:], -1.0, None, ALU.add))
            dve.tensor_scalar(rt.slot[:, 0, :], rt.slot[:, 1, :], TOKENS - 1, None, ALU.bitwise_and).then_inc(slot_done, 1)
            dve.wait_ge(owner_out, 1)
            dve.tensor_scalar(rt.expert[:], ps_cnt[0:1, P:P + MOE_TILES], float(EXPERTS - 1), None, ALU.min).then_inc(slot_done, 1)
            dve.wait_ge(slot_done, 2)


def expert_tiles(nc, g, a, rt, xn_dram, y_dram):
    DEEP = 3
    ROUNDS = MOE_TILES // DEEP
    with Scope(nc, "ext") as s:
        w1 = s.sb("w1", [KD + 1, DEEP, NKD, HID])
        w2 = s.sb("w2", [P, DEEP, HC, D])
        b2 = s.sb("b2", [P, DEEP, D])
        x = s.sb("x", [P, DEEP, D])
        xT = s.sb("xT", [KD + 1, DEEP, NKD, P])
        H = s.sb("H", [P, DEEP, HC, P])
        y = s.sb("y", [P, DEEP, D])
        xi, yi = ([s.sb(f"{n}{i}", [P, 1], U32) for i in range(DEEP)] for n in ("xi", "yi"))
        hp = [s.ps(f"hp{i}", [P, 2, 512]) for i in range(DEEP)]
        xp, yp = s.ps("xp", [P, 512]), s.ps("yp", [P, 512])
        xi_ready, yi_ready, xp_ready, xT_done, hid_ready, gelu_done, y_ready, y_done, consts, turn = (
            s.sem(n) for n in ("xi_ready", "yi_ready", "xp_ready", "xT_done", "hid_ready", "gelu_done", "y_ready",
                               "y_done", "consts", "turn"))
        w1_in, w2_in, x_in, y_out = ([s.sem(f"{n}{i}") for i in range(DEEP)] for n in ("w1_in", "w2_in", "x_in", "y_out"))
        block = s.block()

        def program(eng, tile):
            for p in range(DEEP):
                tile(p, p, 0, True, False)
            with eng.Fori(1, ROUNDS - 1) as r:
                for p in range(DEEP):
                    tile(DEEP * r + p, p, r, False, False)
            for p in range(DEEP):
                tile(DEEP * (ROUNDS - 1) + p, p, ROUNDS - 1, False, True)

        @block.sync
        def _(sp):
            def load(t, p, r, first, last):
                e = sp.value_load(rt.expert[0:1, bass.ds(t, 1)], min_val=0, max_val=EXPERTS - 1)
                if not first:
                    sp.wait_ge(hid_ready, t - DEEP + 1)
                sp.dma_start(w1[0:KD, p], a["W1"][bass.ds(e, 1)].rearrange("o k c n -> (o k) c n")).then_inc(w1_in[p], 16)
                sp.dma_start(w1[KD:KD + 1, p, 1, :], a["B1"][bass.ds(e, 1), :]).then_inc(w1_in[p], 16)
                if not first:
                    sp.wait_ge(y_done, t - DEEP + 1)
                sp.dma_start(w2[:, p], a["W2"][bass.ds(e, 1)].rearrange("o p c n -> (o p) c n")).then_inc(w2_in[p], 16)
                sp.dma_start(b2[:, p, :], a["B2"][bass.ds(e, 1), :].to_broadcast([P, D])).then_inc(w2_in[p], 16)

            program(sp, load)

        @block.tensor
        def _(pe):
            pe.wait_ge(consts, 1)

            def transpose_x(t, p, r):
                pe.wait_ge(x_in[p], 16 * r + 16)
                if not isinstance(t, int) or t > 0:
                    pe.wait_ge(xT_done, t)
                for k in range(NKD):
                    tr = pe.transpose(xp[0:KD, k * P:(k + 1) * P], x[:, p, k * KD:(k + 1) * KD], g.ident[:])
                tr.then_inc(xp_ready, 1)

            def up(t, p, r, first):
                pe.wait_ge(w1_in[p], 32 * r + 32)
                pe.wait_ge(xT_done, t + 1)
                if not first:
                    pe.wait_ge(gelu_done, t - DEEP + 1)
                for c in range(HC):
                    for k in range(NKD):
                        rows = KD + k
                        mm = pe.matmul(hp[p][:, c // 3, (c % 3) * P:(c % 3 + 1) * P], w1[0:rows, p, k, c * P:(c + 1) * P],
                                       xT[0:rows, p, k, :], start=(k == 0), stop=(k == NKD - 1))
                mm.then_inc(hid_ready, 1)

            def down(t, p, r):
                pe.wait_ge(w2_in[p], 32 * r + 32)
                pe.wait_ge(gelu_done, t + 1)
                if not isinstance(t, int) or t > 0:
                    pe.wait_ge(y_done, t)
                for c in range(HC):
                    mm = pe.matmul(yp[:, 0:D], H[:, p, c, :], w2[:, p, c, :], start=(c == 0), stop=(c == HC - 1))
                mm.then_inc(y_ready, 1)

            def tile(t, p, r, first, last):
                if first and p == 0:
                    transpose_x(0, 0, 0)
                if not (last and p == DEEP - 1):
                    transpose_x(t + 1, (p + 1) % DEEP, r + (p + 1) // DEEP)
                up(t, p, r, first)
                if not (first and p == 0):
                    down(t - 1, (p - 1) % DEEP, r + (p - 1) // DEEP)

            program(pe, tile)
            down(MOE_TILES - 1, DEEP - 1, ROUNDS - 1)

        @block.scalar
        def _(act):
            def gelu(t, p, r, first, last):
                act.wait_ge(hid_ready, t + 1)
                if not first:
                    act.wait_ge(y_ready, t - DEEP + 1)
                act.activation(H[:, p].rearrange("p (a c) n -> p a (c n)", a=2), hp[p][:, :, 0:3 * P], ACT.Gelu).then_inc(gelu_done, 1)

            program(act, gelu)

        @block.vector
        def _(dve):
            dve.memset(xT[KD:KD + 1], 1.0).then_inc(consts, 1)

            def index(n, t, p):
                dve.tensor_copy((xi, yi)[n][p][:], rt.slot[:, n, bass.ds(t, 1)]).then_inc((xi_ready, yi_ready)[n], 1)

            def leave_x(t, p, first):
                dve.wait_ge(xp_ready, t + 1)
                if not first:
                    dve.wait_ge(hid_ready, t - DEEP + 1)
                dve.tensor_copy(xT[0:KD, p], xp[0:KD, 0:2 * P].rearrange("p (k c) -> p k c", k=NKD)).then_inc(xT_done, 1)

            def leave_y(t, p, r, first):
                dve.wait_ge(y_ready, t + 1)
                if not first:
                    dve.wait_ge(y_out[p], 16 * r)
                index(1, t, p)
                dve.wait_ge(w2_in[p], 32 * r + 32)
                dve.tensor_tensor(y[:, p, :], yp[:, 0:D], b2[:, p, :], ALU.add).then_inc(y_done, 1)

            def tile(t, p, r, first, last):
                if first and p == 0:
                    for q in range(DEEP):
                        index(0, q, q)
                    leave_x(0, 0, True)
                if not (last and p == DEEP - 1):
                    leave_x(t + 1, (p + 1) % DEEP, first and p + 1 < DEEP)
                if not last:
                    dve.wait_ge(x_in[p], 16 * r + 16)
                    index(0, t + DEEP, p)
                if not (first and p == 0):
                    leave_y(t - 1, (p - 1) % DEEP, r + (p - 1) // DEEP, first)

            program(dve, tile)
            leave_y(MOE_TILES - 1, DEEP - 1, ROUNDS - 1, False)

        @block.gpsimd
        def _(pool):
            def gather(t, p):
                pool.wait_ge(xi_ready, t + 1)
                pool.sem_inc(turn, 1)
                pool.indirect_dma_start(out=x[:, p, :], out_offset=None, in_=xn_dram,
                                        in_offset=bass.IndirectOffsetOnAxis(ap=xi[p][:], axis=0)).then_inc(x_in[p], 16)

            def scatter(t, p, r, first):
                pool.wait_ge(yi_ready, t + 1)
                pool.wait_ge(y_done, t + 1)
                if not first:
                    pool.wait_ge(y_out[(p - 1) % DEEP], 16 * (r + (p - 1) // DEEP) + 16)
                pool.sem_inc(turn, 1)
                pool.indirect_dma_start(out=y_dram, out_offset=bass.IndirectOffsetOnAxis(ap=yi[p][:], axis=0),
                                        in_=y[:, p, :], in_offset=None).then_inc(y_out[p], 16)

            def tile(t, p, r, first, last):
                if not last:
                    pool.wait_ge(xp_ready, t + 1)
                    gather(t + DEEP, p)
                if not (first and p == 0):
                    scatter(t - 1, (p - 1) % DEEP, r + (p - 1) // DEEP, first and p == 1)

            for q in range(DEEP):
                gather(q, q)
            program(pool, tile)
            scatter(MOE_TILES - 1, DEEP - 1, ROUNDS - 1, False)
            for p in range(DEEP):
                pool.wait_ge(y_out[p], 16 * ROUNDS)
            pool.wait_ge(turn, 2 * MOE_TILES)


def combine(nc, g, rt, y_dram, out):
    with Scope(nc, "cmb") as s:
        rows = s.sb("rows", [P, TILES, TOPK, D])
        row_in = [s.sem(f"row_in{i}") for i in range(TILES)]
        h_step = [s.sem(f"h_step{i}") for i in range(TILES)]
        by_choice = y_dram[0:TOPK * TOKENS].rearrange("(k i p) d -> i p k d", k=TOPK, i=TILES)
        block = s.block()

        def load(eng, i):
            eng.dma_start(rows[:, i], by_choice[i]).then_inc(row_in[i], 16)

        @block.scalar
        def _(act):
            for i in range(1, TILES, 2):
                load(act, i)

        @block.vector
        def _(dve):
            for i in range(0, TILES, 2):
                dve.wait_ge(row_in[i], 16)
                dve.wait_ge(row_in[i + 1], 16)
                for k in range(TOPK):
                    for j in (i, i + 1):
                        if k > 0:
                            dve.wait_ge(h_step[j], k)
                        dve.scalar_tensor_tensor(g.h[:, j, :], rows[:, j, k, :], rt.gate[:, j, k:k + 1], g.h[:, j, :],
                                                 ALU.mult, ALU.add).then_inc(h_step[j], 1)

        @block.sync
        def _(sp):
            for i in range(0, TILES, 2):
                load(sp, i)
            for i in range(TILES):
                sp.wait_ge(h_step[i], TOPK)
                sp.dma_start(out[i * P:(i + 1) * P, :], g.h[:, i, :]).then_inc(g.out_done, 16)
            sp.wait_ge(g.out_done, 16 * TILES)


def routed_moe(nc, g, a, out):
    with Scope(nc, "rmoe") as s:
        rt = Globals()
        rt.gate = s.sb("gate", [P, TILES, TOPK])
        rt.slot = s.sb("slot", [P, 2, MOE_TILES], U32)
        rt.expert = s.sb("expert", [1, MOE_TILES], I32)
        xn_dram = nc.dram_tensor("xn", (TOKENS, D), F32).ap()
        y_dram = nc.dram_tensor("y_by_choice", (TOPK * TOKENS + P, D), F32).ap()
        route(nc, g, a, rt, xn_dram)
        expert_tiles(nc, g, a, rt, xn_dram, y_dram)
        combine(nc, g, rt, y_dram, out)


def build(nc, a, out):
    Scope.ended = []
    with Scope(nc, "vit") as s:
        g = Globals()
        g.h = s.sb("h", [P, TILES, D])
        g.xn = s.sb("xn", [P, TILES, D])
        g.xnT = s.sb("xnT", [KD, NKD, TOKENS])
        g.ident = s.sb("ident", [P, P])
        g.phi = s.sb("phi", [KD, NKD, ALL_SLOTS])
        g.w1 = s.sb("w1", [KD, NKD, SLOT_E * HID])
        g.w2 = s.sb("w2", [P, SLOT_E * HC, D])
        g.g_out = [nc.alloc_semaphore(f"pieces_out{i}") for i in range(2)]
        g.d_phi, g.d_w1, g.d_w2, g.d_ident = a["phi"], a["w1"], a["w2"], a["ident"]
        g.phi_in, g.w1_in, g.w2_in, g.ident_in, g.out_done = (nc.alloc_semaphore(n) for n in ("phi_in", "w1_in", "w2_in", "ident_in", "out_done"))
        embed(nc, g, a["xT"], a["tokW"], a["pos_rows"], a["tok_b_rows"])
        attention0(nc, g, a)
        layernorm(nc, g, "ln1")
        soft_moe(nc, g, a)
        Scope.retire(nc)
        attention1(nc, g, a)
        routed_moe(nc, g, a, out)


def layouts(x, L0_tok_W, L0_tok_b, L0_tok_pos_emb, L0_attn_W_qkv, L0_attn_b_qkv, L0_ffn_phi, L0_ffn_w1, L0_ffn_b1,
            L0_ffn_w2, L0_ffn_b2, L1_attn_qA, L1_attn_qB, L1_attn_kA, L1_attn_kB, L1_attn_vA, L1_attn_vB, L1_attn_o_w,
            L1_ffn_Wg, L1_ffn_bg, L1_ffn_Wge, L1_ffn_bge, L1_ffn_W1, L1_ffn_b1, L1_ffn_W2, L1_ffn_b2):
    c = np.ascontiguousarray
    kd = lambda w: c(np.asarray(w).reshape(NKD, KD, -1).transpose(1, 0, 2))
    rows = lambda v: c(np.broadcast_to(np.asarray(v).reshape(1, -1), (P, np.asarray(v).size)))
    x = np.asarray(x)
    patches = x.reshape(IMAGES, 4, 16, 4, 16, 3).transpose(0, 1, 3, 2, 4, 5).reshape(TOKENS, 768)
    a = {}
    a["xT"] = c(patches.T.reshape(PATCH_CHUNKS, P, TOKENS).transpose(1, 0, 2))
    a["tokW"] = c(np.asarray(L0_tok_W).reshape(PATCH_CHUNKS, P, D).transpose(1, 0, 2))
    a["pos_rows"] = c(np.tile(np.asarray(L0_tok_pos_emb), (TILE_IMAGES, 1)))
    a["tok_b_rows"] = rows(L0_tok_b)
    a["ident"] = np.eye(P, dtype=np.float32)
    a["wqkv"] = kd(L0_attn_W_qkv)
    bq = np.asarray(L0_attn_b_qkv)
    a["bqk"] = c(bq[0:2 * D].reshape(4, KD).T)
    a["bv_rows"] = rows(bq[2 * D:])
    p = np.arange(KD)
    a["head_mask0"] = (p[:, None] // 16 == np.arange(6)[None, :]).astype(np.float32)
    a["head_mask1"] = (p[:, None] // 32 == np.arange(3)[None, :]).astype(np.float32)
    q = np.arange(P)
    a["mask_q"] = c(np.tile(np.concatenate([
        (q[None, :] // PATCHES == np.arange(8)[:, None]), (q[None, :] % PATCHES == np.arange(16)[:, None])
    ]).astype(np.float32), (1, TILES)))
    mk = np.concatenate([(q[None, :] // PATCHES != np.arange(8)[:, None]),
                         (q[None, :] % PATCHES > np.arange(16)[:, None])]).astype(np.float32) * np.float32(-BIG)
    a["mask_k"] = c(np.broadcast_to(mk[:, None, :], (24, 6, P)))
    a["phi"] = kd(np.asarray(L0_ffn_phi).reshape(ALL_SLOTS, D).T)
    a["w1"] = kd(np.asarray(L0_ffn_w1).transpose(1, 0, 2).reshape(D, SLOT_E * HID))
    a["b1"] = c(np.asarray(L0_ffn_b1).reshape(P, SLOT_E * HID // P))
    a["w2"] = c(np.asarray(L0_ffn_w2).reshape(SLOT_E * HC, P, D).transpose(1, 0, 2))
    a["b2_rows"] = rows(L0_ffn_b2)
    rank = np.asarray(L1_attn_qA).shape[1]
    both = np.zeros((D, 64 + rank), np.float32)
    both[:, :rank], both[:, 64:] = np.asarray(L1_attn_qA), np.asarray(L1_attn_kA)
    a["qkA"] = kd(both)
    a["qkB"] = np.zeros((64 + rank, 2, D), np.float32)
    a["qkB"][:rank, 0], a["qkB"][64:, 1] = np.asarray(L1_attn_qB), np.asarray(L1_attn_kB)
    a["vA"], a["vB"] = kd(L1_attn_vA), c(np.asarray(L1_attn_vB))
    a["o_w"] = kd(L1_attn_o_w)
    hd = 32
    inv = np.float32(1.0) / np.float32(10000.0) ** (np.arange(0, hd, 2, dtype=np.float32) / np.float32(hd))
    fr = np.outer(np.arange(PATCHES, dtype=np.float32), inv).astype(np.float32)
    emb = np.concatenate([fr, fr], -1)
    table = lambda f: c(np.tile(f(emb).astype(np.float32).T, (3, 512 // PATCHES)))
    a["cosT"], a["sinT"] = table(np.cos), table(np.sin)
    a["wgate"] = kd(np.concatenate([np.asarray(L1_ffn_Wg), np.asarray(L1_ffn_Wge).transpose(1, 0, 2).reshape(D, EXPERTS)], 1))
    a["bgate_rows"] = rows(np.concatenate([np.asarray(L1_ffn_bg), np.asarray(L1_ffn_bge).reshape(-1)]))
    a["W1"] = c(np.asarray(L1_ffn_W1).reshape(EXPERTS, NKD, KD, HID).transpose(0, 2, 1, 3))
    a["B1"] = c(np.asarray(L1_ffn_b1))
    a["W2"] = c(np.asarray(L1_ffn_W2).reshape(EXPERTS, HC, P, D).transpose(0, 2, 1, 3))
    a["B2"] = c(np.asarray(L1_ffn_b2))
    a["tri"] = (np.arange(P)[:, None] < np.arange(P)[None, :]).astype(np.float32)
    a["order8"] = rows((E1 - np.arange(E1)).astype(np.float32))
    e = np.arange(EXPERTS)
    a["tri32"] = c(np.broadcast_to((e[None, :] < e[:, None]).astype(np.float32).reshape(1, -1), (P, 1024)))
    a["steps"] = rows((np.arange(8) * P).astype(np.float32))
    a["tile_no"] = rows(np.arange(MOE_TILES).astype(np.float32))
    a["lane"] = rows(np.arange(P).astype(np.float32))
    a["row_tile"] = rows((np.arange(TILES)[:, None] + TILES * np.arange(TOPK)[None, :]).astype(np.float32))
    a["row_lane"] = c(np.broadcast_to(1 + np.arange(P, dtype=np.float32)[:, None], (P, TILES * TOPK)))
    a["spare"] = (TOPK * TOKENS + 1 + np.arange(P, dtype=np.float32))[:, None]
    a["own_tile"] = np.arange(P, dtype=np.float32)[:, None]
    return a


def kernel(**inputs):
    import concourse.bacc as bacc
    from concourse.bass_utils import run_bass_kernel_spmd

    nc = bacc.Bacc("TRN2", target_bir_lowering=False, num_devices=1)
    arrays = layouts(**inputs)
    args = {n: nc.dram_tensor(n, v.shape, mybir.dt.from_np(v.dtype), kind="ExternalInput").ap() for n, v in arrays.items()}
    out = nc.dram_tensor("out", (TOKENS, D), F32, kind="ExternalOutput").ap()
    build(nc, args, out)
    r = run_bass_kernel_spmd(nc, [arrays], core_ids=[0])
    return r.results[0]["out"].reshape(IMAGES, PATCHES, D)
```
